# Optimizing a Trainium2 kernel written in Bass

```python
import numpy as np
import jax
import jax.numpy as jnp

def _softmax(x, axis=-1):
    return jax.nn.softmax(x, axis=axis)
def _gelu(x):
    return jax.nn.gelu(x, approximate=True)
def _silu(x):
    return jax.nn.silu(x)
def _sigmoid(x):
    return jax.nn.sigmoid(x)
def _layernorm(x, axis=-1, eps=1e-5):
    m = jnp.mean(x, axis=axis, keepdims=True)
    v = jnp.var(x, axis=axis, keepdims=True)
    return (x - m) / jnp.sqrt(v + eps)
def _scatter_add(tgt, idx, src, axis=0):
    return tgt.at[idx].add(src)
def _segment_sum(src, seg, n):
    return jax.ops.segment_sum(src, seg, n)

kernel_name = 'mk_conv_attn_hybrid_d2_conv_nhwc128_65abf6'

def setup_inputs(seed: int = 0):
    np.random.seed(seed)
    _w = jnp.asarray
    def _rec_inputs():
        import jax
        import jax.numpy as jnp
        _gk = jax.random.key(seed)
        x = -0.0002023 + 1 * jax.random.normal(jax.random.fold_in(_gk, 1), (16, 56, 56, 128), jnp.float32)
        return x
    x = _rec_inputs()
    def _L0_conv_setup():
        import jax, jax.numpy as jnp
        import numpy as np
        WS = 7
        DISP = WS // 2
        HEADS = 4
        HEAD_DIM = 32
        DIM = 128
        INNER = HEADS * HEAD_DIM
        B, H, W = (16, 56, 56)
        NW_H, NW_W = (H // WS, W // WS)

        def _create_mask(ws, disp, upper_lower, left_right):
            mask = np.zeros((ws * ws, ws * ws), dtype=np.float32)
            if upper_lower:
                mask[-disp * ws:, :-disp * ws] = -np.inf
                mask[:-disp * ws, -disp * ws:] = -np.inf
            if left_right:
                mask = mask.reshape(ws, ws, ws, ws)
                mask[:, -disp:, :, :-disp] = -np.inf
                mask[:, :-disp, :, -disp:] = -np.inf
                mask = mask.reshape(ws * ws, ws * ws)
            return mask
        _UL = _create_mask(WS, DISP, True, False)
        _LR = _create_mask(WS, DISP, False, True)
        _MASK_NP = np.zeros((NW_H * NW_W, WS * WS, WS * WS), dtype=np.float32)
        _MASK_NP[-NW_W:] += _UL
        _MASK_NP[NW_W - 1::NW_W] += _LR
        MASK = jnp.asarray(_MASK_NP)
        _idx = np.array([[x, y] for x in range(WS) for y in range(WS)])
        REL_IDX = jnp.asarray(_idx[None, :, :] - _idx[:, None, :] + WS - 1)
        key = jax.random.key(seed)
        k1, k2, k3, k4, k5 = jax.random.split(key, 5)
        return {'x': jax.random.normal(k1, (B, H, W, DIM), dtype=jnp.float32), 'w_qkv': jax.random.normal(k2, (DIM, 3 * INNER), dtype=jnp.float32) * DIM ** (-0.5), 'pos_emb': jax.random.normal(k3, (2 * WS - 1, 2 * WS - 1), dtype=jnp.float32), 'w_out': jax.random.normal(k4, (INNER, DIM), dtype=jnp.float32) * INNER ** (-0.5), 'b_out': jax.random.normal(k5, (DIM,), dtype=jnp.float32) * 0.01}
    _L0_conv_all = _L0_conv_setup()
    _L0_conv_in = {k: v for k, v in _L0_conv_all.items() if k in ('w_qkv', 'pos_emb', 'w_out', 'b_out', )}
    del _L0_conv_all

    def _L1_attn_setup():
        import jax, jax.numpy as jnp
        import numpy as np
        B, T, D = (4, 2048, 128)
        key = jax.random.key(seed)
        k1, k2, k3 = jax.random.split(key, 3)
        x = jax.random.normal(k1, (B, T, D), dtype=jnp.float32)
        lim = 1.0 / np.sqrt(D)
        W = jax.random.uniform(k2, (3 * D, D), dtype=jnp.float32, minval=-lim, maxval=lim)
        b = jax.random.uniform(k3, (3 * D,), dtype=jnp.float32, minval=-lim, maxval=lim)
        return {'x': x, 'W': W, 'b': b}
    _L1_attn_all = _L1_attn_setup()
    _L1_attn_in = {k: v for k, v in _L1_attn_all.items() if k in ('W', 'b', )}
    del _L1_attn_all

    def _L1_ffn_setup():
        import jax, jax.numpy as jnp
        import numpy as np
        BN_EPS = 1e-05
        key = jax.random.key(seed)
        k1, k2, k3 = jax.random.split(key, 3)
        B, T, I, H = (64, 2048, 128, 128)
        x = jax.random.normal(k1, (B, T, I), dtype=jnp.float32)
        W = jax.random.normal(k2, (H, I), dtype=jnp.float32) * (1.0 / np.sqrt(I))
        V = jnp.linalg.qr(jax.random.normal(k3, (H, H), dtype=jnp.float32))[0]
        gamma = jnp.ones((H,), dtype=jnp.float32)
        beta = jnp.zeros((H,), dtype=jnp.float32)
        return {'x': x, 'W': W, 'V': V, 'gamma': gamma, 'beta': beta}
    _L1_ffn_all = _L1_ffn_setup()
    _L1_ffn_in = {k: v for k, v in _L1_ffn_all.items() if k in ('W', 'V', 'gamma', 'beta', )}
    del _L1_ffn_all

    return {
        "x": x,
        "L0_conv_w_qkv": _L0_conv_in["w_qkv"],
        "L0_conv_pos_emb": _L0_conv_in["pos_emb"],
        "L0_conv_w_out": _L0_conv_in["w_out"],
        "L0_conv_b_out": _L0_conv_in["b_out"],
        "L1_attn_W": _L1_attn_in["W"],
        "L1_attn_b": _L1_attn_in["b"],
        "L1_ffn_W": _L1_ffn_in["W"],
        "L1_ffn_V": _L1_ffn_in["V"],
        "L1_ffn_gamma": _L1_ffn_in["gamma"],
        "L1_ffn_beta": _L1_ffn_in["beta"],
    }

def reference(x, L0_conv_w_qkv, L0_conv_pos_emb, L0_conv_w_out, L0_conv_b_out, L1_attn_W, L1_attn_b, L1_ffn_W, L1_ffn_V, L1_ffn_gamma, L1_ffn_beta):
    import jax
    import jax.numpy as jnp
    def _L0_conv_ref(x, w_qkv, pos_emb, w_out, b_out):
        import jax, jax.numpy as jnp
        import numpy as np
        WS = 7
        DISP = WS // 2
        HEADS = 4
        HEAD_DIM = 32
        DIM = 128
        INNER = HEADS * HEAD_DIM
        B, H, W = (16, 56, 56)
        NW_H, NW_W = (H // WS, W // WS)

        def _create_mask(ws, disp, upper_lower, left_right):
            mask = np.zeros((ws * ws, ws * ws), dtype=np.float32)
            if upper_lower:
                mask[-disp * ws:, :-disp * ws] = -np.inf
                mask[:-disp * ws, -disp * ws:] = -np.inf
            if left_right:
                mask = mask.reshape(ws, ws, ws, ws)
                mask[:, -disp:, :, :-disp] = -np.inf
                mask[:, :-disp, :, -disp:] = -np.inf
                mask = mask.reshape(ws * ws, ws * ws)
            return mask
        _UL = _create_mask(WS, DISP, True, False)
        _LR = _create_mask(WS, DISP, False, True)
        _MASK_NP = np.zeros((NW_H * NW_W, WS * WS, WS * WS), dtype=np.float32)
        _MASK_NP[-NW_W:] += _UL
        _MASK_NP[NW_W - 1::NW_W] += _LR
        MASK = jnp.asarray(_MASK_NP)
        _idx = np.array([[x, y] for x in range(WS) for y in range(WS)])
        REL_IDX = jnp.asarray(_idx[None, :, :] - _idx[:, None, :] + WS - 1)
        scale = HEAD_DIM ** (-0.5)
        x = jnp.roll(x, (-DISP, -DISP), axis=(1, 2))
        b = x.shape[0]
        qkv = x @ w_qkv
        q, k, v = jnp.split(qkv, 3, axis=-1)

        def to_windows(t):
            t = t.reshape(b, NW_H, WS, NW_W, WS, HEADS, HEAD_DIM)
            return t.transpose(0, 5, 1, 3, 2, 4, 6).reshape(b, HEADS, NW_H * NW_W, WS * WS, HEAD_DIM)
        q, k, v = (to_windows(q), to_windows(k), to_windows(v))
        dots = jnp.einsum('bhwid,bhwjd->bhwij', q, k) * scale
        bias = pos_emb[REL_IDX[:, :, 0], REL_IDX[:, :, 1]]
        dots = dots + bias[None, None, None] + MASK[None, None]
        attn = jax.nn.softmax(dots, axis=-1)
        out = jnp.einsum('bhwij,bhwjd->bhwid', attn, v)
        out = out.reshape(b, HEADS, NW_H, NW_W, WS, WS, HEAD_DIM)
        out = out.transpose(0, 2, 4, 3, 5, 1, 6).reshape(b, H, W, INNER)
        out = out @ w_out + b_out
        return jnp.roll(out, (DISP, DISP), axis=(1, 2))

    def _L1_attn_ref(x, W, b):
        import jax, jax.numpy as jnp
        import numpy as np
        B, T, D = (4, 2048, 128)
        Bx, Tx, Dx = x.shape
        qkv = (x @ W.T + b).reshape(Bx, Tx, 3, Dx)
        q, k, v = (qkv[:, :, 0], qkv[:, :, 1], qkv[:, :, 2])
        q = jax.nn.elu(q) + 1.0
        k = jax.nn.elu(k) + 1.0
        kv = jnp.einsum('bti,btj->btij', k, v)
        kv_cum = jnp.cumsum(kv, axis=1)
        k_cum = jnp.cumsum(k, axis=1)
        num = jnp.einsum('bti,btij->btj', q, kv_cum)
        den = jnp.einsum('bti,bti->bt', q, k_cum)[..., None] + 1e-06
        return num / den

    def _L1_ffn_ref(x, W, V, gamma, beta):
        import jax, jax.numpy as jnp
        import numpy as np
        BN_EPS = 1e-05
        B, T, H = (x.shape[0], x.shape[1], W.shape[0])
        Wx = jnp.einsum('bti,hi->bth', x, W)
        flat = Wx.reshape(B * T, H)
        mean = jnp.mean(flat, axis=0)
        var = jnp.var(flat, axis=0)
        Wx = ((flat - mean) * jax.lax.rsqrt(var + BN_EPS) * gamma + beta).reshape(B, T, H)
        Vt = V.T

        def step(yt, wx_t):
            yt = jax.nn.sigmoid(wx_t + yt @ Vt)
            return (yt, yt)
        y0 = jnp.zeros((B, H), dtype=Wx.dtype)
        _, ys = jax.lax.scan(step, y0, jnp.swapaxes(Wx, 0, 1))
        return jnp.swapaxes(ys, 0, 1)

    def _gn(v, G=32, eps=1e-5):
        B_, H_, W_, C_ = v.shape
        g = v.reshape(B_, H_, W_, G, C_ // G)
        m = jnp.mean(g, axis=(1, 2, 4), keepdims=True)
        s = jnp.var(g, axis=(1, 2, 4), keepdims=True)
        return ((g - m) / jnp.sqrt(s + eps)).reshape(v.shape)

    def _ln_c(v, eps=1e-6):
        m = jnp.mean(v, axis=-1, keepdims=True)
        s = jnp.var(v, axis=-1, keepdims=True)
        return (v - m) / jnp.sqrt(s + eps)

    def _ln_t(v, eps=1e-5):
        m = jnp.mean(v, axis=-1, keepdims=True)
        s = jnp.var(v, axis=-1, keepdims=True)
        return (v - m) / jnp.sqrt(s + eps)

    def _to_tokens(v):
        B_, H_, W_, C_ = v.shape
        return v.reshape(B_, H_ * W_, C_)
    def _from_tokens(t, like):
        return t.reshape(like.shape)

    x = x + _L0_conv_ref(_gn(x), L0_conv_w_qkv, L0_conv_pos_emb, L0_conv_w_out, L0_conv_b_out)
    t = _to_tokens(x)
    t = t + _L1_attn_ref(_ln_t(t), L1_attn_W, L1_attn_b)
    t = t + _L1_ffn_ref(_ln_t(t), L1_ffn_W, L1_ffn_V, L1_ffn_gamma, L1_ffn_beta)
    x = _from_tokens(t, x)
    return x


_drawn_inputs = setup_inputs


def setup_inputs(seed=0):
    import zlib

    import numpy as np

    out = dict(_drawn_inputs(seed))
    spreads = {'L1_ffn_gamma': (1.0, 0.594), 'L1_ffn_beta': (0.0, 0.469)}
    factors = {'L0_conv_b_out': 5.829}
    for name, (base, spread) in spreads.items():
        noise = np.random.default_rng([zlib.crc32(name.encode()), seed]).standard_normal(out[name].shape)
        drawn = base * np.exp(spread * noise) if base else spread * noise
        out[name] = jnp.asarray(drawn.astype(out[name].dtype))
    for name, factor in factors.items():
        out[name] = (out[name] * factor).astype(out[name].dtype)
    return out
```

```python
from contextlib import ExitStack

import concourse.bass as bass
from concourse import mybir

F32 = mybir.dt.float32
ALU = mybir.AluOpType
ACT = mybir.ActivationFunctionType
AX = mybir.AxisListType

B, H, W, C = 16, 56, 56, 128
T = H * W
WS, DISP = 7, 3
HEADS, HD = 4, 32
WIN = WS * WS
NWR = H // WS
NWC = W // WS
ROWTOK = WS * W
NU = B * NWR
WPAD = 64
GROUP = 4
GN_EPS, LN_EPS, BN_EPS, DEN_EPS = 1e-5, 1e-5, 1e-5, 1e-6
CH = 112
NCH = T // CH
NC2 = B * NCH // 2
GI = 4
NG = B // GI
COLS = B * NCH
SB = 4
NSB = CH // SB
WARM = 16
AGREE = 5e-7


def at_least(eng, sem, value):
    if not isinstance(value, int) or value > 0:
        eng.wait_ge(sem, value)


def pipeline(eng, step, first, last, lo, hi):
    for n in range(first, lo):
        step(n, n % 2)
    if lo < hi:
        with eng.Fori(lo // 2, hi // 2) as m:
            step(m * 2, 0)
            step(m * 2 + 1, 1)
    for n in range(hi, last):
        step(n, n % 2)


def apart(eng, passed):
    eng.sem_inc(passed, 1)


def inside(n, count):
    return not isinstance(n, int) or 0 <= n < count


def build(nc, x, w_qkv, pos_emb, w_out, b_out, attn_wt, attn_b, ffn_w, ffn_wt, ffn_vt, gamma, beta,
          ident_d, head_mask_d, v_mask_d, shift_mask_d, causal_d, group_d, keep_d, out, agree=AGREE):
    x1 = nc.dram_tensor("x1", (B, T, C), F32, kind="Internal").ap()
    t2 = nc.dram_tensor("t2", (B, T, C), F32, kind="Internal").ap()
    top = ExitStack()

    def sb(name, shape, stack=top):
        return stack.enter_context(nc.sbuf_tensor("k_" + name, shape, F32))

    bank = [top.enter_context(nc.psum_tensor(f"k_bank{i}", [128, 512], F32)) for i in range(8)]
    ident = sb("ident", [128, 128])
    ones = sb("ones", [128, 128])
    exponent = sb("exponent", [128, B])
    gn_rstd = sb("gn_rstd", [128, B])
    gn_shift = sb("gn_shift", [128, B])
    ln2_rstd = sb("ln2_rstd", [CH, COLS])
    ln2_shift = sb("ln2_shift", [CH, COLS])
    gram = sb("gram", [128, C + 1])
    gn_statistics(nc, x, ident_d, group_d, ident, ones, exponent, gn_rstd, gn_shift, bank)
    window_attention(nc, x, x1, w_qkv, pos_emb, w_out, b_out, head_mask_d, v_mask_d, shift_mask_d,
                     ident, gn_rstd, gn_shift, bank)
    linear_attention(nc, x1, t2, attn_wt, attn_b, causal_d, keep_d, ident, exponent, ln2_rstd, ln2_shift, gram, bank)
    recurrence(nc, t2, out, ffn_w, ffn_wt, ffn_vt, gamma, beta, ident, ones, exponent, ln2_rstd, ln2_shift, gram,
               bank, agree)
    top.close()


def gn_statistics(nc, x, ident_d, group_d, ident, ones, exponent, gn_rstd, gn_shift, bank):
    P, TT = CH, T // CH
    ctx = ExitStack()
    with ctx:
        def sb(name, shape):
            return ctx.enter_context(nc.sbuf_tensor("gn_" + name, shape, F32))

        def sem(name):
            return ctx.enter_context(nc.semaphore(name))

        xi = sb("xi", [P, 2, TT * C])
        sq = sb("sq", [P, 2, TT * C])
        part = sb("part", [P, 2, 2, C])
        group = sb("group", [128, 128])
        sums = sb("sums", [128, 2 * B])
        moments = sb("moments", [128, 2, B])
        work = sb("work", [128, 3, B])
        consts = sem("gn_consts")
        loaded = [sem(f"gn_loaded{i}") for i in range(2)]
        ones_set, exponent_set = sem("gn_ones"), sem("gn_exponent")
        squared = sem("gn_squared")
        reduced = sem("gn_reduced")
        summed = sem("gn_summed")
        sums_out = sem("gn_sums_out")
        grouped = sem("gn_grouped")
        chain, rooted = sem("gn_chain"), sem("gn_rooted")

        with nc.Block() as block:
            @block.sync
            def _(sp):
                sp.dma_start(ident[:, :], ident_d).then_inc(consts, 16)
                sp.dma_start(group[:, :], group_d).then_inc(consts, 16)

                def step(n, k):
                    at_least(sp, squared, n - 1)
                    at_least(sp, reduced, n - 1)
                    sp.dma_start(xi[:, k, :], x[bass.ds(n, 1)].rearrange("a t c -> (a t c)")
                                 .rearrange("(p f) -> p f", p=P)).then_inc(loaded[k], 16)
                pipeline(sp, step, 0, B, 2, B)

            @block.scalar
            def _(act):
                def step(n, k):
                    act.wait_ge(loaded[k], (n // 2 + 1) * 16)
                    at_least(act, reduced, n - 1)
                    nc.scalar.activation(sq[:, k, :], xi[:, k, :], ACT.Square).then_inc(squared, 1)
                pipeline(act, step, 0, B, 2, B)

            @block.vector
            def _(dve):
                nc.vector.memset(ones[:, :], 1.0).then_inc(ones_set, 1)

                def step(n, k):
                    dve.wait_ge(loaded[k], (n // 2 + 1) * 16)
                    at_least(dve, summed, n - 1)
                    nc.vector.tensor_reduce(part[:, k, 0, :], xi[:, k, :].rearrange("p (t c) -> p c t", c=C),
                                            AX.X, ALU.add)
                    dve.wait_ge(squared, n + 1)
                    nc.vector.tensor_reduce(part[:, k, 1, :], sq[:, k, :].rearrange("p (t c) -> p c t", c=C),
                                            AX.X, ALU.add).then_inc(reduced, 1)
                pipeline(dve, step, 0, B, 2, B)
                dve.wait_ge(summed, B)
                nc.vector.tensor_copy(sums[:, :], bank[0][:, 0:2 * B]).then_inc(sums_out, 1)
                dve.wait_ge(grouped, 1)
                done = [0]

                def link(ins):
                    done[0] += 1
                    ins.then_inc(chain, 1)
                    dve.wait_ge(chain, done[0])
                link(nc.vector.tensor_scalar(moments[:, :, :].rearrange("p a b -> p (a b)"), bank[1][:, 0:2 * B],
                                             1.0 / (T * GROUP), None, ALU.mult))
                mean, square = moments[:, 0, :], moments[:, 1, :]
                link(nc.vector.tensor_tensor(work[:, 0, :], mean, mean, ALU.mult))
                link(nc.vector.tensor_tensor(work[:, 1, :], square, work[:, 0, :], ALU.subtract))
                link(nc.vector.tensor_scalar(work[:, 2, :], work[:, 1, :], 0.0, GN_EPS, ALU.max, ALU.add))
                dve.wait_ge(rooted, 1)
                link(nc.vector.scalar_tensor_tensor(gn_shift[:, :], mean, -1.0, gn_rstd[:, :], ALU.mult, ALU.mult))

            @block.gpsimd
            def _(pool):
                nc.gpsimd.memset(exponent[:, :], -0.5).then_inc(exponent_set, 1)
                pool.wait_ge(exponent_set, 1)
                pool.wait_ge(chain, 4)
                nc.gpsimd.tensor_tensor(gn_rstd[:, :], work[:, 2, :], exponent[:, :], ALU.pow).then_inc(rooted, 1)

            @block.tensor
            def _(pe):
                pe.wait_ge(ones_set, 1)
                def step(n, k):
                    pe.wait_ge(reduced, n + 1)
                    for j in range(2):
                        mm = nc.tensor.matmul(bank[0][:, bass.ds(n + j * B, 1)], part[:, k, j, :],
                                              ones[0:P, 0:1], start=True, stop=True)
                    mm.then_inc(summed, 1)
                pipeline(pe, step, 0, B, 2, B)
                pe.wait_ge(consts, 32)
                pe.wait_ge(sums_out, 1)
                nc.tensor.matmul(bank[1][:, 0:2 * B], group[:, :], sums[:, :], start=True, stop=True).then_inc(grouped, 1)


def window_attention(nc, x, x1, w_qkv, pos_emb, w_out, b_out, head_mask_d, v_mask_d, shift_mask_d,
                     ident, gn_rstd, gn_shift, bank):
    ctx = ExitStack()
    with ctx:
        def sb(name, shape):
            return ctx.enter_context(nc.sbuf_tensor("wa_" + name, shape, F32))

        def sem(name):
            return ctx.enter_context(nc.semaphore(name))

        HW_ = NWC // 2
        HC = HW_ * WIN
        wqkv = sb("wqkv", [128, 3 * C])
        wout = sb("wout", [128, C])
        bout = sb("bout", [CH, C])
        head_mask = sb("head_mask", [128, HEADS])
        v_mask = sb("v_mask", [2 * WIN, C])
        shift_mask = sb("shift_mask", [128, NWR, 2, 2, WIN])
        position = sb("position", [128, WIN])
        bias = sb("bias", [128, NWR, 2, 2, WIN])
        xw = sb("xw", [CH, 2, 4, C])
        xb = sb("xb", [CH, 4, 4, C])
        xd = sb("xd", [128, 2, NWC, 2, WIN])
        qT = [sb(f"qT{i}", [128, ROWTOK + WPAD - WIN]) for i in range(2)]
        kT = sb("kT", [128, ROWTOK])
        kb = sb("kb", [128, 2, HEADS, ROWTOK])
        prob = sb("prob", [128, 2, 2, 2, HEADS, WIN])
        peak = sb("peak", [128, 2, 2 * HEADS])
        total = sb("total", [128, 2, 2 * HEADS])
        inv = sb("inv", [128, 2, 2 * HEADS])
        vb = sb("vb", [2 * WIN, 2, 2, HW_, C])
        pT = sb("pT", [2 * WIN, 2, 2, 2, 128])
        oT = sb("oT", [128, 2, WS, W])
        y = sb("y", [CH, 2, 4, C])
        b_tx, b_q, b_k, b_v, b_s, b_pt, b_ot, b_y = bank

        consts = sem("wa_consts")
        prep = sem("wa_prep")
        loaded = [sem(f"wa_loaded{i}") for i in range(2)]
        stored = [sem(f"wa_stored{i}") for i in range(2)]
        x_turned, x_normed = sem("wa_x_turned"), sem("wa_x_normed")
        q_ready, k_ready = sem("wa_q_ready"), sem("wa_k_ready")
        q_out, k_out, k_spread = sem("wa_q_out"), sem("wa_k_out"), sem("wa_k_spread")
        v_ready, v_out = sem("wa_v_ready"), sem("wa_v_out")
        scored, biased, peaked = sem("wa_scored"), sem("wa_biased"), sem("wa_peaked")
        lowered, raised, totalled, inverted = sem("wa_lowered"), sem("wa_raised"), sem("wa_totalled"), sem("wa_inverted")
        weighted = sem("wa_weighted")
        p_turned, p_out = sem("wa_p_turned"), sem("wa_p_out")
        attended, o_out = sem("wa_attended"), sem("wa_o_out")
        projected, summed = sem("wa_projected"), sem("wa_summed")
        passed = sem("wa_passed")
        x_kept, x_doubled = sem("wa_x_kept"), sem("wa_x_doubled")

        def rows(dram, n, first, count):
            image, wr = n // NWR, n % NWR
            r = (wr * WS + (DISP + first)) % H
            return dram[bass.ds(image, 1), bass.ds(r * W, count * W), :].rearrange("a t c -> (a t) c")

        def kept(n):
            return xb[:, bass.ds(n % 4, 1)].rearrange("p s a b -> p (s a) b")

        run = dict(first=-3, last=NU + 2, lo=4, hi=NU - 4)

        with nc.Block() as block:
            @block.sync
            def _(sp):
                sp.dma_start(wqkv[:, :], w_qkv).then_inc(consts, 16)
                sp.dma_start(wout[:, :], w_out).then_inc(consts, 16)
                sp.dma_start(bout[:, :], bass.AP(b_out.tensor, 0, [[0, CH], [1, C]])).then_inc(consts, 16)
                sp.dma_start(head_mask[:, :], head_mask_d).then_inc(consts, 16)
                sp.dma_start(v_mask[:, :], v_mask_d).then_inc(consts, 16)
                sp.dma_start(shift_mask[:, :, :, :, :].rearrange("p a b c d -> p (a b c d)"), shift_mask_d).then_inc(consts, 16)
                sp.wait_ge(prep, 1)
                for half in (0, WPAD):
                    for q in range(WIN):
                        r, c = q // WS, q % WS
                        src = pos_emb[WS - 1 - r:2 * WS - 1 - r, WS - 1 - c:2 * WS - 1 - c]
                        sp.dma_start(position[half + q:half + q + 1, :].rearrange("p (a b) -> p a b", a=WS),
                                     src.unsqueeze(0)).then_inc(consts, 16)
                sp.wait_ge(prep, 2)

                def step(n, k):
                    if inside(n + 3, NU):
                        at_least(sp, x_turned, n + 2)
                        at_least(sp, x_kept, n + 2)
                        kl = 1 - k
                        for tile, count in ((slice(0, 2), 4), (2, 2), (3, 1)):
                            first = {4: 0, 2: 4, 1: 6}[count]
                            src = rows(x, n + 3, first, count)
                            if count == 4:
                                sp.dma_start(xw[:, kl, 0:2, :], src.rearrange("(a p) c -> p a c", p=CH)).then_inc(loaded[kl], 16)
                            else:
                                sp.dma_start(xw[0:count * W, kl, tile, :], src).then_inc(loaded[kl], 16)
                    if inside(n - 1, NU):
                        sp.wait_ge(summed, n)
                        ks = 1 - k
                        sp.dma_start(rows(x1, n - 1, 0, 4).rearrange("(a p) c -> p a c", p=CH), y[:, ks, 0:2, :]).then_inc(stored[ks], 16)
                        sp.dma_start(rows(x1, n - 1, 4, 2), y[:, ks, 2, :]).then_inc(stored[ks], 16)
                        sp.dma_start(rows(x1, n - 1, 6, 1), y[0:W, ks, 3, :]).then_inc(stored[ks], 16)
                pipeline(sp, step, **run)
                for k in range(2):
                    sp.wait_ge(stored[k], NU // 2 * 48)

            @block.tensor
            def _(pe):
                pe.wait_ge(consts, 16 * (6 + 2 * WIN))
                pe.wait_ge(prep, 2)

                def scores(n, k, h):
                    if not inside(n, NU):
                        return
                    pe.wait_ge(q_out, n + 1)
                    pe.wait_ge(k_spread, n + 1)
                    at_least(pe, biased, n * 2 + h)
                    for w in range(HW_):
                        c = (h * HW_ + w) * WIN
                        part = slice(WPAD * (w % 2), WPAD * (w % 2) + WPAD)
                        mm = nc.tensor.matmul(b_s[part, (w // 2) * HEADS * WIN:(w // 2 + 1) * HEADS * WIN],
                                              qT[k][:, c:c + WPAD], kb[:, k, :, c:c + WIN], start=True, stop=True)
                    mm.then_inc(scored, 1)

                def turn_probabilities(n, k, h):
                    if not inside(n, NU):
                        return
                    pe.wait_ge(weighted, n * 2 + h + 1)
                    at_least(pe, p_out, n * 2 + h)
                    for p in range(2):
                        for hp in range(2):
                            q = p * 2 + hp
                            mm = nc.tensor.transpose(b_pt[0:2 * WIN, q * 128:(q + 1) * 128],
                                                     prob[:, k, h, p, 2 * hp:2 * hp + 2, :].rearrange("p a b -> p (a b)"), ident[:, :])
                    mm.then_inc(p_turned, 1)

                def attend(n, k, h):
                    if not inside(n, NU):
                        return
                    pe.wait_ge(p_out, n * 2 + h + 1)
                    pe.wait_ge(v_out, n * 2 + h + 1)
                    at_least(pe, o_out, n)
                    for hp in range(2):
                        for w in range(HW_):
                            c = (h * HW_ + w) * WIN
                            i = WPAD * (w % 2)
                            mm = nc.tensor.matmul(b_ot[64 * hp:64 * hp + 64, c:c + WIN],
                                                  vb[:, k, h, w, 64 * hp:64 * hp + 64],
                                                  pT[:, h, w // 2, hp, i:i + WIN], start=True, stop=True)
                    mm.then_inc(attended, 1)

                def queries(n, k):
                    if inside(n, NU):
                        pe.wait_ge(x_normed, n + 1)
                        at_least(pe, q_out, n)
                        nc.tensor.matmul(b_q[:, 0:ROWTOK], wqkv[:, 0:C], xd[:, k, :, 0, :], start=True, stop=True).then_inc(q_ready, 1)

                def keys(n, k):
                    if inside(n, NU):
                        at_least(pe, k_out, n)
                        nc.tensor.matmul(b_k[:, 0:ROWTOK], wqkv[:, C:2 * C], xd[:, k, :, 0, :], start=True, stop=True).then_inc(k_ready, 1)

                def values(n, k, h):
                    if not inside(n, NU):
                        return
                    at_least(pe, v_out, n * 2 + h)
                    pe.wait_ge(x_doubled, n + 1)
                    for w in range(HW_):
                        tokens = xd[:, k, h * HW_ + w].rearrange("p a b -> p (a b)")
                        mm = nc.tensor.matmul(b_v[0:2 * WIN, w * C:(w + 1) * C], tokens,
                                              wqkv[:, 2 * C:3 * C], start=True, stop=True)
                    mm.then_inc(v_ready, 1)

                def turn_tokens(n, k):
                    if not inside(n, NU):
                        return
                    pe.wait_ge(loaded[k], (n // 2 + 1) * 48)
                    at_least(pe, x_normed, n)
                    for t in range(4):
                        p = CH if t < 3 else W
                        mm = nc.tensor.transpose(b_tx[:, t * CH:t * CH + p], xw[0:p, k, t, :], ident[0:p, 0:p])
                    mm.then_inc(x_turned, 1)

                def project(n, k):
                    if not inside(n, NU):
                        return
                    pe.wait_ge(o_out, n + 1)
                    at_least(pe, summed, n)
                    for t in range(4):
                        p = CH if t < 3 else W
                        ot = oT[:, k, 2 * t:2 * t + p // W, :].rearrange("p a b -> p (a b)")
                        mm = nc.tensor.matmul(b_y[0:p, t * C:(t + 1) * C], ot, wout[:, :], start=True, stop=True)
                    mm.then_inc(projected, 1)

                def step(n, k):
                    scores(n, k, 0)
                    turn_probabilities(n - 1, 1 - k, 0)
                    queries(n + 1, 1 - k)
                    attend(n - 1, 1 - k, 0)
                    scores(n, k, 1)
                    turn_probabilities(n - 1, 1 - k, 1)
                    keys(n + 1, 1 - k)
                    attend(n - 1, 1 - k, 1)
                    values(n + 1, 1 - k, 0)
                    turn_tokens(n + 2, k)
                    values(n + 1, 1 - k, 1)
                    project(n - 1, 1 - k)
                pipeline(pe, step, **run)

            @block.vector
            def _(dve):
                nc.vector.memset(position[:, :], 0.0).then_inc(prep, 1)
                nc.vector.memset(b_y[:, :], 0.0)
                for i in range(2):
                    nc.vector.memset(xw[:, i, 3, :], 0.0)
                    last = nc.vector.memset(qT[i][:, :], 0.0)
                last.then_inc(prep, 1)
                dve.wait_ge(consts, 16 * (6 + 2 * WIN))
                dve.wait_ge(prep, 2)
                nc.vector.tensor_tensor(bias[:, :, :, :, :].rearrange("p a b c d -> p (a b c) d"),
                                        shift_mask[:, :, :, :, :].rearrange("p a b c d -> p (a b c) d"),
                                        position[:, :].unsqueeze(1).broadcast_to([128, NWR * 4, WIN]), ALU.add).then_inc(prep, 1)
                dve.wait_ge(prep, 3)

                def bias_and_peak(n, k, h):
                    if not inside(n, NU):
                        return
                    dve.wait_ge(scored, n * 2 + h + 1)
                    at_least(dve, p_turned, (n - 2) * 2 + h + 1)
                    if isinstance(n, int):
                        bs = bias[:, n % NWR, h]
                    else:
                        bs = bias[:, bass.ds(n % NWR, 1), h].rearrange("p a b c -> p (a b) c")
                    bs = bs.unsqueeze(2).broadcast_to([128, 2, HEADS, WIN])
                    nc.vector.tensor_tensor(prob[:, k, h], b_s[:, 0:2 * HEADS * WIN].rearrange("p (a b c) -> p a b c", a=2, b=HEADS),
                                            bs, ALU.add).then_inc(biased, 1)
                    dve.wait_ge(biased, n * 2 + h + 1)
                    at_least(dve, lowered, n * 2 + h - 1)
                    nc.vector.tensor_reduce(peak[:, h, :], prob[:, k, h].rearrange("p a b c -> p (a b) c"), AX.X, ALU.max).then_inc(peaked, 1)

                def totals(n, k, h):
                    if not inside(n, NU):
                        return
                    dve.wait_ge(raised, n * 2 + h + 1)
                    nc.vector.tensor_reduce(total[:, h, :], prob[:, k, h].rearrange("p a b c -> p (a b) c"), AX.X, ALU.add).then_inc(totalled, 1)
                    dve.wait_ge(totalled, n * 2 + h + 1)
                    at_least(dve, weighted, n * 2 + h - 1)
                    nc.vector.reciprocal(inv[:, h, :], total[:, h, :]).then_inc(inverted, 1)

                def residual(n, k):
                    if not inside(n, NU):
                        return
                    dve.wait_ge(projected, n + 1)
                    dve.wait_ge(x_kept, n + 1)
                    at_least(dve, stored[k], (n // 2) * 48)
                    nc.vector.tensor_tensor(y[:, k].rearrange("p a b -> p (a b)"), b_y[0:CH, :],
                                            kept(n).rearrange("p a b -> p (a b)"), ALU.add).then_inc(summed, 1)

                def queries_out(n, k):
                    if not inside(n, NU):
                        return
                    dve.wait_ge(q_ready, n + 1)
                    at_least(dve, scored, (n - 1) * 2)
                    nc.vector.tensor_scalar(qT[k][:, 0:ROWTOK], b_q[:, 0:ROWTOK],
                                            float(HD) ** -0.5, None, ALU.mult).then_inc(q_out, 1)

                def values_out(n, k, h):
                    if not inside(n, NU):
                        return
                    dve.wait_ge(v_ready, n * 2 + h + 1)
                    at_least(dve, attended, (n - 2) * 2 + h + 1)
                    nc.vector.tensor_tensor(vb[:, k, h], b_v[0:2 * WIN, :].rearrange("p (w c) -> p w c", w=HW_),
                                            v_mask[:, :].unsqueeze(1).broadcast_to([2 * WIN, HW_, C]), ALU.mult).then_inc(v_out, 1)

                def step(n, k):
                    totals(n - 1, 1 - k, 1)
                    bias_and_peak(n, k, 0)
                    residual(n - 2, k)
                    queries_out(n + 1, 1 - k)
                    bias_and_peak(n, k, 1)
                    values_out(n + 1, 1 - k, 0)
                    totals(n, k, 0)
                    values_out(n + 1, 1 - k, 1)
                pipeline(dve, step, **run)

            @block.scalar
            def _(act):
                def normalise(n, k):
                    if not inside(n, NU):
                        return
                    act.wait_ge(x_turned, n + 1)
                    at_least(act, v_ready, (n - 2) * 2 + 2)
                    at_least(act, k_ready, n - 1)
                    src = b_tx[:, 0:ROWTOK].rearrange("p (r c) -> p r c", r=WS)
                    image = bass.ds(n // NWR, 1)
                    windows = xd[:, k, :, 0, :].rearrange("p w (r c) -> p w r c", r=WS)
                    edge = WS - DISP
                    for dst, s in ((windows[:, 0:NWC - 1], src[:, :, DISP:W - edge].rearrange("p r (w c) -> p w r c", c=WS)),
                                   (windows[:, NWC - 1, :, 0:edge], src[:, :, W - edge:W]),
                                   (windows[:, NWC - 1, :, edge:WS], src[:, :, 0:DISP])):
                        last = nc.scalar.activation(dst, s, ACT.Identity,
                                                    bias=gn_shift[:, image], scale=gn_rstd[:, image])
                    last.then_inc(x_normed, 1)

                def keys_out(n, k):
                    if not inside(n, NU):
                        return
                    act.wait_ge(k_ready, n + 1)
                    at_least(act, k_spread, n)
                    nc.scalar.activation(kT[:, :], b_k[:, 0:ROWTOK], ACT.Copy).then_inc(k_out, 1)

                def exps(n, k, h):
                    if inside(n, NU):
                        act.wait_ge(lowered, n * 2 + h + 1)
                        flat = prob[:, k, h].rearrange("p a b c -> p (a b c)")
                        nc.scalar.activation(flat, flat, ACT.Exp).then_inc(raised, 1)

                def probabilities_out(n, k, h):
                    if not inside(n, NU):
                        return
                    act.wait_ge(p_turned, n * 2 + h + 1)
                    at_least(act, attended, n * 2 + h - 1)
                    nc.scalar.activation(pT[:, h].rearrange("p a b c -> p (a b c)"), b_pt[0:2 * WIN, :], ACT.Copy).then_inc(p_out, 1)

                def attended_out(n, k):
                    if not inside(n, NU):
                        return
                    act.wait_ge(attended, n * 2 + 2)
                    at_least(act, projected, n - 1)
                    src = b_ot[:, 0:ROWTOK].rearrange("p (w r c) -> p w r c", w=NWC, r=WS)
                    dst = oT[:, k]
                    nc.scalar.activation(dst[:, :, DISP:W - (WS - DISP)].rearrange("p r (w c) -> p w r c", c=WS),
                                         src[:, 0:NWC - 1], ACT.Copy)
                    nc.scalar.activation(dst[:, :, W - (WS - DISP):W], src[:, NWC - 1, :, 0:WS - DISP], ACT.Copy)
                    nc.scalar.activation(dst[:, :, 0:DISP], src[:, NWC - 1, :, WS - DISP:WS], ACT.Copy).then_inc(o_out, 1)

                def step(n, k):
                    exps(n - 1, 1 - k, 1)
                    probabilities_out(n - 1, 1 - k, 0)
                    exps(n, k, 0)
                    probabilities_out(n - 1, 1 - k, 1)
                    keys_out(n + 1, 1 - k)
                    attended_out(n - 1, 1 - k)
                    normalise(n + 2, k)
                pipeline(act, step, **run)

            @block.gpsimd
            def _(pool):
                pool.wait_ge(consts, 16 * (6 + 2 * WIN))
                pool.wait_ge(prep, 2)

                def lower(n, k, h):
                    if not inside(n, NU):
                        return
                    pool.wait_ge(peaked, n * 2 + h + 1)
                    s = prob[:, k, h].rearrange("p a b c -> p (a b) c")
                    nc.gpsimd.tensor_tensor(s, s, peak[:, h, :].unsqueeze(2).broadcast_to([128, 2 * HEADS, WIN]),
                                            ALU.subtract).then_inc(lowered, 1)

                def weigh(n, k, h):
                    if not inside(n, NU):
                        return
                    pool.wait_ge(inverted, n * 2 + h + 1)
                    s = prob[:, k, h].rearrange("p a b c -> p (a b) c")
                    nc.gpsimd.tensor_tensor(s, s, inv[:, h, :].unsqueeze(2).broadcast_to([128, 2 * HEADS, WIN]),
                                            ALU.mult).then_inc(weighted, 1)

                def spread_keys(n, k):
                    if not inside(n, NU):
                        return
                    pool.wait_ge(k_out, n + 1)
                    at_least(pool, scored, (n - 1) * 2)
                    nc.gpsimd.tensor_tensor(kb[:, k], kT[:, :].unsqueeze(1).broadcast_to([128, HEADS, ROWTOK]),
                                            head_mask[:, :].unsqueeze(2).broadcast_to([128, HEADS, ROWTOK]),
                                            ALU.mult).then_inc(k_spread, 1)

                def keep_tokens(n, k):
                    if not inside(n, NU):
                        return
                    pool.wait_ge(loaded[k], (n // 2 + 1) * 48)
                    at_least(pool, summed, n - 3)
                    apart(pool, passed)
                    nc.gpsimd.tensor_tensor(kept(n), xw[:, k], bout[:, :].unsqueeze(1).broadcast_to([CH, 4, C]),
                                            ALU.add).then_inc(x_kept, 1)

                def double_tokens(n, k):
                    if inside(n, NU):
                        pool.wait_ge(x_normed, n + 1)
                        apart(pool, passed)
                        nc.gpsimd.tensor_copy(xd[:, k, :, 1, :], xd[:, k, :, 0, :]).then_inc(x_doubled, 1)

                def step(n, k):
                    double_tokens(n + 1, 1 - k)
                    weigh(n - 1, 1 - k, 1)
                    lower(n, k, 0)
                    spread_keys(n + 1, 1 - k)
                    weigh(n, k, 0)
                    lower(n, k, 1)
                    keep_tokens(n + 2, k)
                pipeline(pool, step, **run)


def linear_attention(nc, x1, t2, attn_wt, attn_b, causal_d, keep_d, ident, exponent, ln2_rstd, ln2_shift, gram, bank):
    ctx = ExitStack()
    with ctx:
        def sb(name, shape):
            return ctx.enter_context(nc.sbuf_tensor("la_" + name, shape, F32))

        def sem(name):
            return ctx.enter_context(nc.semaphore(name))

        E = C + 1
        UNITS = NCH // 2
        wt = sb("wt", [128, 3 * C])
        bqk = sb("bqk", [128, 2])
        bv = sb("bv", [CH, C])
        causal = sb("causal", [CH, CH])
        keep = sb("keep", [128, NC2])
        xc = sb("xc", [CH, 4, 2, C])
        stats = sb("stats", [CH, 2, 6])
        mv = sb("mv", [CH, 2, 2, 2])
        rstd = sb("rstd", [CH, 2, 2])
        shift = sb("shift", [CH, 2, 2])
        u = sb("u", [CH, 2, 2, C])
        uT = sb("uT", [128, 2, 2 * CH])
        raised = sb("raised", [128, 2, 2 * CH])
        capped = sb("capped", [128, 2, 2 * CH])
        positive = sb("positive", [128, 2, 2 * CH])
        fqk = sb("fqk", [128, 2, 2, 2 * CH])
        ve = sb("ve", [CH, 2, 2, E])
        aT = sb("aT", [CH, 2, 2, CH])
        kt = sb("kt", [CH, 2, 2, C])
        state = sb("state", [128, 2, E])
        carried = sb("carried", [128, E])
        den = sb("den", [CH, 2, 1])
        rden = sb("rden", [CH, 2, 1])
        tn = sb("tn", [CH, 4, 2, C])
        stats2 = sb("stats2", [CH, 2, 6])
        mv2 = sb("mv2", [CH, 2, 2, 2])
        spread = sb("spread", [CH, 2, 2])
        minus = sb("minus", [CH, 2, 2])
        u2 = sb("u2", [CH, 2, 2, E])
        zero = sb("zero", [128, C + E])
        b_u, b_qk, b_v, b_kt, b_at, b_num, b_kv, b_gram = bank

        consts, prep = sem("la_consts"), sem("la_prep")
        loaded = [sem(f"la_loaded{i}") for i in range(2)]
        stored = [sem(f"la_stored{i}") for i in range(2)]
        measured, aggregated, rooted, shifted = sem("la_measured"), sem("la_aggregated"), sem("la_rooted"), sem("la_shifted")
        normed, u_turned, u_out = sem("la_normed"), sem("la_u_turned"), sem("la_u_out")
        qk_ready, qk_raised, qk_out = sem("la_qk_ready"), sem("la_qk_raised"), sem("la_qk_out")
        passed, dve_passed = sem("la_passed"), sem("la_dve_passed")
        spread_out, minus_out = sem("la_spread_out"), sem("la_minus_out")
        spread_out2, minus_out2 = sem("la_spread_out2"), sem("la_minus_out2")
        qk_capped = sem("la_qk_capped")
        v_ready, v_out = sem("la_v_ready"), sem("la_v_out")
        a_ready, a_out = sem("la_a_ready"), sem("la_a_out")
        k_turned, k_out = sem("la_k_turned"), sem("la_k_out")
        kv_ready, kept, moved, advanced = sem("la_kv_ready"), sem("la_kept"), sem("la_moved"), sem("la_advanced")
        num_ready, den_ready, den_inv, attended = sem("la_num_ready"), sem("la_den_ready"), sem("la_den_inv"), sem("la_attended")
        measured2, aggregated2, rooted2, shifted2 = sem("la_measured2"), sem("la_aggregated2"), sem("la_rooted2"), sem("la_shifted2")
        normed2, counted, gram_done = sem("la_normed2"), sem("la_counted"), sem("la_gram_done")

        def chunks(dram, n):
            image, part = n // UNITS, n % UNITS
            return dram[bass.ds(image, 1), bass.ds(part * (2 * CH), 2 * CH), :].rearrange("o (a p) c -> p (o a) c", p=CH)

        def slot4(tile, n):
            return tile[:, bass.ds(n % 4, 1)].rearrange("p s a b -> p (s a) b")

        def column(tile, n, a):
            return tile[:, bass.ds(n * 2 + a, 1)]

        run = dict(first=-3, last=NC2 + 2, lo=4, hi=NC2 - 4)

        with nc.Block() as block:
            @block.sync
            def _(sp):
                sp.dma_start(wt[:, :], attn_wt).then_inc(consts, 16)
                sp.dma_start(bqk[:, :], attn_b[0:2 * C].rearrange("(a p) -> p a", p=C), allow_slow_non_contiguous=True).then_inc(consts, 16)
                sp.dma_start(bv[:, :], bass.AP(attn_b.tensor, 2 * C, [[0, CH], [1, C]])).then_inc(consts, 16)
                sp.dma_start(causal[:, :], causal_d).then_inc(consts, 16)
                sp.dma_start(keep[:, :], keep_d).then_inc(consts, 16)

                def step(n, k):
                    if inside(n + 3, NC2):
                        at_least(sp, attended, n * 2)
                        kl = 1 - k
                        at_least(sp, loaded[kl], (n + 3) // 2 * 16)
                        sp.dma_start(slot4(xc, n + 3), chunks(x1, n + 3)).then_inc(loaded[kl], 16)
                    if inside(n - 1, NC2):
                        sp.wait_ge(attended, n * 2)
                        ks = 1 - k
                        at_least(sp, stored[ks], (n - 1) // 2 * 16)
                        sp.dma_start(chunks(t2, n - 1), slot4(tn, n - 1)).then_inc(stored[ks], 16)
                pipeline(sp, step, **run)
                for k in range(2):
                    sp.wait_ge(stored[k], NC2 // 2 * 16)

            @block.tensor
            def _(pe):
                pe.wait_ge(consts, 80)
                pe.wait_ge(prep, 1)
                nc.tensor.matmul(b_gram[:, 0:E], zero[:, 0:C], zero[:, C:C + E], start=True, stop=False, skip_group_check=True)

                def turn_tokens(n, k):
                    if not inside(n, NC2):
                        return
                    pe.wait_ge(normed, n * 2 + 2)
                    at_least(pe, u_out, n)
                    for a in range(2):
                        mm = nc.tensor.transpose(b_u[:, a * CH:(a + 1) * CH], u[:, k, a, :], ident[0:CH, 0:CH])
                    mm.then_inc(u_turned, 1)

                def project(n, k):
                    if not inside(n, NC2):
                        return
                    pe.wait_ge(u_out, n + 1)
                    at_least(pe, qk_raised, n * 4)
                    for j in range(2):
                        mm = nc.tensor.matmul(b_qk[:, j * 2 * CH:(j + 1) * 2 * CH], wt[:, j * C:(j + 1) * C], uT[:, k, :],
                                              start=True, stop=True)
                    mm.then_inc(qk_ready, 1)
                    at_least(pe, v_out, n)
                    for a in range(2):
                        mm = nc.tensor.matmul(b_v[0:CH, a * C:(a + 1) * C], uT[:, k, a * CH:(a + 1) * CH],
                                              wt[:, 2 * C:3 * C], start=True, stop=True)
                    mm.then_inc(v_ready, 1)

                def inner(n, k):
                    if not inside(n, NC2):
                        return
                    pe.wait_ge(qk_out, n * 2 + 2)
                    at_least(pe, k_out, n)
                    for a in range(2):
                        mm = nc.tensor.transpose(b_kt[0:CH, a * C:(a + 1) * C], fqk[:, k, 1, a * CH:(a + 1) * CH], ident[:, :])
                    mm.then_inc(k_turned, 1)
                    at_least(pe, a_out, n)
                    for a in range(2):
                        c = slice(a * CH, (a + 1) * CH)
                        mm = nc.tensor.matmul(b_at[0:CH, c], fqk[:, k, 1, c], fqk[:, k, 0, c], start=True, stop=True)
                    mm.then_inc(a_ready, 1)

                def outer(n, k):
                    if not inside(n, NC2):
                        return
                    pe.wait_ge(k_out, n + 1)
                    pe.wait_ge(v_out, n + 1)
                    at_least(pe, advanced, n)
                    for a in range(2):
                        mm = nc.tensor.matmul(b_kv[:, a * E:(a + 1) * E], kt[:, k, a, :], ve[:, k, a, :], start=True, stop=True)
                    mm.then_inc(kv_ready, 1)
                    pe.wait_ge(a_out, n + 1)
                    at_least(pe, attended, n * 2)
                    for a in range(2):
                        nc.tensor.matmul(b_num[0:CH, a * E:(a + 1) * E], aT[:, k, a, :], ve[:, k, a, :], start=True, stop=False)
                        pe.wait_ge(kept if a == 0 else moved, n + 1)
                        mm = nc.tensor.matmul(b_num[0:CH, a * E:(a + 1) * E], fqk[:, k, 0, a * CH:(a + 1) * CH], state[:, a, :],
                                              start=False, stop=True)
                    mm.then_inc(num_ready, 1)

                def moments(n, k):
                    if not inside(n, NC2):
                        return
                    pe.wait_ge(normed2, n * 2 + 2)
                    for a in range(2):
                        mm = nc.tensor.matmul(b_gram[:, 0:E], u2[:, k, a, 0:C], u2[:, k, a, :], start=False,
                                              stop=isinstance(n, int) and n == NC2 - 1 and a == 1, skip_group_check=True)
                    mm.then_inc(counted, 1)

                def step(n, k):
                    inner(n, k)
                    turn_tokens(n + 1, 1 - k)
                    outer(n, k)
                    moments(n - 1, 1 - k)
                    project(n + 1, 1 - k)
                pipeline(pe, step, **run)

            @block.scalar
            def _(act):
                act.wait_ge(consts, 80)

                def normalise(n, k):
                    if not inside(n, NC2):
                        return
                    act.wait_ge(shifted, n + 1)
                    act.wait_ge(loaded[k], (n // 2 + 1) * 16)
                    at_least(act, u_turned, n - 1)
                    src = slot4(xc, n)
                    for a in range(2):
                        nc.scalar.activation(u[:, k, a, :], src[:, a], ACT.Identity, bias=shift[:, k, a:a + 1],
                                             scale=rstd[:, k, a:a + 1]).then_inc(normed, 1)

                def turned_out(n, k):
                    if not inside(n, NC2):
                        return
                    act.wait_ge(u_turned, n + 1)
                    at_least(act, v_ready, n - 1)
                    nc.scalar.activation(uT[:, k, :], b_u[:, 0:2 * CH], ACT.Copy).then_inc(u_out, 1)

                def features(n, k):
                    if not inside(n, NC2):
                        return
                    act.wait_ge(qk_ready, n + 1)
                    at_least(act, qk_out, n * 2)
                    for j in range(2):
                        src = b_qk[:, j * 2 * CH:(j + 1) * 2 * CH]
                        nc.scalar.activation(raised[:, j, :], src, ACT.Exp, bias=bqk[:, j:j + 1]).then_inc(qk_raised, 1)
                        nc.scalar.activation(positive[:, j, :], src, ACT.Relu, bias=bqk[:, j:j + 1]).then_inc(qk_raised, 1)

                def keys_out(n, k):
                    if not inside(n, NC2):
                        return
                    act.wait_ge(k_turned, n + 1)
                    at_least(act, kv_ready, n - 1)
                    nc.scalar.activation(kt[:, k].rearrange("p a b -> p (a b)"), b_kt[0:CH, 0:2 * C], ACT.Copy).then_inc(k_out, 1)

                def normalise2(n, k):
                    if not inside(n, NC2):
                        return
                    act.wait_ge(shifted2, n + 1)
                    at_least(act, counted, n - 1)
                    src = slot4(tn, n)
                    for a in range(2):
                        nc.scalar.activation(u2[:, k, a, 0:C], src[:, a], ACT.Identity, bias=column(ln2_shift, n, a),
                                             scale=column(ln2_rstd, n, a)).then_inc(normed2, 1)

                def step(n, k):
                    keys_out(n, k)
                    turned_out(n + 1, 1 - k)
                    normalise2(n - 1, 1 - k)
                    normalise(n + 2, k)
                    features(n + 1, 1 - k)
                pipeline(act, step, **run)

            @block.gpsimd
            def _(pool):
                pool.wait_ge(prep, 1)

                def features(n, k):
                    if not inside(n, NC2):
                        return
                    at_least(pool, num_ready, n - 1)
                    pool.wait_ge(qk_raised, n * 4 + 4)
                    at_least(pool, qk_out, n * 2)
                    apart(pool, passed)
                    nc.gpsimd.tensor_scalar(capped[:, :, :], raised[:, :, :], 1.0, None, ALU.min).then_inc(qk_capped, 1)
                    pool.wait_ge(qk_capped, n + 1)
                    nc.gpsimd.tensor_tensor(fqk[:, k], capped[:, :, :], positive[:, :, :], ALU.add).then_inc(qk_out, 2)

                def statistics(n, k, which, moments, known, sem_eps, sem_root, sem_minus, sem_done, rstd_out, shift_out):
                    if not inside(n, NC2):
                        return
                    pool.wait_ge(known, n * 2 + 2)
                    at_least(pool, sem_done, n)
                    apart(pool, passed)
                    nc.gpsimd.tensor_scalar(spread[:, which, :], moments[:, k, :, 1], LN_EPS, None, ALU.add).then_inc(sem_eps, 1)
                    nc.gpsimd.tensor_scalar(minus[:, which, :], moments[:, k, :, 0], -1.0, None, ALU.mult).then_inc(sem_minus, 1)
                    pool.wait_ge(sem_eps, n + 1)
                    apart(pool, passed)
                    nc.gpsimd.tensor_tensor(rstd_out, spread[:, which, :], exponent[0:CH, 0:2], ALU.pow).then_inc(sem_root, 1)
                    pool.wait_ge(sem_minus, n + 1)
                    pool.wait_ge(sem_root, n + 1)
                    apart(pool, passed)
                    nc.gpsimd.tensor_tensor(shift_out, minus[:, which, :], rstd_out, ALU.mult).then_inc(sem_done, 1)

                def step(n, k):
                    if inside(n + 2, NC2):
                        at_least(pool, normed, n * 2 + 2)
                    statistics(n + 2, k, 0, mv, aggregated, spread_out, rooted, minus_out, shifted, rstd[:, k, :], shift[:, k, :])
                    features(n + 1, 1 - k)
                    if inside(n, NC2):
                        both = bass.ds(n * 2, 2)
                        statistics(n, k, 1, mv2, aggregated2, spread_out2, rooted2, minus_out2, shifted2,
                                   ln2_rstd[:, both], ln2_shift[:, both])
                pipeline(pool, step, **run)

            @block.vector
            def _(dve):
                nc.vector.memset(zero[:, :], 0.0)
                nc.vector.memset(carried[:, :], 0.0)
                nc.vector.memset(ve[:, :, :, C:E], 1.0)
                nc.vector.memset(u2[:, :, :, C:E], 1.0).then_inc(prep, 1)
                dve.wait_ge(prep, 1)
                dve.wait_ge(consts, 80)

                def measure(n, k):
                    if not inside(n, NC2):
                        return
                    dve.wait_ge(loaded[k], (n // 2 + 1) * 16)
                    at_least(dve, aggregated, n * 2)
                    src = slot4(xc, n)
                    for a in range(2):
                        apart(dve, dve_passed)
                        nc.vector.bn_stats(stats[:, a, :], src[:, a]).then_inc(measured, 1)
                    at_least(dve, shifted, n - 1)
                    for a in range(2):
                        dve.wait_ge(measured, n * 2 + a + 1)
                        apart(dve, dve_passed)
                        nc.vector.bn_aggr(mv[:, k, a, :], stats[:, a, :]).then_inc(aggregated, 1)

                def values_out(n, k):
                    if not inside(n, NC2):
                        return
                    dve.wait_ge(v_ready, n + 1)
                    at_least(dve, num_ready, n - 1)
                    nc.vector.tensor_tensor(ve[:, k, :, 0:C], b_v[0:CH, 0:2 * C].rearrange("p (a b) -> p a b", a=2),
                                            bv[:, :].unsqueeze(1).broadcast_to([CH, 2, C]), ALU.add).then_inc(v_out, 1)

                def inner_out(n, k):
                    if not inside(n, NC2):
                        return
                    dve.wait_ge(a_ready, n + 1)
                    at_least(dve, num_ready, n - 1)
                    nc.vector.tensor_tensor(aT[:, k], b_at[0:CH, 0:2 * CH].rearrange("p (a b) -> p a b", a=2),
                                            causal[:, :].unsqueeze(1).broadcast_to([CH, 2, CH]), ALU.mult).then_inc(a_out, 1)

                def advance(n, k):
                    if not inside(n, NC2):
                        return
                    at_least(dve, num_ready, n)
                    at_least(dve, advanced, n)
                    nc.vector.tensor_scalar(state[:, 0, :], carried[:, :], keep[:, bass.ds(n, 1)], None, ALU.mult).then_inc(kept, 1)
                    dve.wait_ge(kept, n + 1)
                    dve.wait_ge(kv_ready, n + 1)
                    nc.vector.tensor_tensor(state[:, 1, :], b_kv[:, 0:E], state[:, 0, :], ALU.add).then_inc(moved, 1)
                    dve.wait_ge(moved, n + 1)
                    nc.vector.tensor_tensor(carried[:, :], b_kv[:, E:2 * E], state[:, 1, :], ALU.add).then_inc(advanced, 1)

                def attend(n, k):
                    if not inside(n, NC2):
                        return
                    dve.wait_ge(num_ready, n + 1)
                    num = b_num[0:CH, 0:2 * E].rearrange("p (a b) -> p a b", a=2)
                    nc.vector.tensor_scalar(den[:, :, :], num[:, :, C:E], DEN_EPS, None, ALU.add).then_inc(den_ready, 1)
                    dve.wait_ge(den_ready, n + 1)
                    nc.vector.reciprocal(rden[:, :, :], den[:, :, :]).then_inc(den_inv, 1)
                    dve.wait_ge(den_inv, n + 1)
                    at_least(dve, stored[k], (n - 2) // 2 * 16)
                    src, dst = slot4(xc, n), slot4(tn, n)
                    for a in range(2):
                        nc.vector.scalar_tensor_tensor(dst[:, a], num[:, a, 0:C], rden[:, a, :], src[:, a],
                                                       ALU.mult, ALU.add).then_inc(attended, 1)
                    at_least(dve, aggregated2, n * 2)
                    for a in range(2):
                        dve.wait_ge(attended, n * 2 + a + 1)
                        apart(dve, dve_passed)
                        nc.vector.bn_stats(stats2[:, a, :], dst[:, a]).then_inc(measured2, 1)
                    at_least(dve, shifted2, n - 1)
                    for a in range(2):
                        dve.wait_ge(measured2, n * 2 + a + 1)
                        apart(dve, dve_passed)
                        nc.vector.bn_aggr(mv2[:, k, a, :], stats2[:, a, :]).then_inc(aggregated2, 1)

                def step(n, k):
                    inner_out(n, k)
                    advance(n, k)
                    measure(n + 2, k)
                    values_out(n + 1, 1 - k)
                    attend(n, k)
                pipeline(dve, step, **run)
                dve.wait_ge(counted, NC2)
                nc.vector.tensor_copy(gram[:, :], b_gram[:, 0:E]).then_inc(gram_done, 1)


def recurrence(nc, t2, out, ffn_w, ffn_wt, ffn_vt, gamma, beta, ident, ones, exponent, ln2_rstd, ln2_shift, gram, bank, agree):
    ctx = ExitStack()
    with ctx:
        def sb(name, shape, dtype=F32):
            return ctx.enter_context(nc.sbuf_tensor("sc_" + name, shape, dtype))

        def sem(name):
            return ctx.enter_context(nc.semaphore(name))

        E = C + 1
        I32 = mybir.dt.int32
        w = sb("w", [128, C])
        wT = sb("wT", [128, C])
        vT = sb("vT", [128, C])
        gb = sb("gb", [128, 2])
        scaled = sb("scaled", [128, C])
        fT = sb("fT", [128, C])
        prod = sb("prod", [128, C])
        cols = sb("cols", [128, 8])
        bn_rstd = sb("bn_rstd", [128, 1])
        rstd = sb("scan_rstd", [CH, NG, CH])
        shift = sb("scan_shift", [CH, NG, CH])
        start = sb("start", [128, COLS])
        final = sb("final", [128, COLS])
        gap = sb("gap", [128, B, NCH - 1])
        worst = sb("worst", [128, 1])
        worst_row = sb("worst_row", [1, 128])
        flag_f = sb("flag_f", [1, 1])
        flag = sb("flag", [1, 1], I32)
        consts, chain, pchain = sem("sc_consts"), sem("sc_chain"), sem("sc_pchain")
        rooted = sem("sc_rooted")

        with nc.Block() as block:
            @block.sync
            def _(sp):
                sp.dma_start(w[:, :], ffn_w).then_inc(consts, 16)
                sp.dma_start(wT[:, :], ffn_wt).then_inc(consts, 16)
                sp.dma_start(vT[:, :], ffn_vt).then_inc(consts, 16)
                sp.dma_start(gb[:, 0:1], gamma.rearrange("(p a) -> p a", a=1)).then_inc(consts, 16)
                sp.dma_start(gb[:, 1:2], beta.rearrange("(p a) -> p a", a=1)).then_inc(consts, 16)

            @block.tensor
            def _(pe):
                pe.wait_ge(consts, 80)
                nc.tensor.matmul(bank[0][:, 0:C], gram[:, 0:C], wT[:, :], start=True, stop=True).then_inc(pchain, 1)
                nc.tensor.matmul(bank[1][:, 0:1], wT[:, :], gram[:, C:E], start=True, stop=True).then_inc(pchain, 1)
                pe.wait_ge(chain, 1)
                nc.tensor.matmul(bank[2][:, 0:1], prod[:, :], ones[:, 0:1], start=True, stop=True).then_inc(pchain, 1)
                for i, table in enumerate((ln2_rstd, ln2_shift)):
                    for g in range(NG):
                        last = nc.tensor.transpose(bank[4 + i][0:CH, g * CH:(g + 1) * CH], table[:, g * CH:(g + 1) * CH],
                                                   ident[0:CH, 0:CH])
                last.then_inc(pchain, 1)
                pe.wait_ge(chain, 8)
                nc.tensor.transpose(bank[3][:, 0:C], scaled[:, :], ident[:, :]).then_inc(pchain, 1)

            @block.vector
            def _(dve):
                done = [0]

                def link(ins):
                    done[0] += 1
                    ins.then_inc(chain, 1)
                    dve.wait_ge(chain, done[0])

                mean, square, square_mean, var, root, scale = (cols[:, i:i + 1] for i in range(6))
                shift_bn = cols[:, 6:7]
                dve.wait_ge(consts, 80)
                dve.wait_ge(pchain, 1)
                link(nc.vector.tensor_tensor(prod[:, :], bank[0][:, 0:C], wT[:, :], ALU.mult))
                dve.wait_ge(pchain, 3)
                link(nc.vector.tensor_scalar(mean, bank[1][:, 0:1], 1.0 / (B * T), None, ALU.mult))
                link(nc.vector.tensor_scalar(square, bank[2][:, 0:1], 1.0 / (B * T), None, ALU.mult))
                link(nc.vector.tensor_tensor(square_mean, mean, mean, ALU.mult))
                link(nc.vector.tensor_tensor(var, square, square_mean, ALU.subtract))
                link(nc.vector.tensor_scalar(root, var, 0.0, BN_EPS, ALU.max, ALU.add))
                dve.wait_ge(rooted, 1)
                link(nc.vector.tensor_tensor(scale, bn_rstd[:, :], gb[:, 0:1], ALU.mult))
                link(nc.vector.tensor_scalar(scaled[:, :], w[:, :], scale, None, ALU.mult))
                link(nc.vector.tensor_tensor(cols[:, 7:8], mean, scale, ALU.mult))
                link(nc.vector.tensor_tensor(shift_bn, gb[:, 1:2], cols[:, 7:8], ALU.subtract))
                dve.wait_ge(pchain, 4)
                nc.vector.tensor_copy(rstd[:, :, :].rearrange("p a b -> p (a b)"), bank[4][0:CH, 0:NG * CH])
                nc.vector.tensor_copy(shift[:, :, :].rearrange("p a b -> p (a b)"), bank[5][0:CH, 0:NG * CH])
                dve.wait_ge(pchain, 5)
                nc.vector.tensor_copy(fT[:, :], bank[3][:, 0:C])
                nc.vector.memset(start[:, :], 0.5)

            @block.gpsimd
            def _(pool):
                pool.wait_ge(chain, 6)
                nc.gpsimd.tensor_tensor(bn_rstd[:, :], cols[:, 4:5], exponent[:, 0:1], ALU.pow).then_inc(rooted, 1)

        shift_bn = cols[:, 6:7]
        scan(nc, t2, None, CH - WARM, fT, vT, shift_bn, rstd, shift, start, final, ident, bank, "warm")
        hand_over(nc, start, final)
        scan(nc, t2, out, 0, fT, vT, shift_bn, rstd, shift, start, final, ident, bank, "main")

        compared, worst_turned = sem("sc_compared"), sem("sc_worst_turned")
        with nc.Block() as block:
            @block.vector
            def _(dve):
                done = [0]

                def link(ins):
                    done[0] += 1
                    ins.then_inc(compared, 1)
                    dve.wait_ge(compared, done[0])

                ends = final[:, :].rearrange("p (b c) -> p b c", b=B)[:, :, 0:NCH - 1]
                begins = start[:, :].rearrange("p (b c) -> p b c", b=B)[:, :, 1:NCH]
                link(nc.vector.tensor_tensor(gap[:, :, :], ends, begins, ALU.subtract))
                link(nc.vector.tensor_tensor(gap[:, :, :], gap[:, :, :], gap[:, :, :], ALU.mult))
                link(nc.vector.tensor_scalar(gap[:, :, :], gap[:, :, :], agree * abs(agree), None, ALU.is_le))
                link(nc.vector.tensor_reduce(worst[:, :], gap[:, :, :].rearrange("p a b -> p (a b)"), AX.X, ALU.min))
                dve.wait_ge(worst_turned, 1)
                link(nc.vector.tensor_reduce(worst_row[:, 0:1], bank[0][0:1, 0:128], AX.X, ALU.min))
                link(nc.vector.tensor_scalar(flag_f[:, :], worst_row[:, 0:1], -1.0, 1.0, ALU.mult, ALU.add))
                link(nc.vector.tensor_copy(flag[:, :], flag_f[:, :]))

            @block.tensor
            def _(pe):
                pe.wait_ge(compared, 4)
                nc.tensor.transpose(bank[0][0:1, 0:128], worst[:, :], ident[:, :]).then_inc(worst_turned, 1)

        again = nc.values_load(flag[0:1, 0:1], min_val=0, max_val=1)
        with nc.If(again > 0):
            with nc.Fori(0, NCH - 1):
                hand_over(nc, start, final)
                scan(nc, t2, out, 0, fT, vT, shift_bn, rstd, shift, start, final, ident, bank, "again")


def hand_over(nc, start, final):
    with nc.Block() as block:
        @block.vector
        def _(dve):
            begins = start[:, :].rearrange("p (b c) -> p b c", b=B)
            ends = final[:, :].rearrange("p (b c) -> p b c", b=B)
            nc.vector.tensor_copy(begins[:, :, 1:NCH], ends[:, :, 0:NCH - 1])
            nc.vector.memset(begins[:, :, 0:1], 0.0)


def scan(nc, t2, out, s0, fT, vT, shift_bn, rstd, shift, start, final, ident, bank, name):
    ctx = ExitStack()
    with ctx:
        def sb(label, shape):
            return ctx.enter_context(nc.sbuf_tensor(f"{name}_{label}", shape, F32))

        def sem(label):
            return ctx.enter_context(nc.semaphore(f"{name}_{label}"))

        NB = (CH - s0) // SB
        NT = NB * SB
        tb = sb("tb", [CH, 4, NG, SB, C])
        ub = sb("ub", [CH, 2, NG, SB, C])
        ob = sb("ob", [CH, 2, NG, SB, C])
        uT = sb("uT", [128, 2, COLS])
        y = sb("y", [128, 2, COLS])
        b_state, b_u, b_y = bank[0:2], bank[2:4], bank[4:6]
        loaded = [sem(f"loaded{i}") for i in range(2)]
        stored = [sem(f"stored{i}") for i in range(2)]
        u_scaled, u_made, u_turned, u_out = sem("u_scaled"), sem("u_made"), sem("u_turned"), sem("u_out")
        w_done, v_done, y_made, y_turned, summed = sem("w_done"), sem("v_done"), sem("y_made"), sem("y_turned"), sem("summed")
        final_out, passed = sem("final_out"), sem("passed")

        def steps(dram, j):
            return dram.rearrange("b t d -> (b t d)").rearrange("(g p s d) -> p g s d", g=NG, p=CH, s=CH)[:, :, bass.ds(j * SB + s0, SB), :]

        def slot4(tile, j):
            return tile[:, bass.ds(j % 4, 1)].rearrange("p o g s c -> p (o g) s c")

        short = NB < 8
        run = dict(first=-3, last=NB + 2, lo=2 if not short else NB + 2, hi=NB - 4 if not short else NB + 2)

        with nc.Block() as block:
            @block.sync
            def _(sp):
                def step(j, k):
                    if inside(j + 3, NB):
                        kl = 1 - k
                        if out is not None:
                            at_least(sp, summed, j * SB)
                        at_least(sp, u_made, j)
                        at_least(sp, loaded[kl], (j + 3) // 2 * 16)
                        sp.dma_start(slot4(tb, j + 3), steps(t2, j + 3)).then_inc(loaded[kl], 16)
                    if out is not None and inside(j - 1, NB):
                        sp.wait_ge(summed, j * SB)
                        sp.dma_start(steps(out, j - 1), ob[:, 1 - k]).then_inc(stored[1 - k], 16)
                pipeline(sp, step, **run)
                if out is not None:
                    for k in range(2):
                        sp.wait_ge(stored[k], NB // 2 * 16)

            @block.gpsimd
            def _(pool):
                def step(j, k):
                    j, k = j + 1, 1 - k
                    if not inside(j, NB):
                        return
                    pool.wait_ge(loaded[k], (j // 2 + 1) * 16)
                    at_least(pool, u_turned, (j - 1) * SB)
                    apart(pool, passed)
                    src = slot4(tb, j)
                    now = bass.ds(j * SB + s0, SB)
                    nc.gpsimd.tensor_tensor(ub[:, k], src, rstd[:, :, now].unsqueeze(3).broadcast_to([CH, NG, SB, C]),
                                            ALU.mult).then_inc(u_scaled, 1)
                    pool.wait_ge(u_scaled, j + 1)
                    apart(pool, passed)
                    nc.gpsimd.tensor_tensor(ub[:, k], ub[:, k], shift[:, :, now].unsqueeze(3).broadcast_to([CH, NG, SB, C]),
                                            ALU.add).then_inc(u_made, 1)
                pipeline(pool, step, **run)

            @block.tensor
            def _(pe):
                def turn_tokens(t, j, k, i):
                    if not inside(t, NT):
                        return
                    pe.wait_ge(u_made, j + 1)
                    at_least(pe, u_out, t - 1)
                    for g in range(NG):
                        mm = nc.tensor.transpose(b_u[i % 2][:, g * CH:(g + 1) * CH], ub[:, k, g, i, :], ident[0:CH, 0:CH])
                    mm.then_inc(u_turned, 1)

                def input_part(t, i):
                    if not inside(t, NT):
                        return
                    pe.wait_ge(u_out, t + 1)
                    at_least(pe, y_made, t - 1)
                    nc.tensor.matmul(b_state[i % 2][:, 0:COLS], fT[:, :], uT[:, i % 2, :], start=True, stop=False).then_inc(w_done, 1)

                def state_part(t, i):
                    if not inside(t, NT):
                        return
                    at_least(pe, y_made, t)
                    before = start[:, :] if isinstance(t, int) and t == 0 else y[:, 1 - i % 2, :]
                    nc.tensor.matmul(b_state[i % 2][:, 0:COLS], vT[:, :], before, start=False, stop=True).then_inc(v_done, 1)

                def turn_states(t, i):
                    if out is None or not inside(t, NT):
                        return
                    pe.wait_ge(y_made, t + 1)
                    at_least(pe, summed, t - 1)
                    for g in range(NG):
                        mm = nc.tensor.transpose(b_y[i % 2][0:CH, g * C:(g + 1) * C], y[:, i % 2, g * CH:(g + 1) * CH], ident[:, :])
                    mm.then_inc(y_turned, 1)

                def step(j, k):
                    for i in range(SB):
                        t = j * SB + i
                        ahead = (j, k, i + 2) if i + 2 < SB else (j + 1, 1 - k, i + 2 - SB)
                        turn_tokens(t + 2, *ahead)
                        state_part(t, i)
                        turn_states(t - 1, i + 1)
                        input_part(t + 1, i + 1)
                pipeline(pe, step, **run)

            @block.vector
            def _(dve):
                def turned_out(t, i):
                    if not inside(t, NT):
                        return
                    dve.wait_ge(u_turned, t + 1)
                    at_least(dve, w_done, t - 1)
                    nc.vector.tensor_copy(uT[:, i % 2, :], b_u[i % 2][:, 0:COLS]).then_inc(u_out, 1)

                def residual(t, j, k, i):
                    if out is None or not inside(t, NT):
                        return
                    dve.wait_ge(y_turned, t + 1)
                    dve.wait_ge(loaded[k], (j // 2 + 1) * 16)
                    at_least(dve, stored[k], j // 2 * 16)
                    nc.vector.tensor_tensor(ob[:, k, :, i, :], b_y[i % 2][0:CH, :].rearrange("p (g c) -> p g c", g=NG),
                                            slot4(tb, j)[:, :, i, :], ALU.add).then_inc(summed, 1)

                def step(j, k):
                    for i in range(SB):
                        t = j * SB + i
                        turned_out(t + 2, i + 2)
                        now = (j, k, i - 1) if i else (j - 1, 1 - k, SB - 1)
                        residual(t - 1, *now)
                pipeline(dve, step, **run)
                dve.wait_ge(y_made, NT)
                nc.vector.tensor_copy(final[:, :], y[:, 1, :]).then_inc(final_out, 1)

            @block.scalar
            def _(act):
                def step(j, k):
                    for i in range(SB):
                        t = j * SB + i
                        if not inside(t, NT):
                            continue
                        act.wait_ge(v_done, t + 1)
                        if out is not None:
                            at_least(act, y_turned, t - 1)
                        nc.scalar.activation(y[:, i % 2, :], b_state[i % 2][:, 0:COLS], ACT.Sigmoid,
                                             bias=shift_bn).then_inc(y_made, 1)
                pipeline(act, step, **run)


_DATA = ["x", "L0_conv_w_qkv", "L0_conv_pos_emb", "L0_conv_w_out", "L0_conv_b_out", "attn_wt", "L1_attn_b",
         "L1_ffn_W", "ffn_wt", "ffn_vt", "L1_ffn_gamma", "L1_ffn_beta"]
_CONSTS = ["ident", "head_mask", "v_mask", "shift_mask", "causal", "group", "keep"]


def constants():
    import numpy as np
    f = np.float32
    lane = np.arange(128)
    head_mask = (lane[:, None] // HD == np.arange(HEADS)[None]).astype(f)
    v_mask = (np.arange(2 * WIN)[:, None] // WIN == (lane[None] // HD) % 2).astype(f)
    r, c = np.arange(WIN) // WS, np.arange(WIN) % WS
    far = f(-1e30)
    upper = np.where((r[:, None] >= WS - DISP) != (r[None] >= WS - DISP), far, f(0))
    left = np.where((c[:, None] >= WS - DISP) != (c[None] >= WS - DISP), far, f(0))
    shift_mask = np.zeros((128, NWR, NWC, WIN), f)
    for start in (0, WPAD):
        shift_mask[start:start + WIN, NWR - 1] += upper[:, None]
        shift_mask[start:start + WIN, :, NWC - 1] += left[:, None]
    pairs = np.zeros((128, NWR, NWC // 2, WIN), f)
    pairs[0:WPAD] = shift_mask[0:WPAD, :, 0::2]
    pairs[WPAD:] = shift_mask[WPAD:, :, 1::2]
    causal = (np.arange(CH)[:, None] <= np.arange(CH)[None]).astype(f)
    group = (lane[:, None] // GROUP == lane[None] // GROUP).astype(f)
    keep = np.ones((128, NC2), f)
    keep[:, ::NCH // 2] = 0
    return dict(ident=np.eye(128, dtype=f), head_mask=head_mask, v_mask=v_mask,
                shift_mask=np.ascontiguousarray(pairs.reshape(128, -1)), causal=causal, group=group, keep=keep)


def kernel(**inputs):
    import numpy as np
    import concourse.bacc as bacc
    from concourse.bass_utils import run_bass_kernel_spmd

    data = {k: np.ascontiguousarray(v) for k, v in inputs.items()}
    data["x"] = data["x"].reshape(B, T, C)
    data["attn_wt"] = np.ascontiguousarray(data["L1_attn_W"].T)
    data["ffn_wt"] = np.ascontiguousarray(data["L1_ffn_W"].T)
    data["ffn_vt"] = np.ascontiguousarray(data["L1_ffn_V"].T)
    data.update(constants())
    nc = bacc.Bacc("TRN2", target_bir_lowering=False, num_devices=1)
    arrays, args = {}, []
    for name in _DATA + _CONSTS:
        arrays[f"in_{name}"] = data[name]
        args.append(nc.dram_tensor(f"in_{name}", data[name].shape, F32, kind="ExternalInput").ap())
    out = nc.dram_tensor("out", (B, T, C), F32, kind="ExternalOutput").ap()
    build(nc, *args, out)
    result = run_bass_kernel_spmd(nc, [arrays], core_ids=[0])
    return result.results[0]["out"].reshape(B, H, W, C)
```

```python
import itertools
from contextlib import ExitStack

import concourse.bass as bass
from concourse import mybir

F32 = mybir.dt.float32
ALU = mybir.AluOpType
ACT = mybir.ActivationFunctionType
AX = mybir.AxisListType

B, H, W, C = 16, 56, 56, 128
T = H * W
WS, DISP = 7, 3
HEADS, HD = 4, 32
WIN = WS * WS
NWR = H // WS
NWC = W // WS
ROWTOK = WS * W
NU = B * NWR
WPAD = 64
GROUP = 4
GN_EPS, LN_EPS, BN_EPS, DEN_EPS = 1e-5, 1e-5, 1e-5, 1e-6
CH = 112
NCH = T // CH
NC2 = B * NCH // 2
GI = 4
NG = B // GI
COLS = B * NCH
SB = 4
NSB = CH // SB
WARM = 16
AGREE = 5e-7


def at_least(eng, sem, value):
    if not isinstance(value, int) or value > 0:
        eng.wait_ge(sem, value)


def pipeline(eng, step, first, last, lo, hi, unroll=2):
    for n in range(first, lo):
        step(n, n % unroll)
    if lo < hi:
        with eng.Fori(lo // unroll, hi // unroll) as m:
            for k in range(unroll):
                step(m * unroll + k, k)
    for n in range(hi, last):
        step(n, n % unroll)


def apart(eng, passed):
    eng.sem_inc(passed, 1)


def inside(n, count):
    return not isinstance(n, int) or 0 <= n < count


def build(nc, x, w_qkv, pos_emb, w_out, b_out, attn_wt, attn_b, ffn_w, ffn_wt, ffn_vt, gamma, beta,
          ident_d, shift_mask_d, causal_d, group_d, keep_d, out, agree=AGREE):
    x1 = nc.dram_tensor("x1", (B, T, C), F32, kind="Internal").ap()
    t2 = nc.dram_tensor("t2", (B, T, C), F32, kind="Internal").ap()
    top = ExitStack()

    def sb(name, shape, stack=top):
        return stack.enter_context(nc.sbuf_tensor("k_" + name, shape, F32))

    bank = [top.enter_context(nc.psum_tensor(f"k_bank{i}", [128, 512], F32)) for i in range(8)]
    ident = sb("ident", [128, 128])
    ones = sb("ones", [128, 128])
    position = sb("position", [128, WIN])
    exponent = sb("exponent", [128, B])
    gn_rstd = sb("gn_rstd", [128, B])
    gn_shift = sb("gn_shift", [128, B])
    ln2_table = sb("ln2_table", [CH, 2, COLS])
    gram = sb("gram", [128, C + 1])
    gn_statistics(nc, x, pos_emb, position, ident_d, group_d, ident, ones, exponent, gn_rstd, gn_shift, bank)
    window_attention(nc, x, x1, w_qkv, w_out, b_out, shift_mask_d, position, ident, gn_rstd, gn_shift, bank)
    linear_attention(nc, x1, t2, attn_wt, attn_b, causal_d, keep_d, ident, exponent, ln2_table, gram, bank)
    recurrence(nc, t2, out, ffn_w, ffn_wt, ffn_vt, gamma, beta, ident, ones, exponent, ln2_table, gram,
               bank, agree)
    top.close()


def gn_statistics(nc, x, pos_emb, position, ident_d, group_d, ident, ones, exponent, gn_rstd, gn_shift, bank):
    P, TT = CH, T // CH
    ctx = ExitStack()
    with ctx:
        def sb(name, shape):
            return ctx.enter_context(nc.sbuf_tensor("gn_" + name, shape, F32))

        def sem(name):
            return ctx.enter_context(nc.semaphore(name))

        xi = sb("xi", [P, 2, TT * C])
        sq = sb("sq", [P, 2, TT * C])
        part = sb("part", [P, 2, 2, C])
        group = sb("group", [128, 128])
        sums = sb("sums", [128, 2 * B])
        moments = sb("moments", [128, 2, B])
        work = sb("work", [128, 3, B])
        consts = sem("gn_consts")
        loaded = [sem(f"gn_loaded{i}") for i in range(2)]
        placed = sem("gn_placed")
        ones_set, exponent_set = sem("gn_ones"), sem("gn_exponent")
        squared = sem("gn_squared")
        reduced = sem("gn_reduced")
        summed = sem("gn_summed")
        sums_out = sem("gn_sums_out")
        grouped = sem("gn_grouped")
        chain, rooted = sem("gn_chain"), sem("gn_rooted")

        with nc.Block() as block:
            @block.sync
            def _(sp):
                sp.dma_start(ident[:, :], ident_d).then_inc(consts, 16)
                sp.dma_start(group[:, :], group_d).then_inc(consts, 16)
                rows = iter(range(WIN))
                for n in range(B):
                    at_least(sp, squared, n - 1)
                    at_least(sp, reduced, n - 1)
                    sp.dma_start(xi[:, n % 2, :], x[n].rearrange("t c -> (t c)")
                                 .rearrange("(p f) -> p f", p=P)).then_inc(loaded[n % 2], 16)
                    if n == 0:
                        sp.wait_ge(ones_set, 1)
                    for q in itertools.islice(rows, 4):
                        r, c = q // WS, q % WS
                        src = pos_emb[WS - 1 - r:2 * WS - 1 - r, WS - 1 - c:2 * WS - 1 - c]
                        sp.dma_start(position[q:q + 1, :].rearrange("p (a b) -> p a b", a=WS),
                                     src.unsqueeze(0)).then_inc(placed, 16)
                sp.wait_ge(placed, 16 * WIN)
                sp.dma_start(position[WPAD:WPAD + WIN, :], position[0:WIN, :]).then_inc(placed, 16)
                sp.wait_ge(placed, 16 * (WIN + 1))

            @block.scalar
            def _(act):
                def step(n, k):
                    act.wait_ge(loaded[k], (n // 2 + 1) * 16)
                    at_least(act, reduced, n - 1)
                    nc.scalar.activation(sq[:, k, :], xi[:, k, :], ACT.Square).then_inc(squared, 1)
                pipeline(act, step, 0, B, 2, B)

            @block.vector
            def _(dve):
                nc.vector.memset(position[:, :], 0.0)
                nc.vector.memset(ones[:, :], 1.0).then_inc(ones_set, 1)

                def step(n, k):
                    dve.wait_ge(loaded[k], (n // 2 + 1) * 16)
                    at_least(dve, summed, n - 1)
                    nc.vector.tensor_reduce(part[:, k, 0, :], xi[:, k, :].rearrange("p (t c) -> p c t", c=C),
                                            AX.X, ALU.add)
                    dve.wait_ge(squared, n + 1)
                    nc.vector.tensor_reduce(part[:, k, 1, :], sq[:, k, :].rearrange("p (t c) -> p c t", c=C),
                                            AX.X, ALU.add).then_inc(reduced, 1)
                pipeline(dve, step, 0, B, 2, B)
                dve.wait_ge(summed, B)
                nc.vector.tensor_copy(sums[:, :], bank[0][:, 0:2 * B]).then_inc(sums_out, 1)
                dve.wait_ge(grouped, 1)
                done = [0]

                def link(ins):
                    done[0] += 1
                    ins.then_inc(chain, 1)
                    dve.wait_ge(chain, done[0])
                link(nc.vector.tensor_scalar(moments[:, :, :].rearrange("p a b -> p (a b)"), bank[1][:, 0:2 * B],
                                             1.0 / (T * GROUP), None, ALU.mult))
                mean, square = moments[:, 0, :], moments[:, 1, :]
                link(nc.vector.tensor_tensor(work[:, 0, :], mean, mean, ALU.mult))
                link(nc.vector.tensor_tensor(work[:, 1, :], square, work[:, 0, :], ALU.subtract))
                link(nc.vector.tensor_scalar(work[:, 2, :], work[:, 1, :], 0.0, GN_EPS, ALU.max, ALU.add))
                dve.wait_ge(rooted, 1)
                link(nc.vector.scalar_tensor_tensor(gn_shift[:, :], mean, -1.0, gn_rstd[:, :], ALU.mult, ALU.mult))

            @block.gpsimd
            def _(pool):
                nc.gpsimd.memset(exponent[:, :], -0.5).then_inc(exponent_set, 1)
                pool.wait_ge(exponent_set, 1)
                pool.wait_ge(chain, 4)
                nc.gpsimd.tensor_tensor(gn_rstd[:, :], work[:, 2, :], exponent[:, :], ALU.pow).then_inc(rooted, 1)

            @block.tensor
            def _(pe):
                pe.wait_ge(ones_set, 1)
                def step(n, k):
                    pe.wait_ge(reduced, n + 1)
                    for j in range(2):
                        mm = nc.tensor.matmul(bank[0][:, bass.ds(n + j * B, 1)], part[:, k, j, :],
                                              ones[0:P, 0:1], start=True, stop=True)
                    mm.then_inc(summed, 1)
                pipeline(pe, step, 0, B, 2, B)
                pe.wait_ge(consts, 32)
                pe.wait_ge(sums_out, 1)
                nc.tensor.matmul(bank[1][:, 0:2 * B], group[:, :], sums[:, :], start=True, stop=True).then_inc(grouped, 1)


def window_attention(nc, x, x1, w_qkv, w_out, b_out, shift_mask_d, position, ident, gn_rstd, gn_shift, bank):
    ctx = ExitStack()
    with ctx:
        def sb(name, shape):
            return ctx.enter_context(nc.sbuf_tensor("wa_" + name, shape, F32))

        def sem(name):
            return ctx.enter_context(nc.semaphore(name))

        HW_ = NWC // 2
        HC = HW_ * WIN
        wqkv = sb("wqkv", [128, 3 * C])
        wout = sb("wout", [128, C])
        bout = sb("bout", [CH, C])
        shift_mask = sb("shift_mask", [128, NWR, 2, 2, WIN])
        bias = sb("bias", [128, NWR, 2, 2, WIN])
        xw = sb("xw", [CH, 2, 4, C])
        xb = sb("xb", [CH, 8, 4, C])
        xT = sb("xT", [128, 2, NWC, WIN])
        qT = [sb(f"qT{i}", [128, ROWTOK + WPAD - WIN]) for i in range(2)]
        kb = sb("kb", [128, 2, HEADS, ROWTOK])
        prob = sb("prob", [128, 2, 2, 2, HEADS, WPAD])
        peak = sb("peak", [128, 2, 2 * HEADS])
        total = sb("total", [128, 2, 2 * HEADS])
        inv = sb("inv", [128, 2, 2 * HEADS])
        vb = sb("vb", [128, 2, 2, HW_, 2, 2, HD])
        pT = sb("pT", [128, 2, 2, 2, 128])
        oT = sb("oT", [128, 2, WS, W])
        y = sb("y", [CH, 2, 4, C])
        b_tx, b_q, b_k, b_v, b_s, b_pt, b_ot, b_y = bank

        consts = sem("wa_consts")
        prep = sem("wa_prep")
        loaded = [sem(f"wa_loaded{i}") for i in range(2)]
        stored = [sem(f"wa_stored{i}") for i in range(2)]
        x_turned, x_normed = sem("wa_x_turned"), sem("wa_x_normed")
        q_ready, k_ready = sem("wa_q_ready"), sem("wa_k_ready")
        q_out, k_spread = sem("wa_q_out"), sem("wa_k_spread")
        v_ready, v_out = sem("wa_v_ready"), sem("wa_v_out")
        scored, biased, peaked = sem("wa_scored"), sem("wa_biased"), sem("wa_peaked")
        lowered, raised, totalled, inverted = sem("wa_lowered"), sem("wa_raised"), sem("wa_totalled"), sem("wa_inverted")
        weighted = sem("wa_weighted")
        p_turned, p_out = sem("wa_p_turned"), sem("wa_p_out")
        attended, o_out = sem("wa_attended"), sem("wa_o_out")
        projected, summed = sem("wa_projected"), sem("wa_summed")
        passed = sem("wa_passed")
        x_kept = sem("wa_x_kept")

        def rows(dram, n, first, count):
            image, wr = n // NWR, n % NWR
            r = (wr * WS + (DISP + first)) % H
            return dram[bass.ds(image, 1), bass.ds(r * W, count * W), :].rearrange("a t c -> (a t) c")

        def kept(n):
            return xb[:, bass.ds(n % 8, 1)].rearrange("p s a b -> p (s a) b")

        run = dict(first=-3, last=NU + 3, lo=6, hi=NU - 4)

        with nc.Block() as block:
            @block.sync
            def _(sp):
                sp.dma_start(wqkv[:, :], w_qkv).then_inc(consts, 16)
                sp.dma_start(wout[:, :], w_out).then_inc(consts, 16)
                sp.dma_start(bout[:, :], bass.AP(b_out.tensor, 0, [[0, CH], [1, C]])).then_inc(consts, 16)
                sp.dma_start(shift_mask[:, :, :, :, :].rearrange("p a b c d -> p (a b c d)"), shift_mask_d).then_inc(consts, 16)
                sp.wait_ge(prep, 2)

                def step(n, k):
                    if inside(n + 3, NU):
                        at_least(sp, x_turned, n + 2)
                        at_least(sp, x_kept, n + 2)
                        kl = 1 - k
                        for tile, count in ((slice(0, 2), 4), (2, 2), (3, 1)):
                            first = {4: 0, 2: 4, 1: 6}[count]
                            src = rows(x, n + 3, first, count)
                            if count == 4:
                                sp.dma_start(xw[:, kl, 0:2, :], src.rearrange("(a p) c -> p a c", p=CH)).then_inc(loaded[kl], 16)
                            else:
                                sp.dma_start(xw[0:count * W, kl, tile, :], src).then_inc(loaded[kl], 16)
                    if inside(n - 2, NU):
                        sp.wait_ge(summed, n - 1)
                        sp.dma_start(rows(x1, n - 2, 0, 4).rearrange("(a p) c -> p a c", p=CH), y[:, k, 0:2, :]).then_inc(stored[k], 16)
                        sp.dma_start(rows(x1, n - 2, 4, 2), y[:, k, 2, :]).then_inc(stored[k], 16)
                        sp.dma_start(rows(x1, n - 2, 6, 1), y[0:W, k, 3, :]).then_inc(stored[k], 16)
                pipeline(sp, step, **run)
                for k in range(2):
                    sp.wait_ge(stored[k], NU // 2 * 48)

            @block.tensor
            def _(pe):
                pe.wait_ge(consts, 64)
                pe.wait_ge(prep, 2)

                def scores(n, k, h):
                    if not inside(n, NU):
                        return
                    pe.wait_ge(q_out, n + 1)
                    pe.wait_ge(k_spread, n + 1)
                    at_least(pe, biased, n * 2 + h)
                    for w in range(HW_):
                        c = (h * HW_ + w) * WIN
                        part = slice(WPAD * (w % 2), WPAD * (w % 2) + WPAD)
                        mm = nc.tensor.matmul(b_s[part, (w // 2) * HEADS * WIN:(w // 2 + 1) * HEADS * WIN],
                                              qT[k][:, c:c + WPAD], kb[:, k, :, c:c + WIN], start=True, stop=True)
                    mm.then_inc(scored, 1)

                def turn_probabilities(n, k, h):
                    if not inside(n, NU):
                        return
                    pe.wait_ge(weighted, n * 2 + h + 1)
                    at_least(pe, p_out, n * 2 + h)
                    for p in range(2):
                        for hp in range(2):
                            q = p * 2 + hp
                            mm = nc.tensor.transpose(b_pt[:, q * 128:(q + 1) * 128],
                                                     prob[:, k, h, p, 2 * hp:2 * hp + 2, :].rearrange("p a b -> p (a b)"), ident[:, :])
                    mm.then_inc(p_turned, 1)

                def attend(n, k, h):
                    if not inside(n, NU):
                        return
                    pe.wait_ge(p_out, n * 2 + h + 1)
                    pe.wait_ge(v_out, n * 2 + h + 1)
                    at_least(pe, o_out, n)
                    for w in range(HW_):
                        for hp in range(2):
                            c = (h * HW_ + w) * WIN
                            i = WPAD * (w % 2)
                            mm = nc.tensor.matmul(b_ot[64 * hp:64 * hp + 64, c:c + WIN],
                                                  vb[:, k, h, w, hp].rearrange("p a b -> p (a b)"),
                                                  pT[:, h, w // 2, hp, i:i + WIN], start=True, stop=True)
                    mm.then_inc(attended, 1)

                def queries(n, k):
                    if inside(n, NU):
                        pe.wait_ge(x_normed, n + 1)
                        at_least(pe, q_out, n)
                        nc.tensor.matmul(b_q[:, 0:ROWTOK], wqkv[:, 0:C], xT[:, k], start=True, stop=True).then_inc(q_ready, 1)

                def keys(n, k):
                    if inside(n, NU):
                        at_least(pe, k_spread, n)
                        nc.tensor.matmul(b_k[:, 0:ROWTOK], wqkv[:, C:2 * C], xT[:, k], start=True, stop=True).then_inc(k_ready, 1)

                def values(n, k, h):
                    if not inside(n, NU):
                        return
                    at_least(pe, v_out, n * 2 + h)
                    for w in range(HW_):
                        for odd in range(2):
                            mm = nc.tensor.matmul(b_v[odd * WPAD:odd * WPAD + WIN, w * 2 * HD:(w + 1) * 2 * HD],
                                                  xT[:, k, h * HW_ + w, :],
                                                  wqkv[:, 2 * C:3 * C].rearrange("p (a b c) -> p a b c", a=2, b=2)[:, :, odd, :],
                                                  start=True, stop=True)
                    mm.then_inc(v_ready, 1)

                def turn_tokens(n, k):
                    if not inside(n, NU):
                        return
                    pe.wait_ge(loaded[k], (n // 2 + 1) * 48)
                    at_least(pe, x_normed, n)
                    for t in range(4):
                        p = CH if t < 3 else W
                        mm = nc.tensor.transpose(b_tx[:, t * CH:t * CH + p], xw[0:p, k, t, :], ident[0:p, 0:p])
                    mm.then_inc(x_turned, 1)

                def project(n, k):
                    if not inside(n, NU):
                        return
                    pe.wait_ge(o_out, n + 1)
                    at_least(pe, summed, n)
                    for t in range(4):
                        p = CH if t < 3 else W
                        ot = oT[:, k, 2 * t:2 * t + p // W, :].rearrange("p a b -> p (a b)")
                        mm = nc.tensor.matmul(b_y[0:p, t * C:(t + 1) * C], ot, wout[:, :], start=True, stop=True)
                    mm.then_inc(projected, 1)

                def step(n, k):
                    scores(n, k, 0)
                    turn_probabilities(n - 1, 1 - k, 0)
                    queries(n + 1, 1 - k)
                    values(n + 1, 1 - k, 0)
                    attend(n - 1, 1 - k, 0)
                    scores(n, k, 1)
                    turn_probabilities(n - 1, 1 - k, 1)
                    keys(n + 1, 1 - k)
                    attend(n - 1, 1 - k, 1)
                    values(n + 1, 1 - k, 1)
                    project(n - 2, k)
                    turn_tokens(n + 2, k)
                pipeline(pe, step, **run)

            @block.vector
            def _(dve):
                nc.vector.memset(b_y[:, :], 0.0)
                nc.vector.memset(kb[:, :, :, :], 0.0)
                nc.vector.memset(vb[:, :, :, :, :, :, :], 0.0)
                nc.vector.memset(prob[:, :, :, :, :, :], 0.0).then_inc(prep, 1)
                for i in range(2):
                    nc.vector.memset(xw[:, i, 3, :], 0.0)
                    last = nc.vector.memset(qT[i][:, :], 0.0)
                last.then_inc(prep, 1)
                dve.wait_ge(consts, 64)
                dve.wait_ge(prep, 2)
                nc.vector.tensor_tensor(bias[:, :, :, :, :].rearrange("p a b c d -> p (a b c) d"),
                                        shift_mask[:, :, :, :, :].rearrange("p a b c d -> p (a b c) d"),
                                        position[:, :].unsqueeze(1).broadcast_to([128, NWR * 4, WIN]), ALU.add).then_inc(prep, 1)
                dve.wait_ge(prep, 3)

                def bias_and_peak(n, k, h):
                    if not inside(n, NU):
                        return
                    dve.wait_ge(scored, n * 2 + h + 1)
                    at_least(dve, p_turned, (n - 2) * 2 + h + 1)
                    if isinstance(n, int):
                        bs = bias[:, n % NWR, h]
                    else:
                        bs = bias[:, bass.ds(n % NWR, 1), h].rearrange("p a b c -> p (a b) c")
                    bs = bs.unsqueeze(2).broadcast_to([128, 2, HEADS, WIN])
                    nc.vector.tensor_tensor(prob[:, k, h, :, :, 0:WIN], b_s[:, 0:2 * HEADS * WIN].rearrange("p (a b c) -> p a b c", a=2, b=HEADS),
                                            bs, ALU.add).then_inc(biased, 1)
                    dve.wait_ge(biased, n * 2 + h + 1)
                    at_least(dve, lowered, n * 2 + h - 1)
                    nc.vector.tensor_reduce(peak[:, h, :], prob[:, k, h].rearrange("p a b c -> p (a b) c")[:, :, 0:WIN], AX.X, ALU.max).then_inc(peaked, 1)

                def totals(n, k, h):
                    if not inside(n, NU):
                        return
                    dve.wait_ge(raised, n * 2 + h + 1)
                    nc.vector.tensor_reduce(total[:, h, :], prob[:, k, h].rearrange("p a b c -> p (a b) c")[:, :, 0:WIN], AX.X, ALU.add).then_inc(totalled, 1)
                    dve.wait_ge(totalled, n * 2 + h + 1)
                    at_least(dve, weighted, n * 2 + h - 1)
                    nc.vector.reciprocal(inv[:, h, :], total[:, h, :]).then_inc(inverted, 1)

                def residual(n, k):
                    if not inside(n, NU):
                        return
                    dve.wait_ge(projected, n + 1)
                    dve.wait_ge(x_kept, n + 1)
                    at_least(dve, stored[k], (n // 2) * 48)
                    nc.vector.tensor_tensor(y[:, k].rearrange("p a b -> p (a b)"), b_y[0:CH, :],
                                            kept(n).rearrange("p a b -> p (a b)"), ALU.add).then_inc(summed, 1)

                def queries_out(n, k):
                    if not inside(n, NU):
                        return
                    dve.wait_ge(q_ready, n + 1)
                    at_least(dve, scored, (n - 1) * 2)
                    nc.vector.tensor_scalar(qT[k][:, 0:ROWTOK], b_q[:, 0:ROWTOK],
                                            float(HD) ** -0.5, None, ALU.mult).then_inc(q_out, 1)

                def values_out(n, k, h):
                    if not inside(n, NU):
                        return
                    dve.wait_ge(v_ready, n * 2 + h + 1)
                    at_least(dve, attended, (n - 2) * 2 + h + 1)
                    for odd in range(2):
                        rows_ = slice(odd * WPAD, odd * WPAD + WIN)
                        last = nc.vector.tensor_copy(vb[rows_, k, h, :, :, odd, :].rearrange("p w a c -> p (w a) c"),
                                                     b_v[rows_, 0:HW_ * 2 * HD].rearrange("p (w c) -> p w c", c=HD))
                    last.then_inc(v_out, 1)

                def step(n, k):
                    totals(n - 1, 1 - k, 1)
                    residual(n - 3, 1 - k)
                    bias_and_peak(n, k, 0)
                    queries_out(n + 1, 1 - k)
                    values_out(n + 1, 1 - k, 0)
                    bias_and_peak(n, k, 1)
                    totals(n, k, 0)
                    values_out(n + 1, 1 - k, 1)
                pipeline(dve, step, **run)

            @block.scalar
            def _(act):
                act.wait_ge(prep, 2)

                def normalise(n, k):
                    if not inside(n, NU):
                        return
                    act.wait_ge(x_turned, n + 1)
                    at_least(act, v_ready, (n - 2) * 2 + 2)
                    at_least(act, k_ready, n - 1)
                    src = b_tx[:, 0:ROWTOK].rearrange("p (r c) -> p r c", r=WS)
                    image = bass.ds(n // NWR, 1)
                    windows = xT[:, k].rearrange("p w (r c) -> p w r c", r=WS)
                    edge = WS - DISP
                    for dst, s in ((windows[:, 0:NWC - 1], src[:, :, DISP:W - edge].rearrange("p r (w c) -> p w r c", c=WS)),
                                   (windows[:, NWC - 1, :, 0:edge], src[:, :, W - edge:W]),
                                   (windows[:, NWC - 1, :, edge:WS], src[:, :, 0:DISP])):
                        last = nc.scalar.activation(dst, s, ACT.Identity,
                                                    bias=gn_shift[:, image], scale=gn_rstd[:, image])
                    last.then_inc(x_normed, 1)

                def keys_out(n, k):
                    if not inside(n, NU):
                        return
                    act.wait_ge(k_ready, n + 1)
                    at_least(act, scored, (n - 1) * 2)
                    for h in range(HEADS):
                        part = slice(HD * h, HD * h + HD)
                        last = nc.scalar.activation(kb[part, k, h, :], b_k[part, 0:ROWTOK], ACT.Copy)
                    last.then_inc(k_spread, 1)

                def exps(n, k, h):
                    if inside(n, NU):
                        act.wait_ge(lowered, n * 2 + h + 1)
                        flat = prob[:, k, h].rearrange("p a b c -> p (a b) c")[:, :, 0:WIN]
                        nc.scalar.activation(flat, flat, ACT.Exp).then_inc(raised, 1)

                def probabilities_out(n, k, h):
                    if not inside(n, NU):
                        return
                    act.wait_ge(p_turned, n * 2 + h + 1)
                    at_least(act, attended, n * 2 + h - 1)
                    nc.scalar.activation(pT[:, h].rearrange("p a b c -> p (a b c)"), b_pt[:, :], ACT.Copy).then_inc(p_out, 1)

                def attended_out(n, k):
                    if not inside(n, NU):
                        return
                    act.wait_ge(attended, n * 2 + 2)
                    at_least(act, projected, n - 1)
                    src = b_ot[:, 0:ROWTOK].rearrange("p (w r c) -> p w r c", w=NWC, r=WS)
                    dst = oT[:, k]
                    nc.scalar.activation(dst[:, :, DISP:W - (WS - DISP)].rearrange("p r (w c) -> p w r c", c=WS),
                                         src[:, 0:NWC - 1], ACT.Copy)
                    nc.scalar.activation(dst[:, :, W - (WS - DISP):W], src[:, NWC - 1, :, 0:WS - DISP], ACT.Copy)
                    nc.scalar.activation(dst[:, :, 0:DISP], src[:, NWC - 1, :, WS - DISP:WS], ACT.Copy).then_inc(o_out, 1)

                def step(n, k):
                    exps(n - 1, 1 - k, 1)
                    probabilities_out(n - 1, 1 - k, 0)
                    exps(n, k, 0)
                    probabilities_out(n - 1, 1 - k, 1)
                    keys_out(n + 1, 1 - k)
                    attended_out(n - 1, 1 - k)
                    normalise(n + 2, k)
                pipeline(act, step, **run)

            @block.gpsimd
            def _(pool):
                pool.wait_ge(consts, 64)
                pool.wait_ge(prep, 2)

                def lower(n, k, h):
                    if not inside(n, NU):
                        return
                    pool.wait_ge(peaked, n * 2 + h + 1)
                    s = prob[:, k, h].rearrange("p a b c -> p (a b) c")[:, :, 0:WIN]
                    nc.gpsimd.tensor_tensor(s, s, peak[:, h, :].unsqueeze(2).broadcast_to([128, 2 * HEADS, WIN]),
                                            ALU.subtract).then_inc(lowered, 1)

                def weigh(n, k, h):
                    if not inside(n, NU):
                        return
                    pool.wait_ge(inverted, n * 2 + h + 1)
                    s = prob[:, k, h].rearrange("p a b c -> p (a b) c")[:, :, 0:WIN]
                    nc.gpsimd.tensor_tensor(s, s, inv[:, h, :].unsqueeze(2).broadcast_to([128, 2 * HEADS, WIN]),
                                            ALU.mult).then_inc(weighted, 1)

                def keep_tokens(n, k):
                    if not inside(n, NU):
                        return
                    pool.wait_ge(loaded[k], (n // 2 + 1) * 48)
                    at_least(pool, summed, n - 7)
                    apart(pool, passed)
                    nc.gpsimd.tensor_tensor(kept(n), xw[:, k], bout[:, :].unsqueeze(1).broadcast_to([CH, 4, C]),
                                            ALU.add).then_inc(x_kept, 1)

                def step(n, k):
                    weigh(n - 1, 1 - k, 1)
                    lower(n, k, 0)
                    weigh(n, k, 0)
                    lower(n, k, 1)
                    keep_tokens(n + 2, k)
                pipeline(pool, step, **run)


def linear_attention(nc, x1, t2, attn_wt, attn_b, causal_d, keep_d, ident, exponent, ln2_table, gram, bank):
    ctx = ExitStack()
    with ctx:
        def sb(name, shape):
            return ctx.enter_context(nc.sbuf_tensor("la_" + name, shape, F32))

        def sem(name):
            return ctx.enter_context(nc.semaphore(name))

        E = C + 1
        UNITS = NCH // 2
        S = 4
        XS = 8
        AHEAD = 7
        wt = sb("wt", [128, 3 * C])
        bqk = sb("bqk", [128, 2])
        bv = sb("bv", [CH, C])
        causal = sb("causal", [CH, CH])
        keep = sb("keep", [128, NC2])
        xc = sb("xc", [CH, XS, 2, C])
        stats = sb("stats", [CH, S, 2, 2, 6])
        mv = sb("mv", [CH, S, 2, 2, 2])
        spread = sb("spread", [CH, 4])
        minus = sb("minus", [CH, 4])
        ln = sb("ln", [CH, S, 2, 2, 2])
        u = sb("u", [CH, S, 2, C])
        uT = sb("uT", [128, S, 2 * CH])
        raised = sb("raised", [128, S, 2, 2 * CH])
        positive = sb("positive", [128, S, 2, 2 * CH])
        fqk = sb("fqk", [128, S, 2, 2 * CH])
        ve = sb("ve", [CH, S, 2, E])
        aT = sb("aT", [CH, S, 2, CH])
        kt = sb("kt", [CH, S, 2, C])
        state = sb("state", [128, S, 2, E])
        carried = sb("carried", [128, E])
        den = sb("den", [CH, 2, 1])
        rden = sb("rden", [CH, 2, 1])
        tn = sb("tn", [CH, XS, 2, C])
        u2 = sb("u2", [CH, S, 2, E])
        zero = sb("zero", [128, C + E])
        b_u, b_qk, b_v, b_kt, b_at, b_kv, b_num, b_gram = bank

        consts, prep = sem("la_consts"), sem("la_prep")
        loaded = [sem(f"la_loaded{i}") for i in range(XS)]
        stored = [sem(f"la_stored{i}") for i in range(XS)]
        measured, aggregated = sem("la_measured"), sem("la_aggregated")
        spread_out, minus_out, rooted, shifted = sem("la_spread_out"), sem("la_minus_out"), sem("la_rooted"), sem("la_shifted")
        tabled = sem("la_tabled")
        normed, u_turned, u_out = sem("la_normed"), sem("la_u_turned"), sem("la_u_out")
        qk_ready, qk_raised, qk_out = sem("la_qk_ready"), sem("la_qk_raised"), sem("la_qk_out")
        passed = sem("la_passed")
        v_ready, v_out = sem("la_v_ready"), sem("la_v_out")
        a_ready, a_out = sem("la_a_ready"), sem("la_a_out")
        k_turned, k_out = sem("la_k_turned"), sem("la_k_out")
        kv_ready, moved, advanced = sem("la_kv_ready"), sem("la_moved"), sem("la_advanced")
        num_ready, den_ready, den_inv, attended = sem("la_num_ready"), sem("la_den_ready"), sem("la_den_inv"), sem("la_attended")
        normed2, counted, gram_done = sem("la_normed2"), sem("la_counted"), sem("la_gram_done")

        def chunks(dram, n):
            image, part = n // UNITS, n % UNITS
            return dram[bass.ds(image, 1), bass.ds(part * (2 * CH), 2 * CH), :].rearrange("o (a p) c -> p (o a) c", p=CH)

        ROWS = NC2 + AHEAD
        run = dict(first=-4, last=NC2 + 8, lo=16, hi=NC2 - 8, unroll=XS)

        with nc.Block() as block:
            @block.sync
            def _(sp):
                sp.dma_start(wt[:, :], attn_wt).then_inc(consts, 16)
                sp.dma_start(bqk[:, :], attn_b[0:2 * C].rearrange("(a p) -> p a", p=C), allow_slow_non_contiguous=True).then_inc(consts, 16)
                sp.dma_start(bv[:, :], bass.AP(attn_b.tensor, 2 * C, [[0, CH], [1, C]])).then_inc(consts, 16)
                sp.dma_start(causal[:, :], causal_d).then_inc(consts, 16)
                sp.dma_start(keep[:, :], keep_d).then_inc(consts, 16)

                def load(n, k):
                    if not inside(n, NC2):
                        return
                    at_least(sp, attended, n - XS + 1)
                    sp.dma_start(xc[:, k], chunks(x1, n)).then_inc(loaded[k], 16)

                def store(n, k):
                    if not inside(n, NC2):
                        return
                    sp.wait_ge(attended, n + 1)
                    sp.dma_start(chunks(t2, n), tn[:, k]).then_inc(stored[k], 16)

                def step(n, k):
                    load(n + 4, (k + 4) % XS)
                    store(n - 4, (k - 4) % XS)
                pipeline(sp, step, **run)
                for k in range(XS):
                    sp.wait_ge(stored[k], NC2 // XS * 16)

            @block.tensor
            def _(pe):
                pe.wait_ge(consts, 80)
                pe.wait_ge(prep, 1)
                nc.tensor.matmul(b_gram[:, 0:E], zero[:, 0:C], zero[:, C:C + E], start=True, stop=False, skip_group_check=True)

                def turn_tokens(n, k):
                    if not inside(n, NC2):
                        return
                    pe.wait_ge(normed, n + 1)
                    at_least(pe, u_out, n)
                    for a in range(2):
                        mm = nc.tensor.transpose(b_u[:, a * CH:(a + 1) * CH], u[:, k, a, :], ident[0:CH, 0:CH])
                    mm.then_inc(u_turned, 1)

                def queries_and_keys(n, k):
                    if not inside(n, NC2):
                        return
                    at_least(pe, qk_raised, n)
                    for j in range(2):
                        mm = nc.tensor.matmul(b_qk[:, j * 2 * CH:(j + 1) * 2 * CH], wt[:, j * C:(j + 1) * C], uT[:, k, :],
                                              start=True, stop=True)
                    mm.then_inc(qk_ready, 1)

                def values(n, k):
                    if not inside(n, NC2):
                        return
                    pe.wait_ge(u_out, n + 1)
                    at_least(pe, v_out, n)
                    for a in range(2):
                        mm = nc.tensor.matmul(b_v[0:CH, a * C:(a + 1) * C], uT[:, k, a * CH:(a + 1) * CH],
                                              wt[:, 2 * C:3 * C], start=True, stop=True)
                    mm.then_inc(v_ready, 1)

                def turn_keys(n, k):
                    if not inside(n, NC2):
                        return
                    pe.wait_ge(qk_out, n + 1)
                    at_least(pe, k_out, n)
                    for a in range(2):
                        mm = nc.tensor.transpose(b_kt[0:CH, a * C:(a + 1) * C], fqk[:, k, 1, a * CH:(a + 1) * CH], ident[:, :])
                    mm.then_inc(k_turned, 1)

                def scores(n, k):
                    if not inside(n, NC2):
                        return
                    pe.wait_ge(qk_out, n + 1)
                    at_least(pe, a_out, n)
                    for a in range(2):
                        c = slice(a * CH, (a + 1) * CH)
                        mm = nc.tensor.matmul(b_at[0:CH, c], fqk[:, k, 1, c], fqk[:, k, 0, c],
                                              start=True, stop=True)
                    mm.then_inc(a_ready, 1)

                def outer(n, k):
                    if not inside(n, NC2):
                        return
                    pe.wait_ge(k_out, n + 1)
                    pe.wait_ge(v_out, n + 1)
                    at_least(pe, advanced, n)
                    for a in range(2):
                        mm = nc.tensor.matmul(b_kv[:, a * E:(a + 1) * E], kt[:, k, a, :], ve[:, k, a, :], start=True, stop=True)
                    mm.then_inc(kv_ready, 1)

                def numerators(n, k):
                    if not inside(n, NC2):
                        return
                    pe.wait_ge(a_out, n + 1)
                    pe.wait_ge(advanced, n + 1)
                    at_least(pe, attended, n)
                    for a in range(2):
                        nc.tensor.matmul(b_num[0:CH, a * E:(a + 1) * E], aT[:, k, a, :], ve[:, k, a, :], start=True, stop=False)
                        mm = nc.tensor.matmul(b_num[0:CH, a * E:(a + 1) * E], fqk[:, k, 0, a * CH:(a + 1) * CH], state[:, k, a, :],
                                              start=False, stop=True)
                    mm.then_inc(num_ready, 1)

                def moments(n, k):
                    if not inside(n, NC2):
                        return
                    pe.wait_ge(normed2, n + 1)
                    for a in range(2):
                        mm = nc.tensor.matmul(b_gram[:, 0:E], u2[:, k, a, 0:C], u2[:, k, a, :], start=False,
                                              stop=isinstance(n, int) and n == NC2 - 1 and a == 1, skip_group_check=True)
                    mm.then_inc(counted, 1)

                def step(n, k):
                    queries_and_keys(n, k % S)
                    turn_keys(n - 1, (k - 1) % S)
                    turn_tokens(n + 1, (k + 1) % S)
                    numerators(n - 3, (k - 3) % S)
                    moments(n - 8, k % S)
                    outer(n - 2, (k - 2) % S)
                    values(n + 1, (k + 1) % S)
                    scores(n, k % S)
                pipeline(pe, step, **run)

            @block.scalar
            def _(act):
                act.wait_ge(consts, 80)

                def normalise(n, kx):
                    if not inside(n, NC2):
                        return
                    k = kx % S
                    act.wait_ge(shifted, n + 1)
                    act.wait_ge(loaded[kx], (n // XS + 1) * 16)
                    for a in range(2):
                        last = nc.scalar.activation(u[:, k, a, :], xc[:, kx, a, :], ACT.Identity, bias=ln[:, k, 1, 0, a:a + 1],
                                                    scale=ln[:, k, 0, 0, a:a + 1])
                    last.then_inc(normed, 1)

                def turned_out(n, k):
                    if not inside(n, NC2):
                        return
                    act.wait_ge(u_turned, n + 1)
                    nc.scalar.activation(uT[:, k, :], b_u[:, 0:2 * CH], ACT.Copy).then_inc(u_out, 1)

                def features(n, k):
                    if not inside(n, NC2):
                        return
                    act.wait_ge(qk_ready, n + 1)
                    at_least(act, qk_out, n - S + 1)
                    for j in range(2):
                        src = b_qk[:, j * 2 * CH:(j + 1) * 2 * CH]
                        nc.scalar.activation(raised[:, k, j, :], src, ACT.Exp, bias=bqk[:, j:j + 1])
                        last = nc.scalar.activation(positive[:, k, j, :], src, ACT.Relu, bias=bqk[:, j:j + 1])
                    last.then_inc(qk_raised, 1)

                def keys_out(n, k):
                    if not inside(n, NC2):
                        return
                    act.wait_ge(k_turned, n + 1)
                    nc.scalar.activation(kt[:, k].rearrange("p a b -> p (a b)"), b_kt[0:CH, 0:2 * C], ACT.Copy).then_inc(k_out, 1)

                def normalise2(n, kx):
                    if not inside(n, NC2):
                        return
                    k, row = kx % S, (kx + AHEAD) % S
                    act.wait_ge(shifted, n + AHEAD + 1)
                    at_least(act, counted, n - S + 1)
                    for a in range(2):
                        last = nc.scalar.activation(u2[:, k, a, 0:C], tn[:, kx, a, :], ACT.Identity, bias=ln[:, row, 1, 1, a:a + 1],
                                                    scale=ln[:, row, 0, 1, a:a + 1])
                    last.then_inc(normed2, 1)

                def step(n, k):
                    normalise(n + 1, (k + 1) % XS)
                    features(n, k % S)
                    turned_out(n + 1, (k + 1) % S)
                    normalise2(n - 5, (k - 5) % XS)
                    keys_out(n - 1, (k - 1) % S)
                pipeline(act, step, **run)

            @block.gpsimd
            def _(pool):
                pool.wait_ge(prep, 1)

                def statistics(n, k):
                    if not inside(n, ROWS):
                        return
                    pool.wait_ge(aggregated, n + 1)
                    at_least(pool, shifted, n)
                    apart(pool, passed)
                    moments = mv[:, k].rearrange("p l a m -> p (l a) m")
                    nc.gpsimd.tensor_scalar(spread[:, :], moments[:, :, 1], LN_EPS, None, ALU.add).then_inc(spread_out, 1)
                    nc.gpsimd.tensor_scalar(minus[:, :], moments[:, :, 0], -1.0, None, ALU.mult).then_inc(minus_out, 1)
                    at_least(pool, normed, min(NC2, n - S + 1) if isinstance(n, int) else n - S + 1)
                    at_least(pool, normed2, n - AHEAD - S + 1)
                    pool.wait_ge(spread_out, n + 1)
                    apart(pool, passed)
                    rstd = ln[:, k, 0].rearrange("p l a -> p (l a)")
                    nc.gpsimd.tensor_tensor(rstd, spread[:, :], exponent[0:CH, 0:4], ALU.pow).then_inc(rooted, 1)
                    pool.wait_ge(minus_out, n + 1)
                    pool.wait_ge(rooted, n + 1)
                    apart(pool, passed)
                    nc.gpsimd.tensor_tensor(ln[:, k, 1].rearrange("p l a -> p (l a)"), minus[:, :], rstd, ALU.mult).then_inc(shifted, 1)

                def remember(n, k):
                    if not inside(n, NC2):
                        return
                    pool.wait_ge(shifted, n + AHEAD + 1)
                    apart(pool, passed)
                    nc.gpsimd.tensor_copy(ln2_table[:, :, bass.ds(n * 2, 2)], ln[:, k, :, 1, :]).then_inc(tabled, 1)

                def step(n, k):
                    remember(n - AHEAD, k % S)
                    statistics(n + 3, (k + 3) % S)
                pipeline(pool, step, **run)

            @block.vector
            def _(dve):
                nc.vector.memset(zero[:, :], 0.0)
                nc.vector.memset(carried[:, :], 0.0)
                nc.vector.memset(mv[:, :, :, :, :], 1.0)
                nc.vector.memset(ve[:, :, :, C:E], 1.0)
                nc.vector.memset(u2[:, :, :, C:E], 1.0).then_inc(prep, 1)
                dve.wait_ge(prep, 1)
                dve.wait_ge(consts, 80)

                def combine(n, k):
                    if inside(n, NC2):
                        dve.wait_ge(qk_raised, n + 1)
                        nc.vector.scalar_tensor_tensor(fqk[:, k], raised[:, k], 1.0, positive[:, k], ALU.min, ALU.add).then_inc(qk_out, 1)

                def inner_out(n, k):
                    if inside(n, NC2):
                        dve.wait_ge(a_ready, n + 1)
                        nc.vector.tensor_tensor(aT[:, k], b_at[0:CH, 0:2 * CH].rearrange("p (a b) -> p a b", a=2),
                                                causal[:, :].unsqueeze(1).broadcast_to([CH, 2, CH]), ALU.mult).then_inc(a_out, 1)

                def advance(n, k):
                    if inside(n, NC2):
                        dve.wait_ge(kv_ready, n + 1)
                        on = keep[:, bass.ds(n, 1)]
                        nc.vector.tensor_scalar(state[:, k, 0, :], carried[:, :], on, None, ALU.mult)
                        nc.vector.scalar_tensor_tensor(state[:, k, 1, :], carried[:, :], on, b_kv[:, 0:E],
                                                       ALU.mult, ALU.add).then_inc(moved, 1)

                def denominators(n, k):
                    if inside(n, NC2):
                        dve.wait_ge(num_ready, n + 1)
                        nc.vector.tensor_scalar(den[:, :, :], b_num[0:CH, 0:2 * E].rearrange("p (a b) -> p a b", a=2)[:, :, C:E],
                                                DEN_EPS, None, ALU.add).then_inc(den_ready, 1)

                def before_measuring(n, k):
                    if inside(n, NC2):
                        dve.wait_ge(loaded[k], (n // XS + 1) * 16)
                    if inside(n - AHEAD, NC2):
                        dve.wait_ge(attended, n - AHEAD + 1)

                def measure(n, k):
                    if inside(n, ROWS):
                        for which, tile, k2, m in ((0, xc, k, n), (1, tn, (k - AHEAD) % XS, n - AHEAD)):
                            if inside(m, NC2):
                                for a in range(2):
                                    last = nc.vector.bn_stats(stats[:, k % S, which, a, :], tile[:, k2, a, :])
                        last.then_inc(measured, 1)

                def aggregate(n, k):
                    if inside(n, ROWS):
                        for which, m in ((0, n), (1, n - AHEAD)):
                            if inside(m, NC2):
                                for a in range(2):
                                    last = nc.vector.bn_aggr(mv[:, k % S, which, a, :], stats[:, k % S, which, a, :])
                        last.then_inc(aggregated, 1)

                def carry(n, k):
                    if inside(n, NC2):
                        dve.wait_ge(moved, n + 1)
                        nc.vector.tensor_tensor(carried[:, :], b_kv[:, E:2 * E], state[:, k, 1, :], ALU.add).then_inc(advanced, 1)

                def values_out(n, k):
                    if inside(n, NC2):
                        dve.wait_ge(v_ready, n + 1)
                        nc.vector.tensor_tensor(ve[:, k, :, 0:C], b_v[0:CH, 0:2 * C].rearrange("p (a b) -> p a b", a=2),
                                                bv[:, :].unsqueeze(1).broadcast_to([CH, 2, C]), ALU.add).then_inc(v_out, 1)

                def invert(n):
                    if inside(n, NC2):
                        dve.wait_ge(den_ready, n + 1)
                        nc.vector.reciprocal(rden[:, :, :], den[:, :, :]).then_inc(den_inv, 1)

                def attend(n, k):
                    if inside(n, NC2):
                        dve.wait_ge(den_inv, n + 1)
                        at_least(dve, stored[k], n // XS * 16)
                        for a in range(2):
                            last = nc.vector.scalar_tensor_tensor(tn[:, k, a, :], b_num[0:CH, a * E:a * E + C], rden[:, a, :],
                                                                  xc[:, k, a, :], ALU.mult, ALU.add)
                        last.then_inc(attended, 1)

                def step(n, k):
                    measure(n + 3, (k + 3) % XS)
                    denominators(n - 3, (k - 3) % XS)
                    combine(n, k % S)
                    if inside(n + 3, ROWS):
                        dve.wait_ge(measured, n + 4)
                    invert(n - 3)
                    aggregate(n + 3, (k + 3) % XS)
                    advance(n - 2, (k - 2) % S)
                    attend(n - 3, (k - 3) % XS)
                    carry(n - 2, (k - 2) % S)
                    inner_out(n, k % S)
                    before_measuring(n + 4, (k + 4) % XS)
                    values_out(n + 1, (k + 1) % S)
                pipeline(dve, step, **run)
                dve.wait_ge(counted, NC2)
                nc.vector.tensor_copy(gram[:, :], b_gram[:, 0:E]).then_inc(gram_done, 1)


def recurrence(nc, t2, out, ffn_w, ffn_wt, ffn_vt, gamma, beta, ident, ones, exponent, ln2_table, gram, bank, agree):
    ctx = ExitStack()
    with ctx:
        def sb(name, shape, dtype=F32):
            return ctx.enter_context(nc.sbuf_tensor("sc_" + name, shape, dtype))

        def sem(name):
            return ctx.enter_context(nc.semaphore(name))

        E = C + 1
        I32 = mybir.dt.int32
        w = sb("w", [128, C])
        wT = sb("wT", [128, C])
        vT = sb("vT", [128, C])
        gb = sb("gb", [128, 2])
        scaled = sb("scaled", [128, C])
        fT = sb("fT", [128, C])
        prod = sb("prod", [128, C])
        cols = sb("cols", [128, 8])
        bn_rstd = sb("bn_rstd", [128, 1])
        rstd = sb("scan_rstd", [CH, NG, CH])
        shift = sb("scan_shift", [CH, NG, CH])
        start = sb("start", [128, COLS])
        final = sb("final", [128, COLS])
        gap = sb("gap", [128, B, NCH - 1])
        worst = sb("worst", [128, 1])
        worst_row = sb("worst_row", [1, 128])
        flag_f = sb("flag_f", [1, 1])
        flag = sb("flag", [1, 1], I32)
        consts, chain, pchain = sem("sc_consts"), sem("sc_chain"), sem("sc_pchain")
        rooted = sem("sc_rooted")

        with nc.Block() as block:
            @block.sync
            def _(sp):
                sp.dma_start(w[:, :], ffn_w).then_inc(consts, 16)
                sp.dma_start(wT[:, :], ffn_wt).then_inc(consts, 16)
                sp.dma_start(vT[:, :], ffn_vt).then_inc(consts, 16)
                sp.dma_start(gb[:, 0:1], gamma.rearrange("(p a) -> p a", a=1)).then_inc(consts, 16)
                sp.dma_start(gb[:, 1:2], beta.rearrange("(p a) -> p a", a=1)).then_inc(consts, 16)

            @block.tensor
            def _(pe):
                pe.wait_ge(consts, 80)
                nc.tensor.matmul(bank[0][:, 0:C], gram[:, 0:C], wT[:, :], start=True, stop=True).then_inc(pchain, 1)
                nc.tensor.matmul(bank[1][:, 0:1], wT[:, :], gram[:, C:E], start=True, stop=True).then_inc(pchain, 1)
                pe.wait_ge(chain, 1)
                nc.tensor.matmul(bank[2][:, 0:1], prod[:, :], ones[:, 0:1], start=True, stop=True).then_inc(pchain, 1)
                for i, table in enumerate((ln2_table[:, 0], ln2_table[:, 1])):
                    for g in range(NG):
                        last = nc.tensor.transpose(bank[4 + i][0:CH, g * CH:(g + 1) * CH], table[:, g * CH:(g + 1) * CH],
                                                   ident[0:CH, 0:CH])
                last.then_inc(pchain, 1)
                pe.wait_ge(chain, 8)
                nc.tensor.transpose(bank[3][:, 0:C], scaled[:, :], ident[:, :]).then_inc(pchain, 1)

            @block.vector
            def _(dve):
                done = [0]

                def link(ins):
                    done[0] += 1
                    ins.then_inc(chain, 1)
                    dve.wait_ge(chain, done[0])

                mean, square, square_mean, var, root, scale = (cols[:, i:i + 1] for i in range(6))
                shift_bn = cols[:, 6:7]
                dve.wait_ge(consts, 80)
                dve.wait_ge(pchain, 1)
                link(nc.vector.tensor_tensor(prod[:, :], bank[0][:, 0:C], wT[:, :], ALU.mult))
                dve.wait_ge(pchain, 3)
                link(nc.vector.tensor_scalar(mean, bank[1][:, 0:1], 1.0 / (B * T), None, ALU.mult))
                link(nc.vector.tensor_scalar(square, bank[2][:, 0:1], 1.0 / (B * T), None, ALU.mult))
                link(nc.vector.tensor_tensor(square_mean, mean, mean, ALU.mult))
                link(nc.vector.tensor_tensor(var, square, square_mean, ALU.subtract))
                link(nc.vector.tensor_scalar(root, var, 0.0, BN_EPS, ALU.max, ALU.add))
                dve.wait_ge(rooted, 1)
                link(nc.vector.tensor_tensor(scale, bn_rstd[:, :], gb[:, 0:1], ALU.mult))
                link(nc.vector.tensor_scalar(scaled[:, :], w[:, :], scale, None, ALU.mult))
                link(nc.vector.tensor_tensor(cols[:, 7:8], mean, scale, ALU.mult))
                link(nc.vector.tensor_tensor(shift_bn, gb[:, 1:2], cols[:, 7:8], ALU.subtract))
                dve.wait_ge(pchain, 4)
                nc.vector.tensor_copy(rstd[:, :, :].rearrange("p a b -> p (a b)"), bank[4][0:CH, 0:NG * CH])
                nc.vector.tensor_copy(shift[:, :, :].rearrange("p a b -> p (a b)"), bank[5][0:CH, 0:NG * CH])
                dve.wait_ge(pchain, 5)
                nc.vector.tensor_copy(fT[:, :], bank[3][:, 0:C])
                nc.vector.memset(start[:, :], 0.5)

            @block.gpsimd
            def _(pool):
                pool.wait_ge(chain, 6)
                nc.gpsimd.tensor_tensor(bn_rstd[:, :], cols[:, 4:5], exponent[:, 0:1], ALU.pow).then_inc(rooted, 1)

        shift_bn = cols[:, 6:7]
        scan(nc, t2, None, CH - WARM, fT, vT, shift_bn, rstd, shift, start, final, ident, bank, "warm")
        hand_over(nc, start, final)
        scan(nc, t2, out, 0, fT, vT, shift_bn, rstd, shift, start, final, ident, bank, "main")

        compared, worst_turned = sem("sc_compared"), sem("sc_worst_turned")
        with nc.Block() as block:
            @block.vector
            def _(dve):
                done = [0]

                def link(ins):
                    done[0] += 1
                    ins.then_inc(compared, 1)
                    dve.wait_ge(compared, done[0])

                ends = final[:, :].rearrange("p (b c) -> p b c", b=B)[:, :, 0:NCH - 1]
                begins = start[:, :].rearrange("p (b c) -> p b c", b=B)[:, :, 1:NCH]
                link(nc.vector.tensor_tensor(gap[:, :, :], ends, begins, ALU.subtract))
                link(nc.vector.tensor_tensor(gap[:, :, :], gap[:, :, :], gap[:, :, :], ALU.mult))
                link(nc.vector.tensor_scalar(gap[:, :, :], gap[:, :, :], agree * abs(agree), None, ALU.is_le))
                link(nc.vector.tensor_reduce(worst[:, :], gap[:, :, :].rearrange("p a b -> p (a b)"), AX.X, ALU.min))
                dve.wait_ge(worst_turned, 1)
                link(nc.vector.tensor_reduce(worst_row[:, 0:1], bank[0][0:1, 0:128], AX.X, ALU.min))
                link(nc.vector.tensor_scalar(flag_f[:, :], worst_row[:, 0:1], -1.0, 1.0, ALU.mult, ALU.add))
                link(nc.vector.tensor_copy(flag[:, :], flag_f[:, :]))

            @block.tensor
            def _(pe):
                pe.wait_ge(compared, 4)
                nc.tensor.transpose(bank[0][0:1, 0:128], worst[:, :], ident[:, :]).then_inc(worst_turned, 1)

        again = nc.values_load(flag[0:1, 0:1], min_val=0, max_val=1)
        with nc.If(again > 0):
            with nc.Fori(0, NCH - 1):
                hand_over(nc, start, final)
                scan(nc, t2, out, 0, fT, vT, shift_bn, rstd, shift, start, final, ident, bank, "again", repeated=True)


def hand_over(nc, start, final):
    with nc.Block() as block:
        @block.vector
        def _(dve):
            begins = start[:, :].rearrange("p (b c) -> p b c", b=B)
            ends = final[:, :].rearrange("p (b c) -> p b c", b=B)
            nc.vector.tensor_copy(begins[:, :, 1:NCH], ends[:, :, 0:NCH - 1])
            nc.vector.memset(begins[:, :, 0:1], 0.0)


def scan(nc, t2, out, s0, fT, vT, shift_bn, rstd, shift, start, final, ident, bank, name, repeated=False):
    ctx = ExitStack()
    with ctx:
        def sb(label, shape):
            return ctx.enter_context(nc.sbuf_tensor(f"{name}_{label}", shape, F32))

        used = []

        def sem(label):
            used.append(ctx.enter_context(nc.semaphore(f"{name}_{label}")))
            return used[-1]

        NB = (CH - s0) // SB
        NT = NB * SB
        tb = sb("tb", [CH, 4, NG, SB, C])
        ub = sb("ub", [CH, 2, NG, SB, C])
        ob = sb("ob", [CH, 2, NG, SB, C])
        uT = sb("uT", [128, 2, COLS])
        y = sb("y", [128, 2, COLS])
        b_state, b_u, b_y = bank[0:2], bank[2:4], bank[4:6]
        loaded = [sem(f"loaded{i}") for i in range(2)]
        stored = [sem(f"stored{i}") for i in range(2)]
        u_scaled, u_made, u_turned, u_out = sem("u_scaled"), sem("u_made"), sem("u_turned"), sem("u_out")
        w_done, v_done, y_made, y_turned, summed = sem("w_done"), sem("v_done"), sem("y_made"), sem("y_turned"), sem("summed")
        final_out, passed = sem("final_out"), sem("passed")

        def steps(dram, j):
            return dram.rearrange("b t d -> (b t d)").rearrange("(g p s d) -> p g s d", g=NG, p=CH, s=CH)[:, :, bass.ds(j * SB + s0, SB), :]

        def slot4(tile, j):
            return tile[:, bass.ds(j % 4, 1)].rearrange("p o g s c -> p (o g) s c")

        short = NB < 8
        run = dict(first=-3, last=NB + 2, lo=2 if not short else NB + 2, hi=NB - 4 if not short else NB + 2)

        with nc.Block() as block:
            @block.sync
            def _(sp):
                def step(j, k):
                    if inside(j + 3, NB):
                        kl = 1 - k
                        if out is not None:
                            at_least(sp, summed, j * SB)
                        at_least(sp, u_made, j)
                        at_least(sp, loaded[kl], (j + 3) // 2 * 16)
                        sp.dma_start(slot4(tb, j + 3), steps(t2, j + 3)).then_inc(loaded[kl], 16)
                    if out is not None and inside(j - 1, NB):
                        sp.wait_ge(summed, j * SB)
                        sp.dma_start(steps(out, j - 1), ob[:, 1 - k]).then_inc(stored[1 - k], 16)
                pipeline(sp, step, **run)
                if out is not None:
                    for k in range(2):
                        sp.wait_ge(stored[k], NB // 2 * 16)

            @block.gpsimd
            def _(pool):
                def step(j, k):
                    j, k = j + 1, 1 - k
                    if not inside(j, NB):
                        return
                    pool.wait_ge(loaded[k], (j // 2 + 1) * 16)
                    at_least(pool, u_turned, (j - 1) * SB)
                    apart(pool, passed)
                    src = slot4(tb, j)
                    now = bass.ds(j * SB + s0, SB)
                    nc.gpsimd.tensor_tensor(ub[:, k], src, rstd[:, :, now].unsqueeze(3).broadcast_to([CH, NG, SB, C]),
                                            ALU.mult).then_inc(u_scaled, 1)
                    pool.wait_ge(u_scaled, j + 1)
                    apart(pool, passed)
                    nc.gpsimd.tensor_tensor(ub[:, k], ub[:, k], shift[:, :, now].unsqueeze(3).broadcast_to([CH, NG, SB, C]),
                                            ALU.add).then_inc(u_made, 1)
                pipeline(pool, step, **run)

            @block.tensor
            def _(pe):
                def turn_tokens(t, j, k, i):
                    if not inside(t, NT):
                        return
                    pe.wait_ge(u_made, j + 1)
                    at_least(pe, u_out, t - 1)
                    for g in range(NG):
                        mm = nc.tensor.transpose(b_u[i % 2][:, g * CH:(g + 1) * CH], ub[:, k, g, i, :], ident[0:CH, 0:CH])
                    mm.then_inc(u_turned, 1)

                def input_part(t, i):
                    if not inside(t, NT):
                        return
                    pe.wait_ge(u_out, t + 1)
                    at_least(pe, y_made, t - 1)
                    nc.tensor.matmul(b_state[i % 2][:, 0:COLS], fT[:, :], uT[:, i % 2, :], start=True, stop=False).then_inc(w_done, 1)

                def state_part(t, i):
                    if not inside(t, NT):
                        return
                    at_least(pe, y_made, t)
                    before = start[:, :] if isinstance(t, int) and t == 0 else y[:, 1 - i % 2, :]
                    nc.tensor.matmul(b_state[i % 2][:, 0:COLS], vT[:, :], before, start=False, stop=True).then_inc(v_done, 1)

                def turn_states(t, i):
                    if out is None or not inside(t, NT):
                        return
                    pe.wait_ge(y_made, t + 1)
                    at_least(pe, summed, t - 1)
                    for g in range(NG):
                        mm = nc.tensor.transpose(b_y[i % 2][0:CH, g * C:(g + 1) * C], y[:, i % 2, g * CH:(g + 1) * CH], ident[:, :])
                    mm.then_inc(y_turned, 1)

                def step(j, k):
                    for i in range(SB):
                        t = j * SB + i
                        ahead = (j, k, i + 2) if i + 2 < SB else (j + 1, 1 - k, i + 2 - SB)
                        turn_tokens(t + 2, *ahead)
                        state_part(t, i)
                        turn_states(t - 1, i + 1)
                        input_part(t + 1, i + 1)
                pipeline(pe, step, **run)

            @block.vector
            def _(dve):
                def turned_out(t, i):
                    if not inside(t, NT):
                        return
                    dve.wait_ge(u_turned, t + 1)
                    at_least(dve, w_done, t - 1)
                    nc.vector.tensor_copy(uT[:, i % 2, :], b_u[i % 2][:, 0:COLS]).then_inc(u_out, 1)

                def residual(t, j, k, i):
                    if out is None or not inside(t, NT):
                        return
                    dve.wait_ge(y_turned, t + 1)
                    dve.wait_ge(loaded[k], (j // 2 + 1) * 16)
                    at_least(dve, stored[k], j // 2 * 16)
                    nc.vector.tensor_tensor(ob[:, k, :, i, :], b_y[i % 2][0:CH, :].rearrange("p (g c) -> p g c", g=NG),
                                            slot4(tb, j)[:, :, i, :], ALU.add).then_inc(summed, 1)

                def step(j, k):
                    for i in range(SB):
                        t = j * SB + i
                        turned_out(t + 2, i + 2)
                        now = (j, k, i - 1) if i else (j - 1, 1 - k, SB - 1)
                        residual(t - 1, *now)
                pipeline(dve, step, **run)
                dve.wait_ge(y_made, NT)
                nc.vector.tensor_copy(final[:, :], y[:, 1, :]).then_inc(final_out, 1)

            @block.scalar
            def _(act):
                def step(j, k):
                    for i in range(SB):
                        t = j * SB + i
                        if not inside(t, NT):
                            continue
                        act.wait_ge(v_done, t + 1)
                        if out is not None:
                            at_least(act, y_turned, t - 1)
                        nc.scalar.activation(y[:, i % 2, :], b_state[i % 2][:, 0:COLS], ACT.Sigmoid,
                                             bias=shift_bn).then_inc(y_made, 1)
                pipeline(act, step, **run)

        if repeated:
            with nc.Block() as block:
                @block.gpsimd
                def _(pool):
                    for semaphore in used:
                        pool.sem_clear(semaphore)


_DATA = ["x", "L0_conv_w_qkv", "L0_conv_pos_emb", "L0_conv_w_out", "L0_conv_b_out", "attn_wt", "L1_attn_b",
         "L1_ffn_W", "ffn_wt", "ffn_vt", "L1_ffn_gamma", "L1_ffn_beta"]
_CONSTS = ["ident", "shift_mask", "causal", "group", "keep"]


def constants():
    import numpy as np
    f = np.float32
    lane = np.arange(128)
    r, c = np.arange(WIN) // WS, np.arange(WIN) % WS
    far = f(-1e30)
    upper = np.where((r[:, None] >= WS - DISP) != (r[None] >= WS - DISP), far, f(0))
    left = np.where((c[:, None] >= WS - DISP) != (c[None] >= WS - DISP), far, f(0))
    shift_mask = np.zeros((128, NWR, NWC, WIN), f)
    for start in (0, WPAD):
        shift_mask[start:start + WIN, NWR - 1] += upper[:, None]
        shift_mask[start:start + WIN, :, NWC - 1] += left[:, None]
    pairs = np.zeros((128, NWR, NWC // 2, WIN), f)
    pairs[0:WPAD] = shift_mask[0:WPAD, :, 0::2]
    pairs[WPAD:] = shift_mask[WPAD:, :, 1::2]
    causal = (np.arange(CH)[:, None] <= np.arange(CH)[None]).astype(f)
    group = (lane[:, None] // GROUP == lane[None] // GROUP).astype(f)
    keep = np.ones((128, NC2), f)
    keep[:, ::NCH // 2] = 0
    return dict(ident=np.eye(128, dtype=f), 
                shift_mask=np.ascontiguousarray(pairs.reshape(128, -1)), causal=causal, group=group, keep=keep)


def kernel(**inputs):
    import numpy as np
    import concourse.bacc as bacc
    from concourse.bass_utils import run_bass_kernel_spmd

    data = {k: np.ascontiguousarray(v) for k, v in inputs.items()}
    data["x"] = data["x"].reshape(B, T, C)
    data["attn_wt"] = np.ascontiguousarray(data["L1_attn_W"].T)
    data["ffn_wt"] = np.ascontiguousarray(data["L1_ffn_W"].T)
    data["ffn_vt"] = np.ascontiguousarray(data["L1_ffn_V"].T)
    data.update(constants())
    nc = bacc.Bacc("TRN2", target_bir_lowering=False, num_devices=1)
    arrays, args = {}, []
    for name in _DATA + _CONSTS:
        arrays[f"in_{name}"] = data[name]
        args.append(nc.dram_tensor(f"in_{name}", data[name].shape, F32, kind="ExternalInput").ap())
    out = nc.dram_tensor("out", (B, T, C), F32, kind="ExternalOutput").ap()
    build(nc, *args, out)
    result = run_bass_kernel_spmd(nc, [arrays], core_ids=[0])
    return result.results[0]["out"].reshape(B, H, W, C)
```

```python
import itertools
from contextlib import ExitStack

import concourse.bass as bass
from concourse import mybir

F32 = mybir.dt.float32
ALU = mybir.AluOpType
ACT = mybir.ActivationFunctionType
AX = mybir.AxisListType

B, H, W, C = 16, 56, 56, 128
T = H * W
WS, DISP = 7, 3
HEADS, HD = 4, 32
WIN = WS * WS
NWR = H // WS
NWC = W // WS
ROWTOK = WS * W
NU = B * NWR
WPAD = 64
GROUP = 4
GN_EPS, LN_EPS, BN_EPS, DEN_EPS = 1e-5, 1e-5, 1e-5, 1e-6
CH = 112
NCH = T // CH
NC2 = B * NCH // 2
GI = 4
NG = B // GI
COLS = B * NCH
SB = 4
NSB = CH // SB
WARM = 12
AGREE = 5e-7


def at_least(eng, sem, value):
    if not isinstance(value, int) or value > 0:
        eng.wait_ge(sem, value)


def pipeline(eng, step, first, last, lo, hi, unroll=2):
    for n in range(first, lo):
        step(n, n % unroll)
    if lo < hi:
        with eng.Fori(lo // unroll, hi // unroll) as m:
            for k in range(unroll):
                step(m * unroll + k, k)
    for n in range(hi, last):
        step(n, n % unroll)


def apart(eng, passed):
    eng.sem_inc(passed, 1)


def inside(n, count):
    return not isinstance(n, int) or 0 <= n < count


def build(nc, x, w_qkv, pos_emb, w_out, b_out, attn_wt, attn_b, ffn_w, ffn_wt, ffn_vt, gamma, beta,
          ident_d, shift_mask_d, causal_d, group_d, keep_d, out, agree=AGREE):
    x1 = nc.dram_tensor("x1", (B, T, C), F32, kind="Internal").ap()
    t2 = nc.dram_tensor("t2", (B, T, C), F32, kind="Internal").ap()
    top = ExitStack()

    def sb(name, shape, stack=top):
        return stack.enter_context(nc.sbuf_tensor("k_" + name, shape, F32))

    bank = [top.enter_context(nc.psum_tensor(f"k_bank{i}", [128, 512], F32)) for i in range(8)]
    ident = sb("ident", [128, 128])
    ones = sb("ones", [128, 128])
    position = sb("position", [128, WIN])
    exponent = sb("exponent", [128, B])
    gn_rstd = sb("gn_rstd", [128, B])
    gn_shift = sb("gn_shift", [128, B])
    ln2_table = sb("ln2_table", [CH, 2, COLS])
    gram = sb("gram", [128, C + 1])
    gn_statistics(nc, x, pos_emb, position, ident_d, group_d, ident, ones, exponent, gn_rstd, gn_shift, bank)
    window_attention(nc, x, x1, w_qkv, w_out, b_out, shift_mask_d, position, ident, gn_rstd, gn_shift, bank)
    linear_attention(nc, x1, t2, attn_wt, attn_b, causal_d, keep_d, ident, exponent, ln2_table, gram, bank)
    recurrence(nc, t2, out, ffn_w, ffn_wt, ffn_vt, gamma, beta, ident, ones, exponent, ln2_table, gram,
               bank, agree)
    top.close()


def gn_statistics(nc, x, pos_emb, position, ident_d, group_d, ident, ones, exponent, gn_rstd, gn_shift, bank):
    P, TT = CH, T // CH
    ctx = ExitStack()
    with ctx:
        def sb(name, shape):
            return ctx.enter_context(nc.sbuf_tensor("gn_" + name, shape, F32))

        def sem(name):
            return ctx.enter_context(nc.semaphore(name))

        xi = sb("xi", [P, 2, TT * C])
        sq = sb("sq", [P, 2, TT * C])
        part = sb("part", [P, 2, 2, C])
        group = sb("group", [128, 128])
        sums = sb("sums", [128, 2 * B])
        moments = sb("moments", [128, 2, B])
        work = sb("work", [128, 3, B])
        consts = sem("gn_consts")
        loaded = [sem(f"gn_loaded{i}") for i in range(2)]
        placed = sem("gn_placed")
        ones_set, exponent_set = sem("gn_ones"), sem("gn_exponent")
        squared = sem("gn_squared")
        reduced = sem("gn_reduced")
        summed = sem("gn_summed")
        sums_out = sem("gn_sums_out")
        grouped = sem("gn_grouped")
        chain, rooted = sem("gn_chain"), sem("gn_rooted")

        with nc.Block() as block:
            @block.sync
            def _(sp):
                sp.dma_start(ident[:, :], ident_d).then_inc(consts, 16)
                sp.dma_start(group[:, :], group_d).then_inc(consts, 16)
                rows = iter(range(WIN))
                for n in range(B):
                    at_least(sp, squared, n - 1)
                    at_least(sp, reduced, n - 1)
                    sp.dma_start(xi[:, n % 2, :], x[n].rearrange("t c -> (t c)")
                                 .rearrange("(p f) -> p f", p=P)).then_inc(loaded[n % 2], 16)
                    if n == 0:
                        sp.wait_ge(ones_set, 1)
                    for q in itertools.islice(rows, 4):
                        r, c = q // WS, q % WS
                        src = pos_emb[WS - 1 - r:2 * WS - 1 - r, WS - 1 - c:2 * WS - 1 - c]
                        sp.dma_start(position[q:q + 1, :].rearrange("p (a b) -> p a b", a=WS),
                                     src.unsqueeze(0)).then_inc(placed, 16)
                sp.wait_ge(placed, 16 * WIN)
                sp.dma_start(position[WPAD:WPAD + WIN, :], position[0:WIN, :]).then_inc(placed, 16)
                sp.wait_ge(placed, 16 * (WIN + 1))

            @block.scalar
            def _(act):
                def step(n, k):
                    act.wait_ge(loaded[k], (n // 2 + 1) * 16)
                    at_least(act, reduced, n - 1)
                    nc.scalar.activation(sq[:, k, :], xi[:, k, :], ACT.Square).then_inc(squared, 1)
                pipeline(act, step, 0, B, 2, B)

            @block.vector
            def _(dve):
                nc.vector.memset(position[:, :], 0.0)
                nc.vector.memset(ones[:, :], 1.0).then_inc(ones_set, 1)

                def step(n, k):
                    dve.wait_ge(loaded[k], (n // 2 + 1) * 16)
                    at_least(dve, summed, n - 1)
                    nc.vector.tensor_reduce(part[:, k, 0, :], xi[:, k, :].rearrange("p (t c) -> p c t", c=C),
                                            AX.X, ALU.add)
                    dve.wait_ge(squared, n + 1)
                    nc.vector.tensor_reduce(part[:, k, 1, :], sq[:, k, :].rearrange("p (t c) -> p c t", c=C),
                                            AX.X, ALU.add).then_inc(reduced, 1)
                pipeline(dve, step, 0, B, 2, B)
                dve.wait_ge(summed, B)
                nc.vector.tensor_copy(sums[:, :], bank[0][:, 0:2 * B]).then_inc(sums_out, 1)
                dve.wait_ge(grouped, 1)
                done = [0]

                def link(ins):
                    done[0] += 1
                    ins.then_inc(chain, 1)
                    dve.wait_ge(chain, done[0])
                link(nc.vector.tensor_scalar(moments[:, :, :].rearrange("p a b -> p (a b)"), bank[1][:, 0:2 * B],
                                             1.0 / (T * GROUP), None, ALU.mult))
                mean, square = moments[:, 0, :], moments[:, 1, :]
                link(nc.vector.tensor_tensor(work[:, 0, :], mean, mean, ALU.mult))
                link(nc.vector.tensor_tensor(work[:, 1, :], square, work[:, 0, :], ALU.subtract))
                link(nc.vector.tensor_scalar(work[:, 2, :], work[:, 1, :], 0.0, GN_EPS, ALU.max, ALU.add))
                dve.wait_ge(rooted, 1)
                link(nc.vector.scalar_tensor_tensor(gn_shift[:, :], mean, -1.0, gn_rstd[:, :], ALU.mult, ALU.mult))

            @block.gpsimd
            def _(pool):
                nc.gpsimd.memset(exponent[:, :], -0.5).then_inc(exponent_set, 1)
                pool.wait_ge(exponent_set, 1)
                pool.wait_ge(chain, 4)
                nc.gpsimd.tensor_tensor(gn_rstd[:, :], work[:, 2, :], exponent[:, :], ALU.pow).then_inc(rooted, 1)

            @block.tensor
            def _(pe):
                pe.wait_ge(ones_set, 1)
                def step(n, k):
                    pe.wait_ge(reduced, n + 1)
                    for j in range(2):
                        mm = nc.tensor.matmul(bank[0][:, bass.ds(n + j * B, 1)], part[:, k, j, :],
                                              ones[0:P, 0:1], start=True, stop=True)
                    mm.then_inc(summed, 1)
                pipeline(pe, step, 0, B, 2, B)
                pe.wait_ge(consts, 32)
                pe.wait_ge(sums_out, 1)
                nc.tensor.matmul(bank[1][:, 0:2 * B], group[:, :], sums[:, :], start=True, stop=True).then_inc(grouped, 1)


def window_attention(nc, x, x1, w_qkv, w_out, b_out, shift_mask_d, position, ident, gn_rstd, gn_shift, bank):
    ctx = ExitStack()
    with ctx:
        def sb(name, shape):
            return ctx.enter_context(nc.sbuf_tensor("wa_" + name, shape, F32))

        def sem(name):
            return ctx.enter_context(nc.semaphore(name))

        S = 4
        HW_ = NWC // 2
        wqkv = sb("wqkv", [128, 3 * C])
        wout = sb("wout", [128, C])
        bout = sb("bout", [CH, C])
        shift_mask = sb("shift_mask", [128, NWR, 2, 2, WIN])
        bias = sb("bias", [128, NWR, 2, 2, WIN])
        xw = sb("xw", [CH, S, 4, C])
        xb = sb("xb", [CH, S, 4, C])
        xT = sb("xT", [128, S, NWC, WPAD])
        qT = [sb(f"qT{i}", [128, ROWTOK + WPAD - WIN]) for i in range(S)]
        kb = sb("kb", [128, S, HEADS, ROWTOK])
        prob = sb("prob", [128, S, 2, 2, HEADS, WPAD])
        peak = sb("peak", [128, S, 2, 2 * HEADS])
        total = sb("total", [128, S, 2, 2 * HEADS])
        inv = sb("inv", [128, S, 2, 2 * HEADS])
        vb = sb("vb", [128, S, NWC // 2, 2, 2, 2, HD])
        pT = sb("pT", [128, S, 2, 2, 2, 128])
        oT = sb("oT", [128, S, WS, W])
        y = sb("y", [CH, S, 4, C])
        b_tx, b_q, b_k, b_v, b_s, b_pt, b_ot, b_y = bank

        consts = sem("wa_consts")
        prep = sem("wa_prep")
        loaded = [sem(f"wa_loaded{i}") for i in range(S)]
        stored = [sem(f"wa_stored{i}") for i in range(S)]
        x_turned, x_normed = sem("wa_x_turned"), sem("wa_x_normed")
        q_ready, k_ready = sem("wa_q_ready"), sem("wa_k_ready")
        q_out, k_out = sem("wa_q_out"), sem("wa_k_out")
        v_ready, v_half_out, v_out = sem("wa_v_ready"), sem("wa_v_half_out"), sem("wa_v_out")
        scored, biased, peaked = sem("wa_scored"), sem("wa_biased"), sem("wa_peaked")
        lowered, raised, totalled, inverted = sem("wa_lowered"), sem("wa_raised"), sem("wa_totalled"), sem("wa_inverted")
        weighted = sem("wa_weighted")
        p_turned, p_out = sem("wa_p_turned"), sem("wa_p_out")
        attended, o_out = sem("wa_attended"), sem("wa_o_out")
        projected, summed = sem("wa_projected"), sem("wa_summed")
        x_kept = sem("wa_x_kept")

        def rows(dram, n, wr, first, count):
            r = (wr * WS + (DISP + first)) % H
            return dram[bass.ds(n // NWR, 1), r * W:(r + count) * W, :].rearrange("a t c -> (a t) c")

        def half(tile, k, h):
            return tile[:, k, h].rearrange("p a b c -> p (a b) c")[:, :, 0:WIN]

        run = dict(first=-3, last=NU + 4, lo=NWR, hi=NU - NWR, unroll=NWR)

        with nc.Block() as block:
            @block.sync
            def _(sp):
                sp.dma_start(wqkv[:, :], w_qkv).then_inc(consts, 16)
                sp.dma_start(wout[:, :], w_out).then_inc(consts, 16)
                sp.dma_start(bout[:, :], bass.AP(b_out.tensor, 0, [[0, CH], [1, C]])).then_inc(consts, 16)
                sp.dma_start(shift_mask[:, :, :, :, :].rearrange("p a b c d -> p (a b c d)"), shift_mask_d).then_inc(consts, 16)
                sp.wait_ge(prep, 2)

                def load(n, k):
                    if not inside(n, NU):
                        return
                    at_least(sp, x_turned, n - S + 1)
                    at_least(sp, x_kept, n - S + 1)
                    wr, k = k % NWR, k % S
                    sp.dma_start(xw[:, k, 0:2, :], rows(x, n, wr, 0, 4).rearrange("(a p) c -> p a c", p=CH)).then_inc(loaded[k], 16)
                    sp.dma_start(xw[:, k, 2, :], rows(x, n, wr, 4, 2)).then_inc(loaded[k], 16)
                    sp.dma_start(xw[0:W, k, 3, :], rows(x, n, wr, 6, 1)).then_inc(loaded[k], 16)

                def store(n, k):
                    if not inside(n, NU):
                        return
                    sp.wait_ge(summed, n + 1)
                    wr, k = k % NWR, k % S
                    sp.dma_start(rows(x1, n, wr, 0, 4).rearrange("(a p) c -> p a c", p=CH), y[:, k, 0:2, :]).then_inc(stored[k], 16)
                    sp.dma_start(rows(x1, n, wr, 4, 2), y[:, k, 2, :]).then_inc(stored[k], 16)
                    sp.dma_start(rows(x1, n, wr, 6, 1), y[0:W, k, 3, :]).then_inc(stored[k], 16)

                def step(n, k):
                    load(n + 3, k + 3)
                    store(n - 4, k - 4)
                pipeline(sp, step, **run)
                for k in range(S):
                    sp.wait_ge(stored[k], NU // S * 48)

            @block.tensor
            def _(pe):
                pe.wait_ge(consts, 64)
                pe.wait_ge(prep, 2)

                def turn_tokens(n, k):
                    if not inside(n, NU):
                        return
                    k %= S
                    pe.wait_ge(loaded[k], (n // S + 1) * 48)
                    at_least(pe, x_normed, n)
                    for t in range(4):
                        p = CH if t < 3 else W
                        mm = nc.tensor.transpose(b_tx[:, t * CH:t * CH + p], xw[0:p, k, t, :], ident[0:p, 0:p])
                    mm.then_inc(x_turned, 1)

                def queries(n, k):
                    if inside(n, NU):
                        pe.wait_ge(x_normed, n + 1)
                        at_least(pe, q_out, n)
                        nc.tensor.matmul(b_q[:, 0:ROWTOK], wqkv[:, 0:C], xT[:, k % S, :, 0:WIN], start=True, stop=True).then_inc(q_ready, 1)

                def keys(n, k):
                    if inside(n, NU):
                        pe.wait_ge(x_normed, n + 1)
                        at_least(pe, k_out, n)
                        nc.tensor.matmul(b_k[:, 0:ROWTOK], wqkv[:, C:2 * C], xT[:, k % S, :, 0:WIN], start=True, stop=True).then_inc(k_ready, 1)

                def values(n, k):
                    if not inside(n, NU):
                        return
                    pe.wait_ge(x_normed, n + 1)
                    at_least(pe, v_out, n)
                    for p in range(NWC // 2):
                        mm = nc.tensor.matmul(b_v[:, p * C:(p + 1) * C], xT[:, k % S, 2 * p:2 * p + 2, :].rearrange("p w c -> p (w c)"),
                                              wqkv[:, 2 * C:3 * C], start=True, stop=True)
                    mm.then_inc(v_ready, 1)

                def scores(n, k, h):
                    if not inside(n, NU):
                        return
                    pe.wait_ge(q_out, n + 1)
                    pe.wait_ge(k_out, n + 1)
                    at_least(pe, biased, n * 2 + h)
                    for w in range(HW_):
                        c = (h * HW_ + w) * WIN
                        part = slice(WPAD * (w % 2), WPAD * (w % 2) + WPAD)
                        mm = nc.tensor.matmul(b_s[part, (w // 2) * HEADS * WIN:(w // 2 + 1) * HEADS * WIN],
                                              qT[k % S][:, c:c + WPAD], kb[:, k % S, :, c:c + WIN], start=True, stop=True)
                    mm.then_inc(scored, 1)

                def turn_probabilities(n, k, h):
                    if not inside(n, NU):
                        return
                    pe.wait_ge(weighted, n * 2 + h + 1)
                    at_least(pe, p_out, n * 2 + h)
                    for p in range(2):
                        for hp in range(2):
                            q = p * 2 + hp
                            mm = nc.tensor.transpose(b_pt[:, q * 128:(q + 1) * 128],
                                                     prob[:, k % S, h, p, 2 * hp:2 * hp + 2, :].rearrange("p j c -> p (j c)"), ident[:, :])
                    mm.then_inc(p_turned, 1)

                def attend(n, k, h):
                    if not inside(n, NU):
                        return
                    pe.wait_ge(p_out, n * 2 + h + 1)
                    pe.wait_ge(v_out, n + 1)
                    at_least(pe, o_out, n)
                    for w in range(HW_):
                        for hp in range(2):
                            c = (h * HW_ + w) * WIN
                            i = WPAD * (w % 2)
                            mm = nc.tensor.matmul(b_ot[64 * hp:64 * hp + 64, c:c + WIN],
                                                  vb[:, k % S, h * 2 + w // 2, w % 2, hp].rearrange("p a b -> p (a b)"),
                                                  pT[:, k % S, h, w // 2, hp, i:i + WIN], start=True, stop=True)
                    mm.then_inc(attended, 1)

                def project(n, k):
                    if not inside(n, NU):
                        return
                    pe.wait_ge(o_out, n + 1)
                    at_least(pe, summed, n)
                    for t in range(4):
                        p = CH if t < 3 else W
                        ot = oT[:, k % S, 2 * t:2 * t + p // W, :].rearrange("p a b -> p (a b)")
                        mm = nc.tensor.matmul(b_y[0:p, t * C:(t + 1) * C], ot, wout[:, :], start=True, stop=True)
                    mm.then_inc(projected, 1)

                def step(n, k):
                    keys(n, k)
                    queries(n, k)
                    project(n - 3, k - 3)
                    attend(n - 2, k - 2, 0)
                    turn_tokens(n + 1, k + 1)
                    turn_probabilities(n - 2, k - 2, 1)
                    scores(n, k, 0)
                    values(n, k)
                    attend(n - 2, k - 2, 1)
                    scores(n, k, 1)
                    turn_probabilities(n - 1, k - 1, 0)
                pipeline(pe, step, **run)

            @block.vector
            def _(dve):
                nc.vector.memset(b_y[:, :], 0.0)
                nc.vector.memset(kb[:, :, :, :], 0.0)
                nc.vector.memset(xT[:, :, :, :], 0.0)
                nc.vector.memset(vb[:, :, :, :, :, :, :], 0.0)
                nc.vector.memset(prob[:, :, :, :, :, :], 0.0).then_inc(prep, 1)
                for i in range(S):
                    nc.vector.memset(xw[:, i, 3, :], 0.0)
                    last = nc.vector.memset(qT[i][:, :], 0.0)
                last.then_inc(prep, 1)
                dve.wait_ge(consts, 64)
                dve.wait_ge(prep, 2)
                nc.vector.tensor_tensor(bias[:, :, :, :, :].rearrange("p a b c d -> p (a b c) d"),
                                        shift_mask[:, :, :, :, :].rearrange("p a b c d -> p (a b c) d"),
                                        position[:, :].unsqueeze(1).broadcast_to([128, NWR * 4, WIN]), ALU.add).then_inc(prep, 1)
                dve.wait_ge(prep, 3)

                def add_bias(n, k, h):
                    if not inside(n, NU):
                        return
                    dve.wait_ge(scored, n * 2 + h + 1)
                    at_least(dve, p_turned, (n - S) * 2 + h + 1)
                    nc.vector.tensor_tensor(prob[:, k % S, h, :, :, 0:WIN],
                                            b_s[:, 0:2 * HEADS * WIN].rearrange("p (a b c) -> p a b c", a=2, b=HEADS),
                                            bias[:, k % NWR, h].unsqueeze(2).broadcast_to([128, 2, HEADS, WIN]),
                                            ALU.add).then_inc(biased, 1)

                def find_peak(n, k, h):
                    if inside(n, NU):
                        dve.wait_ge(biased, n * 2 + h + 1)
                        nc.vector.tensor_reduce(peak[:, k % S, h, :], half(prob, k % S, h), AX.X, ALU.max).then_inc(peaked, 1)

                def add_up(n, k, h):
                    if inside(n, NU):
                        dve.wait_ge(raised, n * 2 + h + 1)
                        nc.vector.tensor_reduce(total[:, k % S, h, :], half(prob, k % S, h), AX.X, ALU.add).then_inc(totalled, 1)

                def invert(n, k, h):
                    if inside(n, NU):
                        dve.wait_ge(totalled, n * 2 + h + 1)
                        nc.vector.reciprocal(inv[:, k % S, h, :], total[:, k % S, h, :]).then_inc(inverted, 1)

                def residual(n, k):
                    if not inside(n, NU):
                        return
                    k %= S
                    dve.wait_ge(projected, n + 1)
                    dve.wait_ge(x_kept, n + 1)
                    at_least(dve, stored[k], (n // S) * 48)
                    nc.vector.tensor_tensor(y[:, k].rearrange("p a b -> p (a b)"), b_y[0:CH, :],
                                            xb[:, k].rearrange("p a b -> p (a b)"), ALU.add).then_inc(summed, 1)

                def values_out(n, k):
                    if not inside(n, NU):
                        return
                    dve.wait_ge(v_half_out, n + 1)
                    for par in range(2):
                        src = b_v[par * WPAD:par * WPAD + WIN, :].rearrange("p (w a b c) -> p w a b c", w=NWC // 2, a=2, b=2)[:, :, :, 1 - par, :]
                        to = (1 - par) * WPAD
                        last = nc.vector.tensor_copy(vb[to:to + WIN, k % S, :, par, :, 1 - par, :], src)
                    last.then_inc(v_out, 1)

                def queries_out(n, k):
                    if inside(n, NU):
                        dve.wait_ge(q_ready, n + 1)
                        nc.vector.tensor_scalar(qT[k % S][:, 0:ROWTOK], b_q[:, 0:ROWTOK], float(HD) ** -0.5, None,
                                                ALU.mult).then_inc(q_out, 1)

                def step(n, k):
                    queries_out(n, k)
                    values_out(n - 1, k - 1)
                    residual(n - 3, k - 3)
                    add_up(n - 1, k - 1, 0)
                    invert(n - 1, k - 1, 0)
                    add_bias(n, k, 0)
                    add_up(n - 1, k - 1, 1)
                    find_peak(n, k, 0)
                    add_bias(n, k, 1)
                    find_peak(n, k, 1)
                    invert(n - 1, k - 1, 1)
                pipeline(dve, step, **run)

            @block.scalar
            def _(act):
                act.wait_ge(prep, 2)

                def normalise(n, k):
                    if not inside(n, NU):
                        return
                    act.wait_ge(x_turned, n + 1)
                    src = b_tx[:, 0:ROWTOK].rearrange("p (r c) -> p r c", r=WS)
                    image = bass.ds(n // NWR, 1)
                    windows = xT[:, k % S, :, 0:WIN].rearrange("p w (r c) -> p w r c", r=WS)
                    edge = WS - DISP
                    for dst, s in ((windows[:, 0:NWC - 1], src[:, :, DISP:W - edge].rearrange("p r (w c) -> p w r c", c=WS)),
                                   (windows[:, NWC - 1, :, 0:edge], src[:, :, W - edge:W]),
                                   (windows[:, NWC - 1, :, edge:WS], src[:, :, 0:DISP])):
                        last = nc.scalar.activation(dst, s, ACT.Identity,
                                                    bias=gn_shift[:, image], scale=gn_rstd[:, image])
                    last.then_inc(x_normed, 1)

                def keys_out(n, k):
                    if not inside(n, NU):
                        return
                    act.wait_ge(k_ready, n + 1)
                    for h in range(HEADS):
                        part = slice(HD * h, HD * h + HD)
                        last = nc.scalar.activation(kb[part, k % S, h, :], b_k[part, 0:ROWTOK], ACT.Copy)
                    last.then_inc(k_out, 1)

                def values_out(n, k):
                    if not inside(n, NU):
                        return
                    act.wait_ge(v_ready, n + 1)
                    for par in range(2):
                        rows_ = slice(par * WPAD, par * WPAD + WIN)
                        src = b_v[rows_, :].rearrange("p (w a b c) -> p w a b c", w=NWC // 2, a=2, b=2)[:, :, :, par, :]
                        last = nc.scalar.activation(vb[rows_, k % S, :, par, :, par, :], src, ACT.Copy)
                    last.then_inc(v_half_out, 1)

                def exps(n, k, h):
                    if inside(n, NU):
                        act.wait_ge(lowered, n * 2 + h + 1)
                        nc.scalar.activation(half(prob, k % S, h), half(prob, k % S, h), ACT.Exp).then_inc(raised, 1)

                def probabilities_out(n, k, h):
                    if inside(n, NU):
                        act.wait_ge(p_turned, n * 2 + h + 1)
                        nc.scalar.activation(pT[:, k % S, h].rearrange("p a b c -> p (a b c)"), b_pt[:, :], ACT.Copy).then_inc(p_out, 1)

                def attended_out(n, k):
                    if not inside(n, NU):
                        return
                    act.wait_ge(attended, n * 2 + 2)
                    src = b_ot[:, 0:ROWTOK].rearrange("p (w r c) -> p w r c", w=NWC, r=WS)
                    dst = oT[:, k % S]
                    nc.scalar.activation(dst[:, :, DISP:W - (WS - DISP)].rearrange("p r (w c) -> p w r c", c=WS),
                                         src[:, 0:NWC - 1], ACT.Copy)
                    nc.scalar.activation(dst[:, :, W - (WS - DISP):W], src[:, NWC - 1, :, 0:WS - DISP], ACT.Copy)
                    nc.scalar.activation(dst[:, :, 0:DISP], src[:, NWC - 1, :, WS - DISP:WS], ACT.Copy).then_inc(o_out, 1)

                def step(n, k):
                    normalise(n, k)
                    values_out(n - 1, k - 1)
                    attended_out(n - 3, k - 3)
                    probabilities_out(n - 2, k - 2, 0)
                    keys_out(n, k)
                    exps(n - 1, k - 1, 0)
                    probabilities_out(n - 2, k - 2, 1)
                    exps(n - 1, k - 1, 1)
                pipeline(act, step, **run)

            @block.gpsimd
            def _(pool):
                pool.wait_ge(consts, 64)
                pool.wait_ge(prep, 2)

                def lower(n, k, h):
                    if inside(n, NU):
                        pool.wait_ge(peaked, n * 2 + h + 1)
                        s = half(prob, k % S, h)
                        nc.gpsimd.tensor_tensor(s, s, peak[:, k % S, h, :].unsqueeze(2).broadcast_to([128, 2 * HEADS, WIN]),
                                                ALU.subtract).then_inc(lowered, 1)

                def weigh(n, k, h):
                    if inside(n, NU):
                        pool.wait_ge(inverted, n * 2 + h + 1)
                        s = half(prob, k % S, h)
                        nc.gpsimd.tensor_tensor(s, s, inv[:, k % S, h, :].unsqueeze(2).broadcast_to([128, 2 * HEADS, WIN]),
                                                ALU.mult).then_inc(weighted, 1)

                def keep_tokens(n, k):
                    if not inside(n, NU):
                        return
                    k %= S
                    pool.wait_ge(loaded[k], (n // S + 1) * 48)
                    at_least(pool, summed, n - S + 1)
                    nc.gpsimd.tensor_tensor(xb[:, k], xw[:, k], bout[:, :].unsqueeze(1).broadcast_to([CH, 4, C]),
                                            ALU.add).then_inc(x_kept, 1)

                def step(n, k):
                    lower(n - 1, k - 1, 1)
                    weigh(n - 1, k - 1, 0)
                    keep_tokens(n, k)
                    lower(n, k, 0)
                    weigh(n - 1, k - 1, 1)
                pipeline(pool, step, **run)


def linear_attention(nc, x1, t2, attn_wt, attn_b, causal_d, keep_d, ident, exponent, ln2_table, gram, bank):
    ctx = ExitStack()
    with ctx:
        def sb(name, shape):
            return ctx.enter_context(nc.sbuf_tensor("la_" + name, shape, F32))

        def sem(name):
            return ctx.enter_context(nc.semaphore(name))

        E = C + 1
        UNITS = NCH // 2
        S = 4
        XS = 8
        AHEAD = 7
        wt = sb("wt", [128, 3 * C])
        bqk = sb("bqk", [128, 2])
        bv = sb("bv", [CH, C])
        causal = sb("causal", [CH, CH])
        keep = sb("keep", [128, NC2])
        xc = sb("xc", [CH, XS, 2, C])
        stats = sb("stats", [CH, S, 2, 2, 6])
        mv = sb("mv", [CH, S, 2, 2, 2])
        spread = sb("spread", [CH, 4])
        minus = sb("minus", [CH, 4])
        ln = sb("ln", [CH, S, 2, 2, 2])
        u = sb("u", [CH, S, 2, C])
        uT = sb("uT", [128, S, 2 * CH])
        raised = sb("raised", [128, S, 2, 2 * CH])
        positive = sb("positive", [128, S, 2, 2 * CH])
        fqk = sb("fqk", [128, S, 2, 2 * CH])
        ve = sb("ve", [CH, S, 2, E])
        aT = sb("aT", [CH, S, 2, CH])
        kt = sb("kt", [CH, S, 2, C])
        state = sb("state", [128, S, 2, E])
        carried = sb("carried", [128, E])
        den = sb("den", [CH, 2, 1])
        rden = sb("rden", [CH, 2, 1])
        tn = sb("tn", [CH, XS, 2, C])
        u2 = sb("u2", [CH, S, 2, E])
        zero = sb("zero", [128, C + E])
        b_u, b_qk, b_v, b_kt, b_at, b_kv, b_num, b_gram = bank

        consts, prep = sem("la_consts"), sem("la_prep")
        loaded = [sem(f"la_loaded{i}") for i in range(XS)]
        stored = [sem(f"la_stored{i}") for i in range(XS)]
        measured, aggregated = sem("la_measured"), sem("la_aggregated")
        spread_out, minus_out, rooted, shifted = sem("la_spread_out"), sem("la_minus_out"), sem("la_rooted"), sem("la_shifted")
        tabled = sem("la_tabled")
        normed, u_turned, u_out = sem("la_normed"), sem("la_u_turned"), sem("la_u_out")
        qk_ready, qk_raised, qk_out = sem("la_qk_ready"), sem("la_qk_raised"), sem("la_qk_out")
        passed = sem("la_passed")
        v_ready, v_out = sem("la_v_ready"), sem("la_v_out")
        a_ready, a_out = sem("la_a_ready"), sem("la_a_out")
        k_turned, k_out = sem("la_k_turned"), sem("la_k_out")
        kv_ready, moved, advanced = sem("la_kv_ready"), sem("la_moved"), sem("la_advanced")
        num_ready, den_ready, den_inv, attended = sem("la_num_ready"), sem("la_den_ready"), sem("la_den_inv"), sem("la_attended")
        normed2, counted, gram_done = sem("la_normed2"), sem("la_counted"), sem("la_gram_done")

        def chunks(dram, n):
            image, part = n // UNITS, n % UNITS
            return dram[bass.ds(image, 1), bass.ds(part * (2 * CH), 2 * CH), :].rearrange("o (a p) c -> p (o a) c", p=CH)

        ROWS = NC2 + AHEAD
        run = dict(first=-4, last=NC2 + 8, lo=16, hi=NC2 - 8, unroll=XS)

        with nc.Block() as block:
            @block.sync
            def _(sp):
                sp.dma_start(wt[:, :], attn_wt).then_inc(consts, 16)
                sp.dma_start(bqk[:, :], attn_b[0:2 * C].rearrange("(a p) -> p a", p=C), allow_slow_non_contiguous=True).then_inc(consts, 16)
                sp.dma_start(bv[:, :], bass.AP(attn_b.tensor, 2 * C, [[0, CH], [1, C]])).then_inc(consts, 16)
                sp.dma_start(causal[:, :], causal_d).then_inc(consts, 16)
                sp.dma_start(keep[:, :], keep_d).then_inc(consts, 16)

                def load(n, k):
                    if not inside(n, NC2):
                        return
                    at_least(sp, attended, n - XS + 1)
                    sp.dma_start(xc[:, k], chunks(x1, n)).then_inc(loaded[k], 16)

                def store(n, k):
                    if not inside(n, NC2):
                        return
                    sp.wait_ge(attended, n + 1)
                    sp.dma_start(chunks(t2, n), tn[:, k]).then_inc(stored[k], 16)

                def step(n, k):
                    load(n + 4, (k + 4) % XS)
                    store(n - 4, (k - 4) % XS)
                pipeline(sp, step, **run)
                for k in range(XS):
                    sp.wait_ge(stored[k], NC2 // XS * 16)

            @block.tensor
            def _(pe):
                pe.wait_ge(consts, 80)
                pe.wait_ge(prep, 1)
                nc.tensor.matmul(b_gram[:, 0:E], zero[:, 0:C], zero[:, C:C + E], start=True, stop=False, skip_group_check=True)

                def turn_tokens(n, k):
                    if not inside(n, NC2):
                        return
                    pe.wait_ge(normed, n + 1)
                    at_least(pe, u_out, n)
                    for a in range(2):
                        mm = nc.tensor.transpose(b_u[:, a * CH:(a + 1) * CH], u[:, k, a, :], ident[0:CH, 0:CH])
                    mm.then_inc(u_turned, 1)

                def queries_and_keys(n, k):
                    if not inside(n, NC2):
                        return
                    at_least(pe, qk_raised, n)
                    for j in range(2):
                        mm = nc.tensor.matmul(b_qk[:, j * 2 * CH:(j + 1) * 2 * CH], wt[:, j * C:(j + 1) * C], uT[:, k, :],
                                              start=True, stop=True)
                    mm.then_inc(qk_ready, 1)

                def values(n, k):
                    if not inside(n, NC2):
                        return
                    pe.wait_ge(u_out, n + 1)
                    at_least(pe, v_out, n)
                    for a in range(2):
                        mm = nc.tensor.matmul(b_v[0:CH, a * C:(a + 1) * C], uT[:, k, a * CH:(a + 1) * CH],
                                              wt[:, 2 * C:3 * C], start=True, stop=True)
                    mm.then_inc(v_ready, 1)

                def turn_keys(n, k):
                    if not inside(n, NC2):
                        return
                    pe.wait_ge(qk_out, n + 1)
                    at_least(pe, k_out, n)
                    for a in range(2):
                        mm = nc.tensor.transpose(b_kt[0:CH, a * C:(a + 1) * C], fqk[:, k, 1, a * CH:(a + 1) * CH], ident[:, :])
                    mm.then_inc(k_turned, 1)

                def scores(n, k):
                    if not inside(n, NC2):
                        return
                    pe.wait_ge(qk_out, n + 1)
                    at_least(pe, a_out, n)
                    for a in range(2):
                        c = slice(a * CH, (a + 1) * CH)
                        mm = nc.tensor.matmul(b_at[0:CH, c], fqk[:, k, 1, c], fqk[:, k, 0, c],
                                              start=True, stop=True)
                    mm.then_inc(a_ready, 1)

                def outer(n, k):
                    if not inside(n, NC2):
                        return
                    pe.wait_ge(k_out, n + 1)
                    pe.wait_ge(v_out, n + 1)
                    at_least(pe, advanced, n)
                    for a in range(2):
                        mm = nc.tensor.matmul(b_kv[:, a * E:(a + 1) * E], kt[:, k, a, :], ve[:, k, a, :], start=True, stop=True)
                    mm.then_inc(kv_ready, 1)

                def numerators(n, k):
                    if not inside(n, NC2):
                        return
                    pe.wait_ge(a_out, n + 1)
                    pe.wait_ge(advanced, n + 1)
                    at_least(pe, attended, n)
                    for a in range(2):
                        nc.tensor.matmul(b_num[0:CH, a * E:(a + 1) * E], aT[:, k, a, :], ve[:, k, a, :], start=True, stop=False)
                        mm = nc.tensor.matmul(b_num[0:CH, a * E:(a + 1) * E], fqk[:, k, 0, a * CH:(a + 1) * CH], state[:, k, a, :],
                                              start=False, stop=True)
                    mm.then_inc(num_ready, 1)

                def moments(n, k):
                    if not inside(n, NC2):
                        return
                    pe.wait_ge(normed2, n + 1)
                    for a in range(2):
                        mm = nc.tensor.matmul(b_gram[:, 0:E], u2[:, k, a, 0:C], u2[:, k, a, :], start=False,
                                              stop=isinstance(n, int) and n == NC2 - 1 and a == 1, skip_group_check=True)
                    mm.then_inc(counted, 1)

                def step(n, k):
                    queries_and_keys(n, k % S)
                    turn_keys(n - 1, (k - 1) % S)
                    turn_tokens(n + 1, (k + 1) % S)
                    numerators(n - 3, (k - 3) % S)
                    moments(n - 8, k % S)
                    outer(n - 2, (k - 2) % S)
                    values(n + 1, (k + 1) % S)
                    scores(n, k % S)
                pipeline(pe, step, **run)

            @block.scalar
            def _(act):
                act.wait_ge(consts, 80)

                def normalise(n, kx):
                    if not inside(n, NC2):
                        return
                    k = kx % S
                    act.wait_ge(shifted, n + 1)
                    act.wait_ge(loaded[kx], (n // XS + 1) * 16)
                    for a in range(2):
                        last = nc.scalar.activation(u[:, k, a, :], xc[:, kx, a, :], ACT.Identity, bias=ln[:, k, 1, 0, a:a + 1],
                                                    scale=ln[:, k, 0, 0, a:a + 1])
                    last.then_inc(normed, 1)

                def turned_out(n, k):
                    if not inside(n, NC2):
                        return
                    act.wait_ge(u_turned, n + 1)
                    nc.scalar.activation(uT[:, k, :], b_u[:, 0:2 * CH], ACT.Copy).then_inc(u_out, 1)

                def features(n, k):
                    if not inside(n, NC2):
                        return
                    act.wait_ge(qk_ready, n + 1)
                    at_least(act, qk_out, n - S + 1)
                    for j in range(2):
                        src = b_qk[:, j * 2 * CH:(j + 1) * 2 * CH]
                        nc.scalar.activation(raised[:, k, j, :], src, ACT.Exp, bias=bqk[:, j:j + 1])
                        last = nc.scalar.activation(positive[:, k, j, :], src, ACT.Relu, bias=bqk[:, j:j + 1])
                    last.then_inc(qk_raised, 1)

                def keys_out(n, k):
                    if not inside(n, NC2):
                        return
                    act.wait_ge(k_turned, n + 1)
                    nc.scalar.activation(kt[:, k].rearrange("p a b -> p (a b)"), b_kt[0:CH, 0:2 * C], ACT.Copy).then_inc(k_out, 1)

                def normalise2(n, kx):
                    if not inside(n, NC2):
                        return
                    k, row = kx % S, (kx + AHEAD) % S
                    act.wait_ge(shifted, n + AHEAD + 1)
                    at_least(act, counted, n - S + 1)
                    for a in range(2):
                        last = nc.scalar.activation(u2[:, k, a, 0:C], tn[:, kx, a, :], ACT.Identity, bias=ln[:, row, 1, 1, a:a + 1],
                                                    scale=ln[:, row, 0, 1, a:a + 1])
                    last.then_inc(normed2, 1)

                def step(n, k):
                    normalise(n + 1, (k + 1) % XS)
                    features(n, k % S)
                    turned_out(n + 1, (k + 1) % S)
                    normalise2(n - 5, (k - 5) % XS)
                    keys_out(n - 1, (k - 1) % S)
                pipeline(act, step, **run)

            @block.gpsimd
            def _(pool):
                pool.wait_ge(prep, 1)

                def statistics(n, k):
                    if not inside(n, ROWS):
                        return
                    pool.wait_ge(aggregated, n + 1)
                    at_least(pool, shifted, n)
                    apart(pool, passed)
                    moments = mv[:, k].rearrange("p l a m -> p (l a) m")
                    nc.gpsimd.tensor_scalar(spread[:, :], moments[:, :, 1], LN_EPS, None, ALU.add).then_inc(spread_out, 1)
                    nc.gpsimd.tensor_scalar(minus[:, :], moments[:, :, 0], -1.0, None, ALU.mult).then_inc(minus_out, 1)
                    at_least(pool, normed, min(NC2, n - S + 1) if isinstance(n, int) else n - S + 1)
                    at_least(pool, normed2, n - AHEAD - S + 1)
                    pool.wait_ge(spread_out, n + 1)
                    apart(pool, passed)
                    rstd = ln[:, k, 0].rearrange("p l a -> p (l a)")
                    nc.gpsimd.tensor_tensor(rstd, spread[:, :], exponent[0:CH, 0:4], ALU.pow).then_inc(rooted, 1)
                    pool.wait_ge(minus_out, n + 1)
                    pool.wait_ge(rooted, n + 1)
                    apart(pool, passed)
                    nc.gpsimd.tensor_tensor(ln[:, k, 1].rearrange("p l a -> p (l a)"), minus[:, :], rstd, ALU.mult).then_inc(shifted, 1)

                def remember(n, k):
                    if not inside(n, NC2):
                        return
                    pool.wait_ge(shifted, n + AHEAD + 1)
                    apart(pool, passed)
                    nc.gpsimd.tensor_copy(ln2_table[:, :, bass.ds(n * 2, 2)], ln[:, k, :, 1, :]).then_inc(tabled, 1)

                def step(n, k):
                    remember(n - AHEAD, k % S)
                    statistics(n + 3, (k + 3) % S)
                pipeline(pool, step, **run)

            @block.vector
            def _(dve):
                nc.vector.memset(zero[:, :], 0.0)
                nc.vector.memset(carried[:, :], 0.0)
                nc.vector.memset(mv[:, :, :, :, :], 1.0)
                nc.vector.memset(ve[:, :, :, C:E], 1.0)
                nc.vector.memset(u2[:, :, :, C:E], 1.0).then_inc(prep, 1)
                dve.wait_ge(prep, 1)
                dve.wait_ge(consts, 80)

                def combine(n, k):
                    if inside(n, NC2):
                        dve.wait_ge(qk_raised, n + 1)
                        nc.vector.scalar_tensor_tensor(fqk[:, k], raised[:, k], 1.0, positive[:, k], ALU.min, ALU.add).then_inc(qk_out, 1)

                def inner_out(n, k):
                    if inside(n, NC2):
                        dve.wait_ge(a_ready, n + 1)
                        nc.vector.tensor_tensor(aT[:, k], b_at[0:CH, 0:2 * CH].rearrange("p (a b) -> p a b", a=2),
                                                causal[:, :].unsqueeze(1).broadcast_to([CH, 2, CH]), ALU.mult).then_inc(a_out, 1)

                def advance(n, k):
                    if inside(n, NC2):
                        dve.wait_ge(kv_ready, n + 1)
                        on = keep[:, bass.ds(n, 1)]
                        nc.vector.tensor_scalar(state[:, k, 0, :], carried[:, :], on, None, ALU.mult)
                        nc.vector.scalar_tensor_tensor(state[:, k, 1, :], carried[:, :], on, b_kv[:, 0:E],
                                                       ALU.mult, ALU.add).then_inc(moved, 1)

                def denominators(n, k):
                    if inside(n, NC2):
                        dve.wait_ge(num_ready, n + 1)
                        nc.vector.tensor_scalar(den[:, :, :], b_num[0:CH, 0:2 * E].rearrange("p (a b) -> p a b", a=2)[:, :, C:E],
                                                DEN_EPS, None, ALU.add).then_inc(den_ready, 1)

                def before_measuring(n, k):
                    if inside(n, NC2):
                        dve.wait_ge(loaded[k], (n // XS + 1) * 16)
                    if inside(n - AHEAD, NC2):
                        dve.wait_ge(attended, n - AHEAD + 1)

                def measure(n, k):
                    if inside(n, ROWS):
                        for which, tile, k2, m in ((0, xc, k, n), (1, tn, (k - AHEAD) % XS, n - AHEAD)):
                            if inside(m, NC2):
                                for a in range(2):
                                    last = nc.vector.bn_stats(stats[:, k % S, which, a, :], tile[:, k2, a, :])
                        last.then_inc(measured, 1)

                def aggregate(n, k):
                    if inside(n, ROWS):
                        for which, m in ((0, n), (1, n - AHEAD)):
                            if inside(m, NC2):
                                for a in range(2):
                                    last = nc.vector.bn_aggr(mv[:, k % S, which, a, :], stats[:, k % S, which, a, :])
                        last.then_inc(aggregated, 1)

                def carry(n, k):
                    if inside(n, NC2):
                        dve.wait_ge(moved, n + 1)
                        nc.vector.tensor_tensor(carried[:, :], b_kv[:, E:2 * E], state[:, k, 1, :], ALU.add).then_inc(advanced, 1)

                def values_out(n, k):
                    if inside(n, NC2):
                        dve.wait_ge(v_ready, n + 1)
                        nc.vector.tensor_tensor(ve[:, k, :, 0:C], b_v[0:CH, 0:2 * C].rearrange("p (a b) -> p a b", a=2),
                                                bv[:, :].unsqueeze(1).broadcast_to([CH, 2, C]), ALU.add).then_inc(v_out, 1)

                def invert(n):
                    if inside(n, NC2):
                        dve.wait_ge(den_ready, n + 1)
                        nc.vector.reciprocal(rden[:, :, :], den[:, :, :]).then_inc(den_inv, 1)

                def attend(n, k):
                    if inside(n, NC2):
                        dve.wait_ge(den_inv, n + 1)
                        at_least(dve, stored[k], n // XS * 16)
                        for a in range(2):
                            last = nc.vector.scalar_tensor_tensor(tn[:, k, a, :], b_num[0:CH, a * E:a * E + C], rden[:, a, :],
                                                                  xc[:, k, a, :], ALU.mult, ALU.add)
                        last.then_inc(attended, 1)

                def step(n, k):
                    measure(n + 3, (k + 3) % XS)
                    denominators(n - 3, (k - 3) % XS)
                    combine(n, k % S)
                    if inside(n + 3, ROWS):
                        dve.wait_ge(measured, n + 4)
                    invert(n - 3)
                    aggregate(n + 3, (k + 3) % XS)
                    advance(n - 2, (k - 2) % S)
                    attend(n - 3, (k - 3) % XS)
                    carry(n - 2, (k - 2) % S)
                    inner_out(n, k % S)
                    before_measuring(n + 4, (k + 4) % XS)
                    values_out(n + 1, (k + 1) % S)
                pipeline(dve, step, **run)
                dve.wait_ge(counted, NC2)
                nc.vector.tensor_copy(gram[:, :], b_gram[:, 0:E]).then_inc(gram_done, 1)


def recurrence(nc, t2, out, ffn_w, ffn_wt, ffn_vt, gamma, beta, ident, ones, exponent, ln2_table, gram, bank, agree):
    ctx = ExitStack()
    with ctx:
        def sb(name, shape, dtype=F32):
            return ctx.enter_context(nc.sbuf_tensor("sc_" + name, shape, dtype))

        def sem(name):
            return ctx.enter_context(nc.semaphore(name))

        E = C + 1
        I32 = mybir.dt.int32
        w = sb("w", [128, C])
        wT = sb("wT", [128, C])
        vT = sb("vT", [128, C])
        gb = sb("gb", [128, 2])
        scaled = sb("scaled", [128, C])
        fT = sb("fT", [128, C])
        prod = sb("prod", [128, C])
        cols = sb("cols", [128, 8])
        bn_rstd = sb("bn_rstd", [128, 1])
        rstd = sb("scan_rstd", [CH, NG, CH])
        shift = sb("scan_shift", [CH, NG, CH])
        start = sb("start", [128, COLS])
        final = sb("final", [128, COLS])
        gap = sb("gap", [128, B, NCH - 1])
        worst = sb("worst", [128, 1])
        worst_row = sb("worst_row", [1, 128])
        flag_f = sb("flag_f", [1, 1])
        flag = sb("flag", [1, 1], I32)
        consts, chain, pchain = sem("sc_consts"), sem("sc_chain"), sem("sc_pchain")
        rooted = sem("sc_rooted")

        with nc.Block() as block:
            @block.sync
            def _(sp):
                sp.dma_start(w[:, :], ffn_w).then_inc(consts, 16)
                sp.dma_start(wT[:, :], ffn_wt).then_inc(consts, 16)
                sp.dma_start(vT[:, :], ffn_vt).then_inc(consts, 16)
                sp.dma_start(gb[:, 0:1], gamma.rearrange("(p a) -> p a", a=1)).then_inc(consts, 16)
                sp.dma_start(gb[:, 1:2], beta.rearrange("(p a) -> p a", a=1)).then_inc(consts, 16)

            @block.tensor
            def _(pe):
                pe.wait_ge(consts, 80)
                nc.tensor.matmul(bank[0][:, 0:C], gram[:, 0:C], wT[:, :], start=True, stop=True).then_inc(pchain, 1)
                nc.tensor.matmul(bank[1][:, 0:1], wT[:, :], gram[:, C:E], start=True, stop=True).then_inc(pchain, 1)
                pe.wait_ge(chain, 1)
                nc.tensor.matmul(bank[2][:, 0:1], prod[:, :], ones[:, 0:1], start=True, stop=True).then_inc(pchain, 1)
                for i, table in enumerate((ln2_table[:, 0], ln2_table[:, 1])):
                    for g in range(NG):
                        last = nc.tensor.transpose(bank[4 + i][0:CH, g * CH:(g + 1) * CH], table[:, g * CH:(g + 1) * CH],
                                                   ident[0:CH, 0:CH])
                last.then_inc(pchain, 1)
                pe.wait_ge(chain, 8)
                nc.tensor.transpose(bank[3][:, 0:C], scaled[:, :], ident[:, :]).then_inc(pchain, 1)

            @block.vector
            def _(dve):
                done = [0]

                def link(ins):
                    done[0] += 1
                    ins.then_inc(chain, 1)
                    dve.wait_ge(chain, done[0])

                mean, square, square_mean, var, root, scale = (cols[:, i:i + 1] for i in range(6))
                shift_bn = cols[:, 6:7]
                dve.wait_ge(consts, 80)
                dve.wait_ge(pchain, 1)
                link(nc.vector.tensor_tensor(prod[:, :], bank[0][:, 0:C], wT[:, :], ALU.mult))
                dve.wait_ge(pchain, 3)
                link(nc.vector.tensor_scalar(mean, bank[1][:, 0:1], 1.0 / (B * T), None, ALU.mult))
                link(nc.vector.tensor_scalar(square, bank[2][:, 0:1], 1.0 / (B * T), None, ALU.mult))
                link(nc.vector.tensor_tensor(square_mean, mean, mean, ALU.mult))
                link(nc.vector.tensor_tensor(var, square, square_mean, ALU.subtract))
                link(nc.vector.tensor_scalar(root, var, 0.0, BN_EPS, ALU.max, ALU.add))
                dve.wait_ge(rooted, 1)
                link(nc.vector.tensor_tensor(scale, bn_rstd[:, :], gb[:, 0:1], ALU.mult))
                link(nc.vector.tensor_scalar(scaled[:, :], w[:, :], scale, None, ALU.mult))
                link(nc.vector.tensor_tensor(cols[:, 7:8], mean, scale, ALU.mult))
                link(nc.vector.tensor_tensor(shift_bn, gb[:, 1:2], cols[:, 7:8], ALU.subtract))
                dve.wait_ge(pchain, 4)
                nc.vector.tensor_copy(rstd[:, :, :].rearrange("p a b -> p (a b)"), bank[4][0:CH, 0:NG * CH])
                nc.vector.tensor_copy(shift[:, :, :].rearrange("p a b -> p (a b)"), bank[5][0:CH, 0:NG * CH])
                dve.wait_ge(pchain, 5)
                nc.vector.tensor_copy(fT[:, :], bank[3][:, 0:C])
                nc.vector.memset(start[:, :], 0.5)

            @block.gpsimd
            def _(pool):
                pool.wait_ge(chain, 6)
                nc.gpsimd.tensor_tensor(bn_rstd[:, :], cols[:, 4:5], exponent[:, 0:1], ALU.pow).then_inc(rooted, 1)

        shift_bn = cols[:, 6:7]
        scan(nc, t2, None, CH - WARM, fT, vT, shift_bn, rstd, shift, start, final, ident, bank, "warm")
        hand_over(nc, start, final)
        scan(nc, t2, out, 0, fT, vT, shift_bn, rstd, shift, start, final, ident, bank, "main")

        compared, worst_turned = sem("sc_compared"), sem("sc_worst_turned")
        with nc.Block() as block:
            @block.vector
            def _(dve):
                done = [0]

                def link(ins):
                    done[0] += 1
                    ins.then_inc(compared, 1)
                    dve.wait_ge(compared, done[0])

                ends = final[:, :].rearrange("p (b c) -> p b c", b=B)[:, :, 0:NCH - 1]
                begins = start[:, :].rearrange("p (b c) -> p b c", b=B)[:, :, 1:NCH]
                link(nc.vector.tensor_tensor(gap[:, :, :], ends, begins, ALU.subtract))
                link(nc.vector.tensor_tensor(gap[:, :, :], gap[:, :, :], gap[:, :, :], ALU.mult))
                link(nc.vector.tensor_scalar(gap[:, :, :], gap[:, :, :], agree * abs(agree), None, ALU.is_le))
                link(nc.vector.tensor_reduce(worst[:, :], gap[:, :, :].rearrange("p a b -> p (a b)"), AX.X, ALU.min))
                dve.wait_ge(worst_turned, 1)
                link(nc.vector.tensor_reduce(worst_row[:, 0:1], bank[0][0:1, 0:128], AX.X, ALU.min))
                link(nc.vector.tensor_scalar(flag_f[:, :], worst_row[:, 0:1], -1.0, 1.0, ALU.mult, ALU.add))
                link(nc.vector.tensor_copy(flag[:, :], flag_f[:, :]))

            @block.tensor
            def _(pe):
                pe.wait_ge(compared, 4)
                nc.tensor.transpose(bank[0][0:1, 0:128], worst[:, :], ident[:, :]).then_inc(worst_turned, 1)

        again = nc.values_load(flag[0:1, 0:1], min_val=0, max_val=1)
        with nc.If(again > 0):
            with nc.Fori(0, NCH - 1):
                hand_over(nc, start, final)
                scan(nc, t2, out, 0, fT, vT, shift_bn, rstd, shift, start, final, ident, bank, "again", repeated=True)


def hand_over(nc, start, final):
    with nc.Block() as block:
        @block.vector
        def _(dve):
            begins = start[:, :].rearrange("p (b c) -> p b c", b=B)
            ends = final[:, :].rearrange("p (b c) -> p b c", b=B)
            nc.vector.tensor_copy(begins[:, :, 1:NCH], ends[:, :, 0:NCH - 1])
            nc.vector.memset(begins[:, :, 0:1], 0.0)


def scan(nc, t2, out, s0, fT, vT, shift_bn, rstd, shift, start, final, ident, bank, name, repeated=False):
    ctx = ExitStack()
    with ctx:
        def sb(label, shape):
            return ctx.enter_context(nc.sbuf_tensor(f"{name}_{label}", shape, F32))

        used = []

        def sem(label):
            used.append(ctx.enter_context(nc.semaphore(f"{name}_{label}")))
            return used[-1]

        NB = (CH - s0) // SB
        NT = NB * SB
        tb = sb("tb", [CH, 4, NG, SB, C])
        ub = sb("ub", [CH, 2, NG, SB, C])
        ob = sb("ob", [CH, 2, NG, SB, C])
        uT = sb("uT", [128, 2, COLS])
        y = sb("y", [128, 2, COLS])
        b_state, b_u, b_y = bank[0:2], bank[2:4], bank[4:6]
        loaded = [sem(f"loaded{i}") for i in range(2)]
        stored = [sem(f"stored{i}") for i in range(2)]
        u_scaled, u_made, u_turned, u_out = sem("u_scaled"), sem("u_made"), sem("u_turned"), sem("u_out")
        w_done, v_done, y_made, y_turned, summed = sem("w_done"), sem("v_done"), sem("y_made"), sem("y_turned"), sem("summed")
        final_out, passed = sem("final_out"), sem("passed")

        def steps(dram, j):
            return dram.rearrange("b t d -> (b t d)").rearrange("(g p s d) -> p g s d", g=NG, p=CH, s=CH)[:, :, bass.ds(j * SB + s0, SB), :]

        def slot4(tile, j):
            return tile[:, bass.ds(j % 4, 1)].rearrange("p o g s c -> p (o g) s c")

        short = NB < 8
        run = dict(first=-3, last=NB + 2, lo=2 if not short else NB + 2, hi=NB - 4 if not short else NB + 2)

        with nc.Block() as block:
            @block.sync
            def _(sp):
                def step(j, k):
                    if inside(j + 3, NB):
                        kl = 1 - k
                        if out is not None:
                            at_least(sp, summed, j * SB)
                        at_least(sp, u_made, j)
                        at_least(sp, loaded[kl], (j + 3) // 2 * 16)
                        sp.dma_start(slot4(tb, j + 3), steps(t2, j + 3)).then_inc(loaded[kl], 16)
                    if out is not None and inside(j - 1, NB):
                        sp.wait_ge(summed, j * SB)
                        sp.dma_start(steps(out, j - 1), ob[:, 1 - k]).then_inc(stored[1 - k], 16)
                pipeline(sp, step, **run)
                if out is not None:
                    for k in range(2):
                        sp.wait_ge(stored[k], NB // 2 * 16)

            @block.gpsimd
            def _(pool):
                def step(j, k):
                    j, k = j + 1, 1 - k
                    if not inside(j, NB):
                        return
                    pool.wait_ge(loaded[k], (j // 2 + 1) * 16)
                    at_least(pool, u_turned, (j - 1) * SB)
                    apart(pool, passed)
                    src = slot4(tb, j)
                    now = bass.ds(j * SB + s0, SB)
                    nc.gpsimd.tensor_tensor(ub[:, k], src, rstd[:, :, now].unsqueeze(3).broadcast_to([CH, NG, SB, C]),
                                            ALU.mult).then_inc(u_scaled, 1)
                    pool.wait_ge(u_scaled, j + 1)
                    apart(pool, passed)
                    nc.gpsimd.tensor_tensor(ub[:, k], ub[:, k], shift[:, :, now].unsqueeze(3).broadcast_to([CH, NG, SB, C]),
                                            ALU.add).then_inc(u_made, 1)
                pipeline(pool, step, **run)

            @block.tensor
            def _(pe):
                def turn_tokens(t, j, k, i):
                    if not inside(t, NT):
                        return
                    pe.wait_ge(u_made, j + 1)
                    at_least(pe, u_out, t - 1)
                    for g in range(NG):
                        mm = nc.tensor.transpose(b_u[i % 2][:, g * CH:(g + 1) * CH], ub[:, k, g, i, :], ident[0:CH, 0:CH])
                    mm.then_inc(u_turned, 1)

                def input_part(t, i):
                    if not inside(t, NT):
                        return
                    pe.wait_ge(u_out, t + 1)
                    at_least(pe, y_made, t - 1)
                    nc.tensor.matmul(b_state[i % 2][:, 0:COLS], fT[:, :], uT[:, i % 2, :], start=True, stop=False).then_inc(w_done, 1)

                def state_part(t, i):
                    if not inside(t, NT):
                        return
                    at_least(pe, y_made, t)
                    before = start[:, :] if isinstance(t, int) and t == 0 else y[:, 1 - i % 2, :]
                    nc.tensor.matmul(b_state[i % 2][:, 0:COLS], vT[:, :], before, start=False, stop=True).then_inc(v_done, 1)

                def turn_states(t, i):
                    if out is None or not inside(t, NT):
                        return
                    pe.wait_ge(y_made, t + 1)
                    at_least(pe, summed, t - 1)
                    for g in range(NG):
                        mm = nc.tensor.transpose(b_y[i % 2][0:CH, g * C:(g + 1) * C], y[:, i % 2, g * CH:(g + 1) * CH], ident[:, :])
                    mm.then_inc(y_turned, 1)

                def step(j, k):
                    for i in range(SB):
                        t = j * SB + i
                        ahead = (j, k, i + 2) if i + 2 < SB else (j + 1, 1 - k, i + 2 - SB)
                        turn_tokens(t + 2, *ahead)
                        state_part(t, i)
                        turn_states(t - 1, i + 1)
                        input_part(t + 1, i + 1)
                pipeline(pe, step, **run)

            @block.vector
            def _(dve):
                def turned_out(t, i):
                    if not inside(t, NT):
                        return
                    dve.wait_ge(u_turned, t + 1)
                    at_least(dve, w_done, t - 1)
                    nc.vector.tensor_copy(uT[:, i % 2, :], b_u[i % 2][:, 0:COLS]).then_inc(u_out, 1)

                def residual(t, j, k, i):
                    if out is None or not inside(t, NT):
                        return
                    dve.wait_ge(y_turned, t + 1)
                    dve.wait_ge(loaded[k], (j // 2 + 1) * 16)
                    at_least(dve, stored[k], j // 2 * 16)
                    nc.vector.tensor_tensor(ob[:, k, :, i, :], b_y[i % 2][0:CH, :].rearrange("p (g c) -> p g c", g=NG),
                                            slot4(tb, j)[:, :, i, :], ALU.add).then_inc(summed, 1)

                def step(j, k):
                    for i in range(SB):
                        t = j * SB + i
                        turned_out(t + 2, i + 2)
                        now = (j, k, i - 1) if i else (j - 1, 1 - k, SB - 1)
                        residual(t - 1, *now)
                pipeline(dve, step, **run)
                dve.wait_ge(y_made, NT)
                nc.vector.tensor_copy(final[:, :], y[:, 1, :]).then_inc(final_out, 1)

            @block.scalar
            def _(act):
                def step(j, k):
                    for i in range(SB):
                        t = j * SB + i
                        if not inside(t, NT):
                            continue
                        act.wait_ge(v_done, t + 1)
                        if out is not None:
                            at_least(act, y_turned, t - 1)
                        nc.scalar.activation(y[:, i % 2, :], b_state[i % 2][:, 0:COLS], ACT.Sigmoid,
                                             bias=shift_bn).then_inc(y_made, 1)
                pipeline(act, step, **run)

        if repeated:
            with nc.Block() as block:
                @block.gpsimd
                def _(pool):
                    for semaphore in used:
                        pool.sem_clear(semaphore)


_DATA = ["x", "L0_conv_w_qkv", "L0_conv_pos_emb", "L0_conv_w_out", "L0_conv_b_out", "attn_wt", "L1_attn_b",
         "L1_ffn_W", "ffn_wt", "ffn_vt", "L1_ffn_gamma", "L1_ffn_beta"]
_CONSTS = ["ident", "shift_mask", "causal", "group", "keep"]


def constants():
    import numpy as np
    f = np.float32
    lane = np.arange(128)
    r, c = np.arange(WIN) // WS, np.arange(WIN) % WS
    far = f(-1e30)
    upper = np.where((r[:, None] >= WS - DISP) != (r[None] >= WS - DISP), far, f(0))
    left = np.where((c[:, None] >= WS - DISP) != (c[None] >= WS - DISP), far, f(0))
    shift_mask = np.zeros((128, NWR, NWC, WIN), f)
    for start in (0, WPAD):
        shift_mask[start:start + WIN, NWR - 1] += upper[:, None]
        shift_mask[start:start + WIN, :, NWC - 1] += left[:, None]
    pairs = np.zeros((128, NWR, NWC // 2, WIN), f)
    pairs[0:WPAD] = shift_mask[0:WPAD, :, 0::2]
    pairs[WPAD:] = shift_mask[WPAD:, :, 1::2]
    causal = (np.arange(CH)[:, None] <= np.arange(CH)[None]).astype(f)
    group = (lane[:, None] // GROUP == lane[None] // GROUP).astype(f)
    keep = np.ones((128, NC2), f)
    keep[:, ::NCH // 2] = 0
    return dict(ident=np.eye(128, dtype=f), 
                shift_mask=np.ascontiguousarray(pairs.reshape(128, -1)), causal=causal, group=group, keep=keep)


def kernel(**inputs):
    import numpy as np
    import concourse.bacc as bacc
    from concourse.bass_utils import run_bass_kernel_spmd

    data = {k: np.ascontiguousarray(v) for k, v in inputs.items()}
    data["x"] = data["x"].reshape(B, T, C)
    data["attn_wt"] = np.ascontiguousarray(data["L1_attn_W"].T)
    data["ffn_wt"] = np.ascontiguousarray(data["L1_ffn_W"].T)
    data["ffn_vt"] = np.ascontiguousarray(data["L1_ffn_V"].T)
    data.update(constants())
    nc = bacc.Bacc("TRN2", target_bir_lowering=False, num_devices=1)
    arrays, args = {}, []
    for name in _DATA + _CONSTS:
        arrays[f"in_{name}"] = data[name]
        args.append(nc.dram_tensor(f"in_{name}", data[name].shape, F32, kind="ExternalInput").ap())
    out = nc.dram_tensor("out", (B, T, C), F32, kind="ExternalOutput").ap()
    build(nc, *args, out)
    result = run_bass_kernel_spmd(nc, [arrays], core_ids=[0])
    return result.results[0]["out"].reshape(B, H, W, C)
```
